# Optimizing a Trainium2 kernel written in Bass

```python
import numpy as np
import jax
import jax.numpy as jnp

def _softmax(x, axis=-1):
    return jax.nn.softmax(x, axis=axis)

def _gelu(x):
    return jax.nn.gelu(x, approximate=True)

def _silu(x):
    return jax.nn.silu(x)

def _sigmoid(x):
    return jax.nn.sigmoid(x)

def _layernorm(x, axis=-1, eps=1e-05):
    m = jnp.mean(x, axis=axis, keepdims=True)
    v = jnp.var(x, axis=axis, keepdims=True)
    return (x - m) / jnp.sqrt(v + eps)

def _scatter_add(tgt, idx, src, axis=0):
    return tgt.at[idx].add(src)

def _segment_sum(src, seg, n):
    return jax.ops.segment_sum(src, seg, n)
kernel_name = 'mk_gps_d1_gnn_r32_eaa6de'

def setup_inputs(seed: int=0):
    np.random.seed(seed)
    _w = jnp.asarray

    def _rec_inputs():
        import jax
        import jax.numpy as jnp
        _gk = jax.random.key(seed)
        x = -6.985e-05 + 0.9998 * jax.random.normal(jax.random.fold_in(_gk, 1), (10000, 512), jnp.float32)
        src = jax.random.randint(jax.random.fold_in(_gk, 2), (10000,), 0, 10000, jnp.int32)
        dst = jax.random.randint(jax.random.fold_in(_gk, 3), (10000,), 0, 10000, jnp.int32)
        _o = jnp.argsort(dst, stable=True)
        src = src[_o]
        dst = dst[_o]
        return (x, src, dst)
    x, src, dst = _rec_inputs()

    def _L0_gnn_setup():
        import jax, jax.numpy as jnp
        import numpy as np
        B = 32
        MAXN = 64
        HEADS = 8
        DH = 64
        M = 256
        D = 512
        EPS = 1e-05
        KEPS = 1e-06

        def _batchnorm(x, g, b):
            mu = jnp.mean(x, axis=0)
            var = jnp.mean((x - mu) ** 2, axis=0)
            return (x - mu) * jax.lax.rsqrt(var + EPS) * g + b

        def _forward(x, batch, edge_index, norm1_g, norm1_b, norm2_g, norm2_b, W_conv, b_conv, Wq, Wk, Wv, Wo, proj):
            N = x.shape[0]
            E = edge_index.shape[1]
            h = x
            xn = _batchnorm(x, norm1_g, norm1_b)
            msg = xn[edge_index[0]]
            agg = jax.ops.segment_sum(msg, edge_index[1], num_segments=N)
            deg = jax.ops.segment_sum(jnp.ones((E,), x.dtype), edge_index[1], num_segments=N)
            agg = agg / jnp.maximum(deg, 1.0)[:, None]
            conv_out = jax.nn.relu(agg @ W_conv + b_conv)
            counts = jax.ops.segment_sum(jnp.ones((N,), jnp.int32), batch, num_segments=B)
            offsets = jnp.concatenate([jnp.zeros((1,), jnp.int32), jnp.cumsum(counts)[:-1]])
            pos = jnp.arange(N, dtype=jnp.int32) - offsets[batch]
            h_dense = jnp.zeros((B, MAXN, D), x.dtype).at[batch, pos].set(h)
            mask = jnp.zeros((B, MAXN), bool).at[batch, pos].set(True)

            def heads(t, W):
                return (t @ W).reshape(B, MAXN, HEADS, DH).transpose(0, 2, 1, 3)
            q, k, v = (heads(h_dense, Wq), heads(h_dense, Wk), heads(h_dense, Wv))
            scale = DH ** (-0.25)

            def phi(t, is_query):
                t = t * scale
                u = jnp.einsum('bhnd,md->bhnm', t, proj)
                diag = 0.5 * jnp.sum(t * t, axis=-1, keepdims=True)
                if is_query:
                    m_ = jnp.max(u, axis=-1, keepdims=True)
                else:
                    m_ = jnp.max(u, axis=(-2, -1), keepdims=True)
                return jnp.exp(u - diag - jax.lax.stop_gradient(m_)) / np.sqrt(M) + KEPS
            qf = phi(q, True)
            kf = phi(k, False) * mask[:, None, :, None]
            vm = v * mask[:, None, :, None]
            kv = jnp.einsum('bhnm,bhnd->bhmd', kf, vm)
            z = 1.0 / (jnp.einsum('bhnm,bhm->bhn', qf, kf.sum(axis=2)) + KEPS)
            attn = jnp.einsum('bhnm,bhmd->bhnd', qf, kv) * z[..., None]
            attn = attn.transpose(0, 2, 1, 3).reshape(B, MAXN, D) @ Wo
            h_attn = attn[batch, pos]
            return _batchnorm(conv_out + h_attn + h, norm2_g, norm2_b)
        key = jax.random.key(seed)
        ks = jax.random.split(key, 10)
        sizes = 1024 + np.arange(B) * 131 % 1025
        N = int(sizes.sum())
        E = N * 8
        batch = jnp.asarray(np.repeat(np.arange(B), sizes), dtype=jnp.int32)
        edge_index = jax.random.randint(ks[0], (2, E), 0, N, dtype=jnp.int32)
        s = 1.0 / np.sqrt(D)
        return {'x': jax.random.normal(ks[1], (N, D), jnp.float32), 'batch': batch, 'edge_index': edge_index, 'norm1_g': jnp.ones((D,), jnp.float32), 'norm1_b': jnp.zeros((D,), jnp.float32), 'norm2_g': jnp.ones((D,), jnp.float32), 'norm2_b': jnp.zeros((D,), jnp.float32), 'W_conv': jax.random.normal(ks[2], (D, D), jnp.float32) * s, 'b_conv': jnp.zeros((D,), jnp.float32), 'Wq': jax.random.normal(ks[3], (D, D), jnp.float32) * s, 'Wk': jax.random.normal(ks[4], (D, D), jnp.float32) * s, 'Wv': jax.random.normal(ks[5], (D, D), jnp.float32) * s, 'Wo': jax.random.normal(ks[6], (D, D), jnp.float32) * s, 'proj': jax.random.normal(ks[7], (M, DH), jnp.float32)}
    _L0_gnn_all = _L0_gnn_setup()
    _L0_gnn_in = {k: v for k, v in _L0_gnn_all.items() if k in ('norm1_g', 'norm1_b', 'norm2_g', 'norm2_b', 'W_conv', 'b_conv', 'Wq', 'Wk', 'Wv', 'Wo', 'proj')}
    del _L0_gnn_all

    def _L0_mix_setup():
        import jax, jax.numpy as jnp
        import numpy as np
        DIM, HEADS, NB_FEATURES = (512, 8, 64)
        HEAD_DIM = DIM // HEADS

        def _phi(t, proj_mat):
            return jax.nn.elu(jnp.einsum('bnhd,hdf->bnhf', t, proj_mat)) + 1.0
        key = jax.random.key(seed)
        k_x, k_qkv, k_pm, k_wp, k_bp = jax.random.split(key, 5)
        B, N = (8, 128)
        x = jax.random.normal(k_x, (B, N, DIM), dtype=jnp.float32)
        w_qkv = jax.random.normal(k_qkv, (DIM, 3 * DIM), dtype=jnp.float32) * (1.0 / np.sqrt(DIM))
        proj_mat = jax.random.normal(k_pm, (HEADS, HEAD_DIM, NB_FEATURES), dtype=jnp.float32)
        w_proj = jax.random.normal(k_wp, (DIM, DIM), dtype=jnp.float32) * (1.0 / np.sqrt(DIM))
        b_proj = jax.random.normal(k_bp, (DIM,), dtype=jnp.float32) * 0.01
        return {'x': x, 'w_qkv': w_qkv, 'proj_mat': proj_mat, 'w_proj': w_proj, 'b_proj': b_proj}
    _L0_mix_all = _L0_mix_setup()
    _L0_mix_in = {k: v for k, v in _L0_mix_all.items() if k in ('w_qkv', 'proj_mat', 'w_proj', 'b_proj')}
    del _L0_mix_all

    def _L0_ffn_setup():
        import math
        import jax, jax.numpy as jnp
        import numpy as np
        B, T, D, FF, E = (32, 1024, 512, 64, 8)
        CAPACITY_FACTOR = 1.25
        CAP = int(math.ceil(CAPACITY_FACTOR * B * T / E))

        def _bank_residual(x2, Wr, br, W1, b1, W2, b2):
            N, d = x2.shape
            e = Wr.shape[1]
            logits = x2 @ Wr + br
            probs = jax.nn.softmax(logits, axis=-1)
            expert = jnp.argmax(probs, axis=-1)
            gate = jnp.take_along_axis(probs, expert[:, None], axis=-1)[:, 0]
            oneh = jax.nn.one_hot(expert, e, dtype=x2.dtype)
            pos = (jnp.cumsum(oneh, axis=0) * oneh).sum(-1).astype(jnp.int32) - 1
            keep = pos < CAP
            slot = expert.astype(jnp.int32) * CAP + jnp.minimum(pos, CAP - 1)
            xd = jnp.where(keep[:, None], x2, 0.0)
            buf = jnp.zeros((e * CAP, d), x2.dtype).at[slot].add(xd)
            buf = buf.reshape(e, CAP, d)
            h = jax.nn.gelu(jnp.einsum('ecd,edf->ecf', buf, W1) + b1[:, None, :], approximate=False)
            out = jnp.einsum('ecf,efd->ecd', h, W2) + b2[:, None, :]
            y = out.reshape(e * CAP, d)[slot]
            return y * (gate * keep.astype(x2.dtype))[:, None]
        key = jax.random.key(seed)
        ks = jax.random.split(key, 18)
        s = 0.02
        inp = {'x': jax.random.normal(ks[0], (B, T, D), dtype=jnp.float32), 'Wr_sp': jax.random.normal(ks[1], (D, E)) * s, 'br_sp': jnp.zeros((E,), jnp.float32), 'Wr_fq': jax.random.normal(ks[2], (D, E)) * s, 'br_fq': jnp.zeros((E,), jnp.float32), 'Ws1': jax.random.normal(ks[3], (D, FF)) * s, 'bs1': jnp.zeros((FF,), jnp.float32), 'Ws2': jax.random.normal(ks[4], (FF, D)) * s, 'bs2': jnp.zeros((D,), jnp.float32), 'W1_sp': jax.random.normal(ks[5], (E, D, FF)) * s, 'b1_sp': jnp.zeros((E, FF), jnp.float32), 'W2_sp': jax.random.normal(ks[6], (E, FF, D)) * s, 'b2_sp': jnp.zeros((E, D), jnp.float32), 'W1_fq': jax.random.normal(ks[7], (E, D, FF)) * s, 'b1_fq': jnp.zeros((E, FF), jnp.float32), 'W2_fq': jax.random.normal(ks[8], (E, FF, D)) * s, 'b2_fq': jnp.zeros((E, D), jnp.float32)}
        return inp
    _L0_ffn_all = _L0_ffn_setup()
    _L0_ffn_in = {k: v for k, v in _L0_ffn_all.items() if k in ('Wr_sp', 'br_sp', 'Wr_fq', 'br_fq', 'Ws1', 'bs1', 'Ws2', 'bs2', 'W1_sp', 'b1_sp', 'W2_sp', 'b2_sp', 'W1_fq', 'b1_fq', 'W2_fq', 'b2_fq')}
    del _L0_ffn_all
    return {'x': x, 'src': src, 'dst': dst, 'L0_gnn_norm1_g': _L0_gnn_in['norm1_g'], 'L0_gnn_norm1_b': _L0_gnn_in['norm1_b'], 'L0_gnn_norm2_g': _L0_gnn_in['norm2_g'], 'L0_gnn_norm2_b': _L0_gnn_in['norm2_b'], 'L0_gnn_W_conv': _L0_gnn_in['W_conv'], 'L0_gnn_b_conv': _L0_gnn_in['b_conv'], 'L0_gnn_Wq': _L0_gnn_in['Wq'], 'L0_gnn_Wk': _L0_gnn_in['Wk'], 'L0_gnn_Wv': _L0_gnn_in['Wv'], 'L0_gnn_Wo': _L0_gnn_in['Wo'], 'L0_gnn_proj': _L0_gnn_in['proj'], 'L0_mix_w_qkv': _L0_mix_in['w_qkv'], 'L0_mix_proj_mat': _L0_mix_in['proj_mat'], 'L0_mix_w_proj': _L0_mix_in['w_proj'], 'L0_mix_b_proj': _L0_mix_in['b_proj'], 'L0_ffn_Wr_sp': _L0_ffn_in['Wr_sp'], 'L0_ffn_br_sp': _L0_ffn_in['br_sp'], 'L0_ffn_Wr_fq': _L0_ffn_in['Wr_fq'], 'L0_ffn_br_fq': _L0_ffn_in['br_fq'], 'L0_ffn_Ws1': _L0_ffn_in['Ws1'], 'L0_ffn_bs1': _L0_ffn_in['bs1'], 'L0_ffn_Ws2': _L0_ffn_in['Ws2'], 'L0_ffn_bs2': _L0_ffn_in['bs2'], 'L0_ffn_W1_sp': _L0_ffn_in['W1_sp'], 'L0_ffn_b1_sp': _L0_ffn_in['b1_sp'], 'L0_ffn_W2_sp': _L0_ffn_in['W2_sp'], 'L0_ffn_b2_sp': _L0_ffn_in['b2_sp'], 'L0_ffn_W1_fq': _L0_ffn_in['W1_fq'], 'L0_ffn_b1_fq': _L0_ffn_in['b1_fq'], 'L0_ffn_W2_fq': _L0_ffn_in['W2_fq'], 'L0_ffn_b2_fq': _L0_ffn_in['b2_fq']}

def reference(x, src, dst, L0_gnn_norm1_g, L0_gnn_norm1_b, L0_gnn_norm2_g, L0_gnn_norm2_b, L0_gnn_W_conv, L0_gnn_b_conv, L0_gnn_Wq, L0_gnn_Wk, L0_gnn_Wv, L0_gnn_Wo, L0_gnn_proj, L0_mix_w_qkv, L0_mix_proj_mat, L0_mix_w_proj, L0_mix_b_proj, L0_ffn_Wr_sp, L0_ffn_br_sp, L0_ffn_Wr_fq, L0_ffn_br_fq, L0_ffn_Ws1, L0_ffn_bs1, L0_ffn_Ws2, L0_ffn_bs2, L0_ffn_W1_sp, L0_ffn_b1_sp, L0_ffn_W2_sp, L0_ffn_b2_sp, L0_ffn_W1_fq, L0_ffn_b1_fq, L0_ffn_W2_fq, L0_ffn_b2_fq):
    import jax
    import jax.numpy as jnp

    def _L0_gnn_ref(x, batch, edge_index, norm1_g, norm1_b, norm2_g, norm2_b, W_conv, b_conv, Wq, Wk, Wv, Wo, proj):
        import jax, jax.numpy as jnp
        import numpy as np
        B = 32
        MAXN = 64
        HEADS = 8
        DH = 64
        M = 256
        D = 512
        EPS = 1e-05
        KEPS = 1e-06

        def _batchnorm(x, g, b):
            mu = jnp.mean(x, axis=0)
            var = jnp.mean((x - mu) ** 2, axis=0)
            return (x - mu) * jax.lax.rsqrt(var + EPS) * g + b

        def _forward(x, batch, edge_index, norm1_g, norm1_b, norm2_g, norm2_b, W_conv, b_conv, Wq, Wk, Wv, Wo, proj):
            N = x.shape[0]
            E = edge_index.shape[1]
            h = x
            xn = _batchnorm(x, norm1_g, norm1_b)
            msg = xn[edge_index[0]]
            agg = jax.ops.segment_sum(msg, edge_index[1], num_segments=N)
            deg = jax.ops.segment_sum(jnp.ones((E,), x.dtype), edge_index[1], num_segments=N)
            agg = agg / jnp.maximum(deg, 1.0)[:, None]
            conv_out = jax.nn.relu(agg @ W_conv + b_conv)
            counts = jax.ops.segment_sum(jnp.ones((N,), jnp.int32), batch, num_segments=B)
            offsets = jnp.concatenate([jnp.zeros((1,), jnp.int32), jnp.cumsum(counts)[:-1]])
            pos = jnp.arange(N, dtype=jnp.int32) - offsets[batch]
            h_dense = jnp.zeros((B, MAXN, D), x.dtype).at[batch, pos].set(h)
            mask = jnp.zeros((B, MAXN), bool).at[batch, pos].set(True)

            def heads(t, W):
                return (t @ W).reshape(B, MAXN, HEADS, DH).transpose(0, 2, 1, 3)
            q, k, v = (heads(h_dense, Wq), heads(h_dense, Wk), heads(h_dense, Wv))
            scale = DH ** (-0.25)

            def phi(t, is_query):
                t = t * scale
                u = jnp.einsum('bhnd,md->bhnm', t, proj)
                diag = 0.5 * jnp.sum(t * t, axis=-1, keepdims=True)
                if is_query:
                    m_ = jnp.max(u, axis=-1, keepdims=True)
                else:
                    m_ = jnp.max(u, axis=(-2, -1), keepdims=True)
                return jnp.exp(u - diag - jax.lax.stop_gradient(m_)) / np.sqrt(M) + KEPS
            qf = phi(q, True)
            kf = phi(k, False) * mask[:, None, :, None]
            vm = v * mask[:, None, :, None]
            kv = jnp.einsum('bhnm,bhnd->bhmd', kf, vm)
            z = 1.0 / (jnp.einsum('bhnm,bhm->bhn', qf, kf.sum(axis=2)) + KEPS)
            attn = jnp.einsum('bhnm,bhmd->bhnd', qf, kv) * z[..., None]
            attn = attn.transpose(0, 2, 1, 3).reshape(B, MAXN, D) @ Wo
            h_attn = attn[batch, pos]
            return _batchnorm(conv_out + h_attn + h, norm2_g, norm2_b)
        return _forward(x, batch, edge_index, norm1_g, norm1_b, norm2_g, norm2_b, W_conv, b_conv, Wq, Wk, Wv, Wo, proj)

    def _L0_mix_ref(x, w_qkv, proj_mat, w_proj, b_proj):
        import jax, jax.numpy as jnp
        import numpy as np
        DIM, HEADS, NB_FEATURES = (512, 8, 64)
        HEAD_DIM = DIM // HEADS

        def _phi(t, proj_mat):
            return jax.nn.elu(jnp.einsum('bnhd,hdf->bnhf', t, proj_mat)) + 1.0
        B, N, dim = x.shape
        H, D = (HEADS, dim // HEADS)
        qkv = x @ w_qkv
        q, k, v = jnp.split(qkv, 3, axis=-1)
        q = q.reshape(B, N, H, D)
        k = k.reshape(B, N, H, D)
        v = v.reshape(B, N, H, D)
        q_phi = _phi(q, proj_mat)
        k_phi = _phi(k, proj_mat)
        kv = jnp.einsum('bnhf,bnhd->bhfd', k_phi, v)
        z = 1.0 / jnp.einsum('bnhf,bhf->bnh', q_phi, k_phi.sum(axis=1))
        out = jnp.einsum('bnhf,bhfd,bnh->bnhd', q_phi, kv, z)
        out = out.reshape(B, N, H * D)
        return out @ w_proj + b_proj

    def _L0_ffn_ref(x, Wr_sp, br_sp, Wr_fq, br_fq, Ws1, bs1, Ws2, bs2, W1_sp, b1_sp, W2_sp, b2_sp, W1_fq, b1_fq, W2_fq, b2_fq):
        import math
        import jax, jax.numpy as jnp
        import numpy as np
        B, T, D, FF, E = (32, 1024, 512, 64, 8)
        CAPACITY_FACTOR = 1.25
        CAP = int(math.ceil(CAPACITY_FACTOR * B * T / E))

        def _bank_residual(x2, Wr, br, W1, b1, W2, b2):
            N, d = x2.shape
            e = Wr.shape[1]
            logits = x2 @ Wr + br
            probs = jax.nn.softmax(logits, axis=-1)
            expert = jnp.argmax(probs, axis=-1)
            gate = jnp.take_along_axis(probs, expert[:, None], axis=-1)[:, 0]
            oneh = jax.nn.one_hot(expert, e, dtype=x2.dtype)
            pos = (jnp.cumsum(oneh, axis=0) * oneh).sum(-1).astype(jnp.int32) - 1
            keep = pos < CAP
            slot = expert.astype(jnp.int32) * CAP + jnp.minimum(pos, CAP - 1)
            xd = jnp.where(keep[:, None], x2, 0.0)
            buf = jnp.zeros((e * CAP, d), x2.dtype).at[slot].add(xd)
            buf = buf.reshape(e, CAP, d)
            h = jax.nn.gelu(jnp.einsum('ecd,edf->ecf', buf, W1) + b1[:, None, :], approximate=False)
            out = jnp.einsum('ecf,efd->ecd', h, W2) + b2[:, None, :]
            y = out.reshape(e * CAP, d)[slot]
            return y * (gate * keep.astype(x2.dtype))[:, None]
        b, t, d = x.shape
        x2 = x.reshape(b * t, d)
        shared = jax.nn.gelu(x2 @ Ws1 + bs1, approximate=False) @ Ws2 + bs2
        y = shared
        y = y + _bank_residual(x2, Wr_sp, br_sp, W1_sp, b1_sp, W2_sp, b2_sp)
        y = y + _bank_residual(x2, Wr_fq, br_fq, W1_fq, b1_fq, W2_fq, b2_fq)
        return y.reshape(b, t, d)
    edge_index = jnp.stack([src, dst])
    batch0 = jnp.zeros((10000,), jnp.int32)
    xn = _layernorm(x, axis=-1)
    x = x + _L0_gnn_ref(xn, batch0, edge_index, L0_gnn_norm1_g, L0_gnn_norm1_b, L0_gnn_norm2_g, L0_gnn_norm2_b, L0_gnn_W_conv, L0_gnn_b_conv, L0_gnn_Wq, L0_gnn_Wk, L0_gnn_Wv, L0_gnn_Wo, L0_gnn_proj) + _L0_mix_ref(xn[None], L0_mix_w_qkv, L0_mix_proj_mat, L0_mix_w_proj, L0_mix_b_proj)[0]
    x = x + _L0_ffn_ref(_layernorm(x, axis=-1)[None], L0_ffn_Wr_sp, L0_ffn_br_sp, L0_ffn_Wr_fq, L0_ffn_br_fq, L0_ffn_Ws1, L0_ffn_bs1, L0_ffn_Ws2, L0_ffn_bs2, L0_ffn_W1_sp, L0_ffn_b1_sp, L0_ffn_W2_sp, L0_ffn_b2_sp, L0_ffn_W1_fq, L0_ffn_b1_fq, L0_ffn_W2_fq, L0_ffn_b2_fq)[0]
    return x

_drawn_inputs = setup_inputs


def setup_inputs(seed=0):
    import zlib

    import numpy as np

    out = dict(_drawn_inputs(seed))
    spreads = {'L0_gnn_norm1_g': (1.0, 0.2),
     'L0_gnn_norm1_b': (0.0, 0.38),
     'L0_gnn_norm2_g': (1.0, 0.2),
     'L0_gnn_norm2_b': (0.0, 0.1),
     'L0_gnn_b_conv': (0.0, 0.406),
     'L0_ffn_br_sp': (0.0, 0.8),
     'L0_ffn_br_fq': (0.0, 0.8),
     'L0_ffn_bs1': (0.0, 2.0),
     'L0_ffn_bs2': (0.0, 0.294),
     'L0_ffn_b1_sp': (0.0, 0.8),
     'L0_ffn_b2_sp': (0.0, 0.685),
     'L0_ffn_b1_fq': (0.0, 0.8),
     'L0_ffn_b2_fq': (0.0, 0.684)}
    factors = {'L0_gnn_Wq': 8.0,
     'L0_gnn_Wk': 8.0,
     'L0_gnn_Wv': 64.0,
     'L0_gnn_Wo': 64.0,
     'L0_gnn_proj': 8.0,
     'L0_mix_w_qkv': 6.693,
     'L0_mix_proj_mat': 8.0,
     'L0_mix_w_proj': 6.558,
     'L0_mix_b_proj': 8.0,
     'L0_ffn_Wr_sp': 4.798,
     'L0_ffn_Wr_fq': 4.802,
     'L0_ffn_Ws1': 2.823,
     'L0_ffn_W1_sp': 8.0,
     'L0_ffn_W2_sp': 8.0,
     'L0_ffn_W1_fq': 8.0,
     'L0_ffn_W2_fq': 8.0}
    for name, (base, spread) in spreads.items():
        noise = np.random.default_rng([zlib.crc32(name.encode()), seed]).standard_normal(out[name].shape)
        drawn = base * np.exp(spread * noise) if base else spread * noise
        out[name] = jnp.asarray(drawn.astype(out[name].dtype))
    for name, factor in factors.items():
        out[name] = (out[name] * factor).astype(out[name].dtype)
    return out
```

```python
from contextlib import ExitStack

import concourse.bass as bass
from concourse import mybir

F32 = mybir.dt.float32
BF16 = mybir.dt.bfloat16
I32 = mybir.dt.int32
ALU = mybir.AluOpType
ACT = mybir.ActivationFunctionType
AX = mybir.AxisListType

N, D, E = 10000, 512, 10000
P = 128
R = 125
C = 4
G = R * C
NG = N // G
NT = N // R
KC = D // P
SPRAY = 112
AGG_W = 520
AGG_ROWS = 10240
LN_EPS = 1e-5
BN_EPS = 1e-5
ATT_ROWS, ATT_HEADS, ATT_DH, ATT_M = 64, 8, 64, 256
ATT_KEPS = 1e-6
EXPERTS, FF = 8, 64
CAP = 5120
FC = 9


def wait(eng, sem, value):
    if isinstance(value, int) and value <= 0:
        return
    eng.wait_ge(sem, value)


def settle(eng, passed):
    eng.sem_inc(passed)


class Chain:

    def __init__(self, eng, sem, base=0):
        self.eng, self.sem, self.base, self.n = eng, sem, base, 0

    def link(self, ins):
        ins.then_inc(self.sem, 1)
        self.n += 1
        self.eng.wait_ge(self.sem, self.base + self.n)


def inverse_root(ch, dve, out, root, var, tmp):
    ch.link(dve.reciprocal(out, root))
    ch.link(dve.tensor_tensor(tmp, out, out, ALU.mult))
    ch.link(dve.tensor_tensor(tmp, tmp, var, ALU.mult))
    ch.link(dve.tensor_scalar(tmp, tmp, -0.5, 1.5, ALU.mult, ALU.add))
    ch.link(dve.tensor_tensor(out, out, tmp, ALU.mult))


def dma_rows(eng, out, in_, sem):
    eng.dma_start(out[0:SPRAY], in_[0:SPRAY]).then_inc(sem, 16)
    eng.dma_start(out[SPRAY:R], in_[SPRAY:R]).then_inc(sem, 16)


def groups(eng, step):
    step(0, 0, 0)
    step(1, 1, 0)
    with eng.Fori(1, NG // 2 - 1) as r:
        step(r * 2, 0, r)
        step(r * 2 + 1, 1, r)
    step(NG - 2, 0, NG // 2 - 1)
    step(NG - 1, 1, NG // 2 - 1)


def gps_layer_kernel(nc, a, out):
    x_g = a["x"].rearrange("(s c p) d -> s p c d", c=C, p=R)
    out_g = out.rearrange("(s c p) d -> s p c d", c=C, p=R)
    agg = nc.dram_tensor("agg", [AGG_ROWS, AGG_W], F32, kind="Internal").ap()
    agg_g = agg[0:N, :].rearrange("(s c p) d -> s p c d", c=C, p=R)
    u_dram = nc.dram_tensor("u_dram", [N, D], F32, kind="Internal").ap()
    u_g = u_dram.rearrange("(s c p) d -> s p c d", c=C, p=R)

    top = ExitStack()
    with top:
        def sem(name):
            return top.enter_context(nc.semaphore(name))

        def sb(stack, name, shape, dt=F32):
            return stack.enter_context(nc.sbuf_tensor(name, shape, dt))

        bank = [top.enter_context(nc.psum_tensor(f"bank{i}", [P, 512], F32)) for i in range(8)]

        ident = sb(top, "ident", [P, P])
        ones = sb(top, "ones", [P, P])
        row_stat = sb(top, "row_stat", [P, NG, 2, C])
        att_delta = sb(top, "att_delta", [P, D])
        phi_q = sb(top, "phi_q", [P, KC, D])
        w_proj = sb(top, "w_proj", [P, KC, D])
        kvp = sb(top, "kvp", [P, KC, D])
        ks_bd = sb(top, "ks_bd", [P, KC, P])
        s_const = sem("s_const")
        s_zero = sem("s_zero")
        s_past_dve = sem("s_past_dve")
        s_past_pool = sem("s_past_pool")

        mid = ExitStack()
        w_v = sb(mid, "w_v", [P, KC, D])
        w_conv = sb(mid, "w_conv", [P, KC, D])
        bn_part = sb(mid, "bn_part", [P, KC, NG * 6])
        ks_acc = sb(mid, "ks_acc", [P, D])
        block_mask = sb(mid, "block_mask", [P, P])

        first = ExitStack()
        phi_k = sb(first, "phi_k", [P, KC, D])
        src_i = sb(first, "src_i", [P, NT], I32)
        dst_f = sb(first, "dst_f", [P, NT])
        spare = sb(first, "spare", [P, NT])
        dst_rows = sb(first, "dst_rows", [P, E], I32)
        before = sb(first, "before", [P, R])
        s_dst = sem("s_dst")

        with ExitStack() as st:
            w_qk = sb(st, "w_qk", [P, KC, 2 * D])
            proj_bd = sb(st, "proj_bd", [P, KC, P])
            w_turned = sb(st, "w_turned", [P, D])
            idx_in = sb(st, "idx_in", [NT, 2, R], I32)
            idx_f = sb(st, "idx_f", [NT, 2, R])
            zeros = sb(st, "zeros", [P, 5, AGG_W])
            node_no = sb(st, "node_no", [P, 1])
            g_w = [sb(st, f"g_w{n}", [P, KC, D]) for n in "qkvo"]
            proj2 = sb(st, "proj2", [P, 2, P])
            x64 = sb(st, "x64", [ATT_ROWS, D])
            x64_t = sb(st, "x64_t", [P, KC, ATT_ROWS])
            proj_t = sb(st, "proj_t", [P, ATT_M])
            bn6 = sb(st, "bn6", [ATT_ROWS, 6])
            mv = sb(st, "mv", [ATT_ROWS, 2])
            small = sb(st, "small", [ATT_ROWS, 4])
            qk = sb(st, "qk", [ATT_ROWS, 2, D])
            diag = sb(st, "diag", [ATT_ROWS, 2, ATT_HEADS])
            v_aug = sb(st, "v_aug", [ATT_ROWS, ATT_HEADS, ATT_DH + 1])
            qk_t = sb(st, "qk_t", [P, 2, KC, ATT_ROWS])
            feat = sb(st, "feat", [ATT_ROWS, 2, ATT_HEADS, ATT_M])
            sq = feat[:, 0, 0:4, :].rearrange("p a b -> p (a b)").rearrange("p (w d) -> p w d", w=2)
            top_u = sb(st, "top_u", [ATT_ROWS, 2, ATT_HEADS])
            top_k = sb(st, "top_k", [ATT_HEADS, 1])
            top_d = sb(st, "top_d", [ATT_HEADS, ATT_HEADS])
            qf_t = sb(st, "qf_t", [P, 2 * ATT_HEADS, ATT_ROWS])
            kv_aug = sb(st, "kv_aug", [P, 2 * ATT_HEADS, ATT_DH + 1])
            z_att = sb(st, "z_att", [ATT_ROWS, ATT_HEADS])
            att = sb(st, "att", [ATT_ROWS, D])
            att_t = sb(st, "att_t", [P, KC, ATT_ROWS])
            att_out = sb(st, "att_out", [ATT_ROWS, D])
            delta_sel = sb(st, "delta_sel", [ATT_ROWS, P])

            s_pool = sem("s_pool")
            s_wqk = sem("s_wqk")
            s_bd = sem("s_bd")
            s_wv = sem("s_wv")
            s_idx = sem("s_idx")
            s_att_in = sem("s_att_in")
            s_zeroed = sem("s_zeroed")
            s_turn = sem("s_turn")
            s_turned = sem("s_turned")
            s_fused = sem("s_fused")
            s_fcopy = sem("s_fcopy")
            s_idx_f = sem("s_idx_f")
            s_idx_t = sem("s_idx_t")
            s_idx_c = sem("s_idx_c")
            s_att = sem("s_att")
            s_chain = sem("s_chain")
            STAGES = ["var", "std", "norm", "turn", "turned", "qkv", "scaled", "turn2", "turned2", "u",
                      "top", "turn_top", "top_d", "top_b", "arg", "exp", "phi", "kv", "kv_copy", "att",
                      "att_z", "turn3", "turned3", "wo", "wo_copy", "delta", "done"]
            after = {name: i + 1 for i, name in enumerate(STAGES)}

            with nc.Block() as block:
                @block.sync
                def _(sp):
                    sp.dma_start(x64[:, :], a["x"][0:ATT_ROWS, :]).then_inc(s_att_in, 16)
                    for w, name in zip(g_w, ("Wq", "Wk", "Wv", "Wo")):
                        sp.dma_start(w[:, :, :], a["L0_gnn_" + name].rearrange("(c p) n -> p c n", p=P)).then_inc(s_att_in, 16)
                    for twice in range(2):
                        sp.dma_start(proj2[:, :, twice * 64:twice * 64 + 64],
                                     a["L0_gnn_proj"].rearrange("(c p) d -> p c d", p=P)).then_inc(s_att_in, 16)
                    qkv = a["L0_mix_w_qkv"].rearrange("(c p) n -> p c n", p=P)
                    sp.dma_start(w_qk[:, :, :], qkv[:, :, 0:2 * D]).then_inc(s_wqk, 16)
                    sp.dma_start(idx_in[:, 0, :], a["src"].rearrange("(t p) -> t p", p=R)).then_inc(s_idx, 16)
                    sp.dma_start(idx_in[:, 1, :], a["dst"].rearrange("(t p) -> t p", p=R)).then_inc(s_idx, 16)
                    every = a["dst"].rearrange("(a e) -> a e", a=1).broadcast_to([P, E])
                    sp.dma_start(dst_rows[:, :], every).then_inc(s_dst, 16)
                    sp.dma_start(w_v[:, :, :], qkv[:, :, 2 * D:3 * D]).then_inc(s_wv, 16)
                    sp.dma_start(w_proj[:, :, :], a["L0_mix_w_proj"].rearrange("(c p) n -> p c n", p=P)).then_inc(s_wv, 16)
                    sp.dma_start(w_conv[:, :, :], a["L0_gnn_W_conv"].rearrange("(c p) n -> p c n", p=P)).then_inc(s_wv, 16)
                    sp.wait_ge(s_zero, 1)
                    agg_z = agg.rearrange("(p k r) w -> k p r w", p=P, r=5)
                    for k in range(AGG_ROWS // (P * 5)):
                        sp.dma_start(agg_z[k], zeros[:, :, :]).then_inc(s_zeroed, 16)
                    sp.wait_ge(s_zeroed, 16 * (AGG_ROWS // (P * 5)))
                    sp.wait_ge(s_dst, 16)
                    sp.wait_ge(s_wv, 48)

                @block.gpsimd
                def _(pool):
                    ch = Chain(pool, s_pool)
                    ch.link(pool.memset(proj_bd[:, :, :], 0.0))
                    for h in range(8):
                        b = 64 * (h % 2)
                        pool.dma_start(proj_bd[b:b + 64, h // 2, b:b + 64],
                                       a["L0_mix_proj_mat"][h]).then_inc(s_bd, 16)
                    pool.memset(zeros[:, :, :], 0.0).then_inc(s_zero, 1)
                    pool.memset(ones[:, :], 1.0)
                    ch.link(pool.memset(ident[:, :], 0.0))
                    ch.link(pool.affine_select(out=ident[:, :], in_=ident[:, :], compare_op=ALU.not_equal, fill=1.0,
                                               base=0, pattern=[[-1, P]], channel_multiplier=1))
                    ch.link(pool.affine_select(out=before[0:R, :], in_=ones[0:R, 0:R], compare_op=ALU.is_gt, fill=0.0,
                                               base=0, pattern=[[-1, R]], channel_multiplier=1))
                    ch.link(pool.memset(block_mask[:, :], 0.0))
                    pool.memset(block_mask[0:64, 0:64], 1.0)
                    ch.link(pool.memset(block_mask[64:P, 64:P], 1.0))
                    ch.link(pool.iota(node_no[:, :], pattern=[[0, 1]], base=N, channel_multiplier=1,
                                      allow_small_or_imprecise_dtypes=True))
                    ch.link(pool.tensor_copy(delta_sel[:, :], ident[0:ATT_ROWS, :]))
                    ch.link(pool.affine_select(out=delta_sel[:, 0:63], in_=delta_sel[:, 0:63],
                                               compare_op=ALU.not_equal, fill=-1.0, base=-63,
                                               pattern=[[0, 63]], channel_multiplier=1))
                    ch.link(pool.memset(delta_sel[:, 63:64], 0.0))
                    pool.memset(v_aug[:, :, ATT_DH:ATT_DH + 1], 1.0)
                    pool.memset(ks_acc[:, :], 0.0).then_inc(s_const, 1)

                @block.tensor
                def _(pe):
                    pe.wait_ge(s_const, 1)
                    pe.wait_ge(s_att, after["norm"])
                    pe.wait_ge(s_att_in, 16 * 7)
                    for c in range(KC):
                        pe.transpose(bank[0][:, c * 64:c * 64 + 64], x64[:, c * P:c * P + P], ident[0:64, 0:64])
                    for m in range(2):
                        t = pe.transpose(bank[1][:, m * P:m * P + P], proj2[:, m, :], ident[:, :])
                    t.then_inc(s_att, 1)
                    pe.wait_ge(s_att, after["turned"])
                    for w in range(3):
                        for c in range(KC):
                            m = pe.matmul(bank[2 + w][0:64, :], x64_t[:, c, :], g_w[w][:, c, :],
                                          start=(c == 0), stop=(c == KC - 1))
                    m.then_inc(s_att, 1)
                    pe.wait_ge(s_att, after["scaled"])
                    for w in range(2):
                        for c in range(KC):
                            t = pe.transpose(bank[w][:, c * 64:c * 64 + 64], qk[:, w, c * P:c * P + P], ident[0:64, 0:64])
                    t.then_inc(s_att, 1)
                    pe.wait_ge(s_att, after["turned2"])
                    for w in range(2):
                        for h in range(ATT_HEADS):
                            b = 64 * (h % 2)
                            g, at = 2 * (h % 2) + h // 4, h // 2 % 2
                            m = pe.matmul(bank[(2 + 4 * w + g) % 8][0:64, at * ATT_M:(at + 1) * ATT_M],
                                          qk_t[b:b + 64, w, h // 2, :], proj_t[b:b + 64, :], start=True, stop=True)
                    m.then_inc(s_att, 1)
                    pe.wait_ge(s_att, after["top"])
                    pe.transpose(bank[2][0:8, 0:64], top_u[:, 1, :], ident[0:64, 0:64]).then_inc(s_att, 1)
                    pe.wait_ge(s_att, after["top_d"])
                    pe.matmul(bank[2][0:64, 64:72], ones[0:8, 0:64], top_d[:, :], start=True, stop=True).then_inc(s_att, 1)
                    pe.wait_ge(s_att, after["phi"])
                    for hm in range(2 * ATT_HEADS):
                        h, m = hm // 2, hm % 2
                        pe.transpose(bank[2 + hm // 8][:, (hm % 8) * 64:(hm % 8) * 64 + 64],
                                     feat[:, 0, h, m * P:m * P + P], ident[0:64, 0:64])
                    for hm in range(2 * ATT_HEADS):
                        h, m = hm // 2, hm % 2
                        mm = pe.matmul(bank[4 + hm // 4][:, (hm % 4) * 65:(hm % 4) * 65 + 65],
                                       feat[:, 1, h, m * P:m * P + P], v_aug[:, h, :], start=True, stop=True)
                    mm.then_inc(s_att, 1)
                    pe.wait_ge(s_att, after["kv_copy"])
                    for h in range(ATT_HEADS):
                        for m in range(2):
                            mm = pe.matmul(bank[h // 4][0:64, (h % 4) * 65:(h % 4) * 65 + 65],
                                           qf_t[:, 2 * h + m, :], kv_aug[:, 2 * h + m, :], start=(m == 0), stop=(m == 1))
                    mm.then_inc(s_att, 1)
                    pe.wait_ge(s_att, after["att_z"])
                    for c in range(KC):
                        t = pe.transpose(bank[2][:, c * 64:c * 64 + 64], att[:, c * P:c * P + P], ident[0:64, 0:64])
                    t.then_inc(s_att, 1)
                    pe.wait_ge(s_att, after["turned3"])
                    for c in range(KC):
                        m = pe.matmul(bank[3][0:64, :], att_t[:, c, :], g_w[3][:, c, :], start=(c == 0), stop=(c == KC - 1))
                    m.then_inc(s_att, 1)
                    pe.wait_ge(s_att, after["wo_copy"])
                    pe.matmul(bank[4][:, :], delta_sel[:, :], att_out[:, :], start=True, stop=True).then_inc(s_att, 1)
                    pe.wait_ge(s_wqk, 16)
                    pe.wait_ge(s_bd, 16 * 8)
                    for n in range(8):
                        wait(pe, s_turned, n)
                        for c in range(KC):
                            t = pe.transpose(bank[5][:, c * P:c * P + P], w_qk[:, c, n * P:n * P + P], ident[:, :])
                        t.then_inc(s_turn, 1)
                        pe.wait_ge(s_turned, n + 1)
                        wait(pe, s_fcopy, n)
                        for c in range(KC):
                            m = pe.matmul(bank[6][:, c * P:c * P + P], w_turned[:, c * P:c * P + P],
                                          proj_bd[:, n % 4, :], start=True, stop=True)
                        m.then_inc(s_fused, 1)
                    pe.wait_ge(s_idx_f, 1)
                    for k in range(2):
                        t = pe.transpose(bank[7][0:R, k * P:k * P + NT], idx_f[:, k, :], ident[0:NT, 0:NT])
                    t.then_inc(s_idx_t, 1)

                @block.scalar
                def _(act):
                    act.wait_ge(s_att, after["var"])
                    act.activation(small[:, 0:1], mv[:, 1:2], ACT.Sqrt).then_inc(s_att, 1)
                    act.wait_ge(s_att, after["turn"])
                    act.activation(x64_t[:, :, :].rearrange("p c n -> p (c n)"), bank[0][:, 0:256], ACT.Copy)
                    act.activation(proj_t[:, :], bank[1][:, 0:256], ACT.Copy).then_inc(s_att, 1)
                    act.wait_ge(s_att, after["turn2"])
                    for w in range(2):
                        i = act.activation(qk_t[:, w, :, :].rearrange("p c n -> p (c n)"), bank[w][:, 0:256], ACT.Copy)
                    i.then_inc(s_att, 1)
                    act.wait_ge(s_att, after["arg"])
                    act.activation(feat[:, :, :, :].rearrange("p a h m -> p (a h m)"),
                                   feat[:, :, :, :].rearrange("p a h m -> p (a h m)"), ACT.Exp).then_inc(s_att, 1)
                    act.wait_ge(s_att, after["kv"])
                    for k in range(2):
                        act.activation(qf_t[:, 8 * k:8 * k + 8, :].rearrange("p a n -> p (a n)"), bank[2 + k][:, :], ACT.Copy)
                    for k in range(4):
                        i = act.activation(kv_aug[:, 4 * k:4 * k + 4, :].rearrange("p a n -> p (a n)"),
                                           bank[4 + k][:, 0:260], ACT.Copy)
                    i.then_inc(s_att, 1)
                    act.wait_ge(s_att, after["turn3"])
                    act.activation(att_t[:, :, :].rearrange("p c n -> p (c n)"), bank[2][:, 0:256], ACT.Copy).then_inc(s_att, 1)
                    act.wait_ge(s_att, after["wo"])
                    act.activation(att_out[:, :], bank[3][0:64, :], ACT.Copy).then_inc(s_att, 1)
                    act.wait_ge(s_att, after["delta"])
                    act.activation(att_delta[:, :], bank[4][:, :], ACT.Copy).then_inc(s_att, 1)
                    for n in range(8):
                        act.wait_ge(s_turn, n + 1)
                        wait(act, s_fused, n)
                        act.activation(w_turned[:, :], bank[5][:, :], ACT.Copy).then_inc(s_turned, 1)

                @block.vector
                def _(dve):
                    ch = Chain(dve, s_chain)
                    dve.wait_ge(s_att_in, 16 * 7)
                    ch.link(dve.bn_stats(bn6[:, :], x64[:, :]))
                    ch.link(dve.bn_aggr(mv[:, :], bn6[:, :]))
                    dve.tensor_scalar_add(mv[:, 1:2], mv[:, 1:2], LN_EPS).then_inc(s_att, 1)
                    dve.wait_ge(s_att, after["std"])
                    inverse_root(ch, dve, small[:, 1:2], small[:, 0:1], mv[:, 1:2], small[:, 2:3])
                    dve.tensor_scalar(x64[:, :], x64[:, :], mv[:, 0:1], small[:, 1:2], ALU.subtract, ALU.mult).then_inc(s_att, 1)
                    dve.wait_ge(s_const, 1)
                    dve.wait_ge(s_att, after["qkv"])
                    for w in range(2):
                        ch.link(dve.tensor_scalar(qk[:, w, :], bank[2 + w][0:64, :], ATT_DH ** -0.25, None, ALU.mult))
                    dve.tensor_copy(v_aug[:, :, 0:ATT_DH],
                                    bank[4][0:64, :].rearrange("p (h d) -> p h d", h=ATT_HEADS)).then_inc(s_att, 1)
                    for w in range(2):
                        ch.link(dve.tensor_tensor(sq[:, w, :], qk[:, w, :], qk[:, w, :], ALU.mult))
                    ch.link(dve.tensor_reduce(diag[:, :, :], sq[:, :, :].rearrange("p a (h d) -> p a h d", h=ATT_HEADS), AX.X, ALU.add))
                    ch.link(dve.tensor_scalar(diag[:, :, :], diag[:, :, :], 0.5, None, ALU.mult))
                    dve.wait_ge(s_att, after["u"])
                    for w in range(2):
                        for g in range(4):
                            u = bank[(2 + 4 * w + g) % 8][0:64, :].rearrange("p (h m) -> p h m", h=2)
                            h = 4 * (g % 2) + g // 2
                            i = dve.tensor_reduce(top_u[:, w, h:h + 3:2], u, AX.X, ALU.max)
                    ch.link(i)
                    for w in range(2):
                        for g in range(4):
                            u = bank[(2 + 4 * w + g) % 8][0:64, :].rearrange("p (h m) -> p h m", h=2)
                            h = 4 * (g % 2) + g // 2
                            i = dve.tensor_tensor(feat[:, w, h:h + 3:2, :], u,
                                                  diag[:, w, h:h + 3:2, None].broadcast_to([ATT_ROWS, 2, ATT_M]), ALU.subtract)
                    i.then_inc(s_att, 1)
                    dve.wait_ge(s_att, after["turn_top"])
                    ch.link(dve.tensor_reduce(top_k[:, :], bank[2][0:8, 0:64], AX.X, ALU.max))
                    dve.tensor_scalar(top_d[:, :], ident[0:8, 0:8], top_k[:, 0:1], None, ALU.mult).then_inc(s_att, 1)
                    dve.wait_ge(s_att, after["top_b"])
                    ch.link(dve.tensor_copy(top_u[:, 1, :], bank[2][0:64, 64:72]))
                    for w in range(2):
                        i = dve.tensor_tensor(feat[:, w, :, :], feat[:, w, :, :],
                                              top_u[:, w, :, None].broadcast_to([ATT_ROWS, ATT_HEADS, ATT_M]), ALU.subtract)
                    i.then_inc(s_att, 1)
                    dve.wait_ge(s_att, after["exp"])
                    dve.tensor_scalar(feat[:, :, :, :].rearrange("p a h m -> p (a h m)"),
                                      feat[:, :, :, :].rearrange("p a h m -> p (a h m)"),
                                      ATT_M ** -0.5, ATT_KEPS, ALU.mult, ALU.add).then_inc(s_att, 1)
                    dve.wait_ge(s_att, after["att"])
                    for k in range(2):
                        num = bank[k][0:64, 0:260].rearrange("p (h d) -> p h d", h=4)
                        ch.link(dve.tensor_scalar(z_att[:, 4 * k:4 * k + 4, None], num[:, :, 64:65], ATT_KEPS, None, ALU.add))
                    ch.link(dve.reciprocal(z_att[:, :], z_att[:, :]))
                    for k in range(2):
                        num = bank[k][0:64, 0:260].rearrange("p (h d) -> p h d", h=4)
                        i = dve.tensor_tensor(att[:, 256 * k:256 * k + 256].rearrange("p (h d) -> p h d", h=4),
                                              num[:, :, 0:64], z_att[:, 4 * k:4 * k + 4, None].broadcast_to([ATT_ROWS, 4, 64]), ALU.mult)
                    i.then_inc(s_att, 1)
                    for n in range(8):
                        dve.wait_ge(s_fused, n + 1)
                        to = (phi_q, phi_k)[n // 4][:, :, (n % 4) * P:(n % 4) * P + P]
                        dve.tensor_copy(to, bank[6][:, :].rearrange("p (c f) -> p c f", c=KC)).then_inc(s_fcopy, 1)
                    dve.wait_ge(s_idx, 32)
                    dve.tensor_copy(idx_f[:, :, :], idx_in[:, :, :]).then_inc(s_idx_f, 1)
                    dve.wait_ge(s_idx_t, 1)
                    ch.link(dve.tensor_copy(src_i[0:R, :], bank[7][0:R, 0:NT]))
                    ch.link(dve.tensor_copy(dst_f[0:R, :], bank[7][0:R, P:P + NT]))
                    ch.link(dve.tensor_scalar(spare[0:R, :], dst_f[0:R, :], -1.0, node_no[0:R, 0:1], ALU.mult, ALU.add))
        with ExitStack() as st:
            x_in = [sb(st, f"x_in{i}", [P, C, D]) for i in range(2)]
            xn = [sb(st, f"xn{i}", [P, C, D]) for i in range(2)]
            xn_t = sb(st, "xn_t", [P, KC, G])
            gat = [sb(st, f"gat{i}", [P, C, D]) for i in range(2)]
            src_now = [sb(st, f"src_now{i}", [P, C], I32) for i in range(2)]
            dst_now = [sb(st, f"dst_now{i}", [P, C], I32) for i in range(2)]
            same = [sb(st, f"same{i}", [P, C, R]) for i in range(2)]
            count = [sb(st, f"count{i}", [P, C]) for i in range(2)]
            repeat = sb(st, "repeat", [P, C])
            scratch = sb(st, "scratch", [P, R])
            sums = sb(st, "sums", [P, C, AGG_W])
            low = sb(st, "low", [P, 2, D])
            ph = sb(st, "ph", [P, 2, D])
            bn = sb(st, "bn", [P, 2, C, 6])
            st_mv = sb(st, "st_mv", [P, 2, C, 2])
            st_std = sb(st, "st_std", [P, 2, C])
            st_tmp = sb(st, "st_tmp", [P, 2, C])
            st_rstd = sb(st, "st_rstd", [P, 2, C])

            s_x = [sem(f"s_x{i}") for i in range(2)]
            s_gat = [sem(f"s_gat{i}") for i in range(2)]
            s_src = sem("s_src")
            s_var = sem("s_var")
            s_std = sem("s_std")
            s_xn = sem("s_xn")
            s_gn = sem("s_gn")
            s_t = sem("s_t")
            s_tc = sem("s_tc")
            s_k = sem("s_k")
            s_low = sem("s_low")
            s_exp = sem("s_exp")
            s_ph = sem("s_ph")
            s_g = sem("s_g")
            s_acc = sem("s_acc")
            s_e = sem("s_e")
            s_ec = sem("s_ec")
            s_scat = sem("s_scat")
            s_col = sem("s_col")
            s_ch = sem("s_ch1")
            CHAIN = 30

            with nc.Block() as block:
                @block.sync
                def _(sp):
                    def load(s, par, half):
                        wait(sp, s_xn, (s - 1) * C if not isinstance(s, int) or s >= 2 else 0)
                        dma_rows(sp, x_in[par][0:R], x_g[s], s_x[par])
                    groups(sp, load)

                @block.gpsimd
                def _(pool):
                    pool.memset(sums[:, :, D + 1:AGG_W], 0.0).then_inc(s_ch, 1)

                    def gather(s, par):
                        pool.wait_ge(s_src, s + 1)
                        wait(pool, s_e, (s - 1) * C if not isinstance(s, int) or s >= 2 else 0)
                        settle(pool, s_past_pool)
                        for c in range(C):
                            pool.indirect_dma_start(
                                out=gat[par][0:R, c, :], out_offset=None, in_=a["x"],
                                in_offset=bass.IndirectOffsetOnAxis(ap=src_now[par][0:R, c:c + 1], axis=0),
                            ).then_inc(s_gat[par], 16)

                    def scatter(s, par):
                        for c in range(C):
                            pool.wait_ge(s_ec, s * C + c + 1)
                            wait(pool, s_scat, (s * C + c) * 16)
                            settle(pool, s_past_pool)
                            pool.indirect_dma_start(
                                out=agg, in_=sums[0:R, c, :], in_offset=None, compute_op=ALU.add,
                                out_offset=bass.IndirectOffsetOnAxis(ap=dst_now[par][0:R, c:c + 1], axis=0),
                            ).then_inc(s_scat, 16)

                    def step(s, par, half):
                        gather(s, par)
                        if not isinstance(s, int) or s >= 1:
                            scatter(s - 1, 1 - par)
                    groups(pool, step)
                    scatter(NG - 1, (NG - 1) % 2)
                    pool.wait_ge(s_scat, 16 * NT)

                @block.tensor
                def _(pe):
                    def turn(s, par):
                        for c in range(C):
                            if c == 0:
                                pe.wait_ge(s_xn, (s + 1) * C)
                            n = s * KC + c
                            wait(pe, s_tc, n - 1)
                            if c == 1:
                                wait(pe, s_ec, (s - 1) * C)
                            for j in range(C):
                                t = pe.transpose(bank[4 + c % 2][:, j * R:j * R + R],
                                                 xn[par][0:R, j, c * P:c * P + P], ident[0:R, 0:R])
                            t.then_inc(s_t, 1)

                    def keys(s, j):
                        if j == 0:
                            pe.wait_ge(s_tc, (s + 1) * KC)
                        wait(pe, s_ph, s * C + j - 1)
                        for c in range(KC):
                            m = pe.matmul(bank[6 + j % 2][0:R, :], xn_t[:, c, j * R:j * R + R], phi_k[:, c, :],
                                          start=(c == 0), stop=(c == KC - 1))
                        m.then_inc(s_k, 1)

                    def edges(s, par, j):
                        if j == 0:
                            pe.wait_ge(s_gn, s + 1)
                        wait(pe, s_ec, s * C + j)
                        pe.matmul(bank[5][0:R, :], same[par][0:R, j, :], gat[par][0:R, j, :],
                                  start=True, stop=True).then_inc(s_e, 1)

                    def products(s, par, j):
                        pe.wait_ge(s_ph, s * C + j + 1)
                        for f in range(KC):
                            m = pe.matmul(bank[f][:, :], ph[0:R, j % 2, f * P:f * P + P], xn[par][0:R, j, :],
                                          start=(isinstance(s, int) and s == 0 and j == 0),
                                          stop=(isinstance(s, int) and s == NG - 1 and j == C - 1))
                        m.then_inc(s_g, 1)

                    def step(s, par, half):
                        for j in range(C):
                            keys(s, j)
                            if not isinstance(s, int) or s >= 1:
                                edges(s - 1, 1 - par, j)
                            if j >= 1:
                                products(s, par, j - 1)
                        products(s, par, C - 1)
                        if not isinstance(s, int) or s < NG - 1:
                            turn(s + 1, 1 - par)
                    turn(0, 0)
                    groups(pe, step)
                    for j in range(C):
                        edges(NG - 1, (NG - 1) % 2, j)

                @block.scalar
                def _(act):
                    def root_x(s):
                        act.wait_ge(s_var, 2 * s + 2 if not isinstance(s, int) or s >= 0 else 1)
                        act.activation(st_std[0:R, 0, :], st_mv[0:R, 0, :, 1], ACT.Sqrt).then_inc(s_std, 1)

                    def root_g(s):
                        act.wait_ge(s_var, 2 * s + 3 if not isinstance(s, int) or s < NG - 1 else 2 * NG)
                        act.activation(st_std[0:R, 1, :], st_mv[0:R, 1, :, 1], ACT.Sqrt).then_inc(s_std, 1)

                    def exp(s, j):
                        act.wait_ge(s_low, s * C + j + 1)
                        act.activation(low[0:R, j % 2, :], low[0:R, j % 2, :], ACT.Exp).then_inc(s_exp, 1)

                    def copy_sums(s, par, j):
                        act.wait_ge(s_e, s * C + j + 1)
                        wait(act, s_scat, 16 * (s * C + j - C + 1))
                        act.activation(sums[0:R, j, D:D + 1], count[par][0:R, j:j + 1], ACT.Copy)
                        act.activation(sums[0:R, j, 0:D], bank[5][0:R, :], ACT.Copy).then_inc(s_ec, 1)

                    def copy_turned(s):
                        for c in range(KC):
                            act.wait_ge(s_t, s * KC + c + 1)
                            if c == 0:
                                wait(act, s_col, s)
                            act.activation(xn_t[:, c, :], bank[4 + c % 2][:, 0:G], ACT.Copy).then_inc(s_tc, 1)

                    act.wait_ge(s_ch, 1)
                    root_x(-1)
                    copy_turned(0)

                    def step(s, par, half):
                        for j in range(C):
                            exp(s, j)
                            if not isinstance(s, int) or s >= 1:
                                copy_sums(s - 1, 1 - par, j)
                            if j == 0 and (not isinstance(s, int) or s < NG - 1):
                                root_x(s)
                            if j == 2:
                                root_g(s)
                        if not isinstance(s, int) or s < NG - 1:
                            copy_turned(s + 1)

                    groups(act, step)
                    for j in range(C):
                        copy_sums(NG - 1, (NG - 1) % 2, j)

                @block.vector
                def _(dve):
                    def variances(ch, s, rows, k):
                        for c in range(C):
                            i = dve.bn_stats(bn[0:R, k, c, :], rows[0:R, c, :])
                        ch.link(i)
                        settle(dve, s_past_dve)
                        for c in range(C):
                            i = dve.bn_aggr(st_mv[0:R, k, c, :], bn[0:R, k, c, :])
                        ch.link(i)
                        dve.tensor_scalar(st_mv[0:R, k, :, 1], st_mv[0:R, k, :, 1], LN_EPS, None, ALU.add).then_inc(s_var, 1)

                    def normalise(ch, rows, out_rows, k, last):
                        inverse_root(ch, dve, st_rstd[0:R, k, :], st_std[0:R, k, :], st_mv[0:R, k, :, 1], st_tmp[0:R, k, :])
                        for c in range(C):
                            i = dve.tensor_scalar(out_rows[0:R, c, :], rows[0:R, c, :], st_mv[0:R, k, c, 0:1],
                                                  st_rstd[0:R, k, c:c + 1], ALU.subtract, ALU.mult)
                            if last is not None:
                                i.then_inc(last, 1)
                        return i

                    def x_variances(ch, s, par, half):
                        dve.wait_ge(s_x[par], 32 * (half + 1))
                        variances(ch, s, x_in[par], 0)

                    def x_normalise(ch, s, par):
                        dve.wait_ge(s_std, 2 * s if not isinstance(s, int) or s > 0 else 1)
                        wait(dve, s_g, (s - 1) * C if not isinstance(s, int) or s >= 2 else 0)
                        normalise(ch, x_in[par], xn[par], 0, s_xn)
                        ch.link(dve.tensor_copy(row_stat[0:R, s, 0, :], st_mv[0:R, 0, :, 0]))
                        ch.link(dve.tensor_copy(row_stat[0:R, s, 1, :], st_rstd[0:R, 0, :]))

                    def sources(s, par, half):
                        wait(dve, s_gat[par], 64 * half)
                        dve.tensor_copy(src_now[par][0:R, :], src_i[0:R, bass.ds(s * C, C)]).then_inc(s_src, 1)

                    def phi(ch, s, j):
                        dve.wait_ge(s_k, s * C + j + 1)
                        dve.tensor_scalar(low[0:R, j % 2, :], bank[6 + j % 2][0:R, :], 0.0, None, ALU.min).then_inc(s_low, 1)
                        dve.wait_ge(s_exp, s * C + j + 1)
                        wait(dve, s_g, s * C + j - 1)
                        dve.scalar_tensor_tensor(ph[0:R, j % 2, :], bank[6 + j % 2][0:R, :], 0.0, low[0:R, j % 2, :],
                                                 ALU.max, ALU.add).then_inc(s_ph, 1)
                        dve.wait_ge(s_ph, s * C + j + 1)
                        ch.link(dve.tensor_tensor(ks_acc[0:R, :], ks_acc[0:R, :], ph[0:R, j % 2, :], ALU.add))

                    def repeats(ch, s, par):
                        wait(dve, s_e, (s - 1) * C if not isinstance(s, int) or s >= 2 else 0)
                        wait(dve, s_scat, 16 * (s - 1) * C if not isinstance(s, int) or s >= 2 else 0)
                        for c in range(C):
                            dst_c = dst_f[0:R, bass.ds(s * C + c, 1)]
                            ch.link(dve.tensor_scalar(same[par][0:R, c, :], dst_rows[0:R, bass.ds(s * G + c * R, R)], dst_c, None,
                                                      ALU.is_equal, ALU.add, accum_out=count[par][0:R, c:c + 1]))
                            i = dve.tensor_tensor_reduce(scratch[0:R, :], same[par][0:R, c, :], before[0:R, :], 1.0, 0.0,
                                                         ALU.mult, ALU.add, repeat[0:R, c:c + 1])
                            ch.link(i)
                        ch.link(dve.scalar_tensor_tensor(repeat[0:R, :], repeat[0:R, :], 0.0, spare[0:R, bass.ds(s * C, C)],
                                                         ALU.is_gt, ALU.mult))
                        ch.link(dve.tensor_tensor(dst_now[par][0:R, :], repeat[0:R, :], dst_f[0:R, bass.ds(s * C, C)], ALU.add))

                    def step(s, par, half):
                        ch = Chain(dve, s_ch, 1 + FIRST + s * CHAIN)
                        more = not isinstance(s, int) or s < NG - 1
                        for j in range(C):
                            phi(ch, s, j)
                            if j == 0 and more:
                                sources(s + 1, 1 - par, half + par)
                                x_variances(ch, s + 1, 1 - par, half + par)
                            if j == 1 and more:
                                x_normalise(ch, s + 1, 1 - par)
                            if j == 1:
                                dve.wait_ge(s_tc, (s + 1) * KC)
                                for c in range(KC):
                                    i = dve.bn_stats(bn_part[:, c, bass.ds(s * 6, 6)], xn_t[:, c, :])
                                i.then_inc(s_col, 1)
                            if j == 2:
                                dve.wait_ge(s_gat[par], 64 * (half + 1))
                                variances(ch, s, gat[par], 1)
                                repeats(ch, s, par)
                            if j == 3:
                                dve.wait_ge(s_std, 2 * s + 3 if more else 2 * NG)
                                normalise(ch, gat[par], gat[par], 1, None).then_inc(s_gn, 1)
                        assert not more or ch.n == CHAIN, ch.n

                    FIRST = 9
                    ch = Chain(dve, s_ch, 1)
                    dve.wait_ge(s_ch, 1)
                    sources(0, 0, 0)
                    x_variances(ch, 0, 0, 0)
                    x_normalise(ch, 0, 0)
                    assert ch.n == FIRST
                    groups(dve, step)
        first.close()

        ffn = ExitStack()
        w1 = sb(ffn, "w1", [P, KC, 2 * EXPERTS * FF + FF])
        w2 = sb(ffn, "w2", [P, FC, D])
        wr = sb(ffn, "wr", [P, KC, 2 * EXPERTS])
        br = sb(ffn, "br", [1, 2 * EXPERTS])
        b1 = sb(ffn, "b1", [P, FC])
        scale2 = sb(ffn, "scale2", [P, D])
        shift2 = sb(ffn, "shift2", [P, D])
        s_ffn = sem("s_ffn")
        FFN_DMAS = 22

        def load_experts(eng):
            n = 0
            for k, bank_name in enumerate(("sp", "fq")):
                for c in range(KC):
                    to = w1[:, c, k * 512:k * 512 + 512].rearrange("p (e f) -> p e f", e=EXPERTS)
                    eng.dma_start(to, a["L0_ffn_W1_" + bank_name][:, c * P:c * P + P, :].rearrange("e p f -> p e f")).then_inc(s_ffn, 16)
                    n += 1
                two = a["L0_ffn_W2_" + bank_name].rearrange("e f d -> (e f) d").rearrange("(c p) d -> p c d", p=P)
                eng.dma_start(w2[:, 4 * k:4 * k + 4, :], two).then_inc(s_ffn, 16)
                eng.dma_start(w2[64 + 8 * k:72 + 8 * k, 8, :], a["L0_ffn_b2_" + bank_name]).then_inc(s_ffn, 16)
                eng.dma_start(wr[:, :, 8 * k:8 * k + 8], a["L0_ffn_Wr_" + bank_name].rearrange("(c p) e -> p c e", p=P)).then_inc(s_ffn, 16)
                eng.dma_start(br[:, 8 * k:8 * k + 8], a["L0_ffn_br_" + bank_name].rearrange("(a e) -> a e", a=1)).then_inc(s_ffn, 16)
                eng.dma_start(b1[:, 4 * k:4 * k + 4], a["L0_ffn_b1_" + bank_name].rearrange("e f -> (e f)").rearrange("(c p) -> p c", p=P), allow_slow_non_contiguous=True).then_inc(s_ffn, 16)
                n += 5
            eng.dma_start(w1[:, :, 1024:1088], a["L0_ffn_Ws1"].rearrange("(c p) f -> p c f", p=P)).then_inc(s_ffn, 16)
            eng.dma_start(w2[0:64, 8, :], a["L0_ffn_Ws2"]).then_inc(s_ffn, 16)
            eng.dma_start(w2[80:81, 8, :], a["L0_ffn_bs2"].rearrange("(a d) -> a d", a=1)).then_inc(s_ffn, 16)
            eng.dma_start(b1[0:64, 8:9], a["L0_ffn_bs1"].rearrange("(f a) -> f a", a=1), allow_slow_non_contiguous=True).then_inc(s_ffn, 16)
            assert n + 4 == FFN_DMAS

        conv_rows = sb(ffn, "conv_rows", [2, D])
        with ExitStack() as st:
            g_all = sb(st, "g_all", [P, KC, D])
            g_t = sb(st, "g_t", [P, KC, D])
            kv_bd = sb(st, "kv_bd", [P, KC, P])
            gamma = sb(st, "gamma", [P, KC])
            beta = sb(st, "beta", [P, KC])
            col = sb(st, "col", [P, KC, 2])
            col_std = sb(st, "col_std", [P, KC])
            col_tmp = sb(st, "col_tmp", [P, KC])
            scale1 = sb(st, "scale1", [P, KC])
            shift1 = sb(st, "shift1", [P, KC])

            s_mid_in = sem("s_mid_in")
            s_col_var = sem("s_col_var")
            s_col_std = sem("s_col_std")
            s_shift = sem("s_shift")
            s_tw = sem("s_tw")
            s_kv = sem("s_kv")
            s_ch = sem("s_ch2")
            STAGES2 = ["g_copy", "turn_g", "gt", "kv", "bd", "kvp", "done"]
            now = {name: i + 1 for i, name in enumerate(STAGES2)}

            with nc.Block() as block:
                @block.sync
                def _(sp):
                    sp.dma_start(gamma[:, :], a["L0_gnn_norm1_g"].rearrange("(c p) -> p c", p=P), allow_slow_non_contiguous=True).then_inc(s_mid_in, 16)
                    sp.dma_start(beta[:, :], a["L0_gnn_norm1_b"].rearrange("(c p) -> p c", p=P), allow_slow_non_contiguous=True).then_inc(s_mid_in, 16)
                    sp.dma_start(conv_rows[1:2, :], a["L0_gnn_b_conv"].rearrange("(a d) -> a d", a=1)).then_inc(s_mid_in, 16)
                    load_experts(sp)

                @block.scalar
                def _(act):
                    for f in range(KC):
                        i = act.activation(g_all[:, f, :], bank[f][:, :], ACT.Copy)
                    i.then_inc(s_kv, 1)
                    act.wait_ge(s_col_var, 1)
                    act.activation(col_std[:, :], col[:, :, 1], ACT.Sqrt).then_inc(s_col_std, 1)
                    act.wait_ge(s_kv, now["turn_g"])
                    for c in range(KC):
                        i = act.activation(g_t[:, c, :], bank[4 + c][:, :], ACT.Copy)
                    i.then_inc(s_kv, 1)
                    act.wait_ge(s_kv, now["kvp"])
                    for f in range(KC):
                        i = act.activation(kvp[:, f, :], bank[f][:, :], ACT.Copy)
                    i.then_inc(s_kv, 1)

                @block.tensor
                def _(pe):
                    pe.wait_ge(s_kv, now["g_copy"])
                    for c in range(KC):
                        for f in range(KC):
                            t = pe.transpose(bank[4 + c][:, f * P:f * P + P], g_all[:, f, c * P:c * P + P], ident[:, :])
                    t.then_inc(s_kv, 1)
                    pe.wait_ge(s_kv, now["gt"])
                    for h in range(KC):
                        for c in range(KC):
                            m = pe.matmul(bank[0][:, h * P:h * P + P], w_v[:, c, h * P:h * P + P],
                                          g_t[:, c, h * P:h * P + P], start=(c == 0), stop=(c == KC - 1))
                    m.then_inc(s_kv, 1)
                    for f in range(KC):
                        m = pe.matmul(bank[4][:, f:f + 1], ks_acc[0:R, f * P:f * P + P], ones[0:R, 0:1], start=True, stop=True)
                    pe.wait_ge(s_shift, 1)
                    pe.wait_ge(s_mid_in, 48)
                    for c in range(KC):
                        m = pe.matmul(bank[5][0:1, :], shift1[:, c:c + 1], w_conv[:, c, :], start=(c == 0), stop=(c == KC - 1))
                    m.then_inc(s_tw, 1)
                    pe.wait_ge(s_kv, now["bd"])
                    for h in range(KC):
                        m = pe.matmul(bank[h][:, :], kv_bd[:, h, :], w_proj[:, h, :], start=True, stop=True)
                    m.then_inc(s_kv, 1)

                @block.vector
                def _(dve):
                    ch = Chain(dve, s_ch)
                    for c in range(KC):
                        i = dve.bn_aggr(col[:, c, :], bn_part[:, c, :])
                    ch.link(i)
                    dve.tensor_scalar(col[:, :, 1], col[:, :, 1], BN_EPS, None, ALU.add).then_inc(s_col_var, 1)
                    dve.wait_ge(s_col_std, 1)
                    inverse_root(ch, dve, scale1[:, :], col_std[:, :], col[:, :, 1], col_tmp[:, :])
                    dve.wait_ge(s_mid_in, 48)
                    ch.link(dve.tensor_tensor(scale1[:, :], scale1[:, :], gamma[:, :], ALU.mult))
                    ch.link(dve.tensor_tensor(shift1[:, :], col[:, :, 0], scale1[:, :], ALU.mult))
                    dve.tensor_tensor(shift1[:, :], beta[:, :], shift1[:, :], ALU.subtract).then_inc(s_shift, 1)
                    dve.wait_ge(s_kv, now["kv"])
                    dve.tensor_tensor(kv_bd[:, :, :], bank[0][:, :].rearrange("p (h f) -> p h f", h=KC),
                                      block_mask[:, None, :].broadcast_to([P, KC, P]), ALU.mult).then_inc(s_kv, 1)
                    dve.wait_ge(s_tw, 1)
                    dve.tensor_copy(conv_rows[0:1, :], bank[5][0:1, :])
                    for f in range(KC):
                        dve.tensor_scalar(ks_bd[:, f, :], block_mask[:, :], bank[4][:, f:f + 1], None, ALU.mult)
                        dve.tensor_scalar(w_conv[:, f, :], w_conv[:, f, :], scale1[:, f:f + 1], None, ALU.mult)

        u_acc = sb(ffn, "u_acc", [P, D])
        q_acc = sb(ffn, "q_acc", [P, D])
        with ExitStack() as st:
            xn = [sb(st, f"y_in{i}", [P, C, D]) for i in range(2)]
            agg_in = [sb(st, f"agg_in{i}", [P, C, AGG_W]) for i in range(2)]
            mean = sb(st, "mean", [P, C, D + 2])
            mean_t = sb(st, "mean_t", [P, KC, G])
            deg_t = sb(st, "deg_t", [2, G])
            deg = sb(st, "deg", [P, 2, C])
            now_stat = sb(st, "now_stat", [P, 2, C])
            u = [sb(st, f"u{i}", [P, C, D]) for i in range(2)]
            squares = sb(st, "squares", [P, 2, D])

            s_in = [sem(f"s_in{i}") for i in range(2)]
            s_mean = sem("s_mean")
            s_yn = sem("s_yn")
            s_mt = sem("s_mt")
            s_mc = sem("s_mc")
            s_conv = sem("s_conv")
            s_u = sem("s_u")
            s_sq = sem("s_sq")
            s_q_acc = sem("s_q_acc")
            s_ust = [sem(f"s_ust{i}") for i in range(2)]
            s_ch = sem("s_ch3")
            s_pc = sem("s_pc3")
            CHAIN3 = 6

            with nc.Block() as block:
                @block.sync
                def _(sp):
                    def load(s, par):
                        wait(sp, s_u, (s - 1) * C if not isinstance(s, int) or s >= 2 else 0)
                        dma_rows(sp, agg_in[par][0:R], agg_g[s], s_in[par])
                        dma_rows(sp, xn[par][0:R], x_g[s], s_in[par])

                    def store(s, par):
                        sp.wait_ge(s_u, (s + 1) * C)
                        dma_rows(sp, u_g[s], u[par][0:R], s_ust[par])

                    def step(s, par, half):
                        if not isinstance(s, int) or s < NG - 1:
                            load(s + 1, 1 - par)
                        store(s, par)
                    load(0, 0)
                    groups(sp, step)
                    for i in range(2):
                        sp.wait_ge(s_ust[i], 32 * (NG // 2))
                    sp.wait_ge(s_ffn, 16 * FFN_DMAS)

                @block.gpsimd
                def _(pool):
                    pool.memset(q_acc[:, :], 0.0).then_inc(s_pc, 1)

                    def step(s, par, half):
                        for j in range(C):
                            n = s * C + j
                            pool.wait_ge(s_sq, n + 1)
                            pool.wait_ge(s_q_acc, n) if not isinstance(s, int) or n > 0 else pool.wait_ge(s_pc, 1)
                            pool.tensor_tensor(q_acc[0:R, :], q_acc[0:R, :], squares[0:R, j % 2, :], ALU.add).then_inc(s_q_acc, 1)
                    groups(pool, step)

                @block.tensor
                def _(pe):
                    def turn(s):
                        pe.wait_ge(s_mean, s + 1)
                        for c in range(KC + 1):
                            wait(pe, s_mc, s * (KC + 1) + c - 1)
                            wide = P if c < KC else 2
                            for j in range(C):
                                t = pe.transpose(bank[c % 2][0:wide, j * R:j * R + R],
                                                 mean[0:R, j, c * P:c * P + wide], ident[0:R, 0:R])
                            t.then_inc(s_mt, 1)

                    def conv(s, j):
                        if j == 0:
                            pe.wait_ge(s_mc, (s + 1) * (KC + 1))
                        wait(pe, s_u, s * C + j - 1)
                        to = bank[2 + j % 2][0:R, :]
                        for c in range(KC):
                            pe.matmul(to, mean_t[:, c, j * R:j * R + R], w_conv[:, c, :], start=(c == 0), stop=False)
                        pe.matmul(to, deg_t[:, j * R:j * R + R], conv_rows[:, :], start=False, stop=True).then_inc(s_conv, 1)

                    def step(s, par, half):
                        for j in range(C):
                            conv(s, j)
                        if not isinstance(s, int) or s < NG - 1:
                            turn(s + 1)
                    turn(0)
                    groups(pe, step)

                @block.scalar
                def _(act):
                    def copies(s):
                        for c in range(KC + 1):
                            act.wait_ge(s_mt, s * (KC + 1) + c + 1)
                            if c == 0:
                                wait(act, s_conv, s * C)
                            if c < KC:
                                act.activation(mean_t[:, c, :], bank[c % 2][:, 0:G], ACT.Copy).then_inc(s_mc, 1)
                            else:
                                act.activation(deg_t[:, :], bank[c % 2][0:2, 0:G], ACT.Copy).then_inc(s_mc, 1)

                    def step(s, par, half):
                        for j in range(C):
                            n = s * C + j
                            act.wait_ge(s_u, n + 1)
                            wait(act, s_q_acc, n - 1)
                            act.activation(squares[0:R, j % 2, :], u[par][0:R, j, :], ACT.Square).then_inc(s_sq, 1)
                        if not isinstance(s, int) or s < NG - 1:
                            copies(s + 1)
                    copies(0)
                    groups(act, step)

                @block.vector
                def _(dve):
                    def prepare(ch, s, par, half):
                        dve.wait_ge(s_in[par], 64 * (half + 1))
                        ch.link(dve.tensor_scalar(deg[0:R, 0, :], agg_in[par][0:R, :, D], 1.0, None, ALU.max))
                        ch.link(dve.reciprocal(deg[0:R, 1, :], deg[0:R, 0, :]))
                        wait(dve, s_mt, s * (KC + 1))
                        dve.tensor_scalar(mean[0:R, :, D:D + 1], agg_in[par][0:R, :, D:D + 1], 1.0, None, ALU.min)
                        for c in range(C):
                            i = dve.tensor_scalar(mean[0:R, c, 0:D], agg_in[par][0:R, c, 0:D], deg[0:R, 1, c:c + 1], None, ALU.mult)
                        i.then_inc(s_mean, 1)
                        ch.link(dve.tensor_copy(now_stat[0:R, :, :], row_stat[0:R, s, :, :]))
                        for c in range(C):
                            i = dve.tensor_scalar(xn[par][0:R, c, :], xn[par][0:R, c, :], now_stat[0:R, 0, c:c + 1],
                                                  now_stat[0:R, 1, c:c + 1], ALU.subtract, ALU.mult)
                        ch.link(i)

                    def step(s, par, half):
                        more = not isinstance(s, int) or s < NG - 1
                        ch = Chain(dve, s_ch, 6 + s * 8)
                        wait(dve, s_ust[par], 32 * half)
                        for j in range(C):
                            n = s * C + j
                            dve.wait_ge(s_conv, n + 1)
                            i = dve.scalar_tensor_tensor(u[par][0:R, j, :], bank[2 + j % 2][0:R, :], 0.0, xn[par][0:R, j, :],
                                                         ALU.max, ALU.add)
                            if isinstance(s, int) and n == 0:
                                i.then_inc(s_yn, 1)
                                dve.wait_ge(s_yn, 1)
                                i = dve.tensor_tensor(u[par][0:R, 0, :], u[par][0:R, 0, :], att_delta[0:R, :], ALU.add)
                            i.then_inc(s_u, 1)
                            dve.wait_ge(s_u, n + 1)
                            ch.link(dve.tensor_tensor(u_acc[0:R, :], u_acc[0:R, :], u[par][0:R, j, :], ALU.add))
                            if j == 0 and more:
                                prepare(ch, s + 1, 1 - par, half + par)
                        assert not more or ch.n == 8, ch.n

                    ch = Chain(dve, s_ch)
                    ch.link(dve.memset(u_acc[:, :], 0.0))
                    ch.link(dve.memset(mean[:, :, D + 1:D + 2], 1.0))
                    prepare(ch, 0, 0, 0)
                    assert ch.n == 6
                    groups(dve, step)

        with ExitStack() as st:
            gain = sb(st, "gain", [P, 3, D])
            mu = sb(st, "mu", [P, D])
            var = sb(st, "var", [P, D])
            std = sb(st, "std", [P, D])
            tmp = sb(st, "tmp", [P, D])
            s_gain = sem("s_gain")
            s_tot = sem("s_tot")
            s_v2 = sem("s_v2")
            s_r2 = sem("s_r2")
            s_ch = sem("s_ch4")
            with nc.Block() as block:
                @block.sync
                def _(sp):
                    for k, name in enumerate(("L0_gnn_norm2_g", "L0_gnn_norm2_b", "L0_mix_b_proj")):
                        sp.dma_start(gain[:, k, :], a[name].rearrange("(a d) -> a d", a=1).broadcast_to([P, D])).then_inc(s_gain, 16)

                @block.tensor
                def _(pe):
                    pe.matmul(bank[0][:, :], ones[0:R, :], u_acc[0:R, :], start=True, stop=True)
                    pe.matmul(bank[1][:, :], ones[0:R, :], q_acc[0:R, :], start=True, stop=True).then_inc(s_tot, 1)

                @block.scalar
                def _(act):
                    act.wait_ge(s_v2, 1)
                    act.activation(std[:, :], var[:, :], ACT.Sqrt).then_inc(s_r2, 1)

                @block.vector
                def _(dve):
                    ch = Chain(dve, s_ch)
                    dve.wait_ge(s_tot, 1)
                    ch.link(dve.tensor_scalar(mu[:, :], bank[0][:, :], 1.0 / N, None, ALU.mult))
                    ch.link(dve.tensor_tensor(tmp[:, :], mu[:, :], mu[:, :], ALU.mult))
                    ch.link(dve.scalar_tensor_tensor(var[:, :], bank[1][:, :], 1.0 / N, tmp[:, :], ALU.mult, ALU.subtract))
                    dve.tensor_scalar(var[:, :], var[:, :], 0.0, BN_EPS, ALU.max, ALU.add).then_inc(s_v2, 1)
                    dve.wait_ge(s_r2, 1)
                    inverse_root(ch, dve, scale2[:, :], std[:, :], var[:, :], tmp[:, :])
                    dve.wait_ge(s_gain, 48)
                    ch.link(dve.tensor_tensor(scale2[:, :], scale2[:, :], gain[:, 0, :], ALU.mult))
                    ch.link(dve.tensor_tensor(tmp[:, :], mu[:, :], scale2[:, :], ALU.mult))
                    ch.link(dve.tensor_tensor(shift2[:, :], gain[:, 1, :], gain[:, 2, :], ALU.add))
                    ch.link(dve.tensor_tensor(shift2[:, :], shift2[:, :], tmp[:, :], ALU.subtract))
        with ExitStack() as st:
            x_in = [sb(st, f"z_in{i}", [P, C, D]) for i in range(2)]
            base = [sb(st, f"base{i}", [P, C, D]) for i in range(2)]
            x1 = [sb(st, f"x1_{i}", [P, C, D]) for i in range(2)]
            xn, x2 = w_conv, w_v
            xn_t = sb(st, "zn_t", [P, KC, G])
            low = sb(st, "lowq", [P, 2, G])
            qz = sb(st, "qz", [P, KC, G])
            rden = sb(st, "rden", [P, G])
            x2_t = sb(st, "x2_t", [P, KC, G])
            hid = sb(st, "hid", [P, 2, G])
            gated = sb(st, "gated", [P, FC, G])
            now_stat = sb(st, "z_stat", [P, 2, C])
            bn = sb(st, "bnz", [P, C, 6])
            st_mv = sb(st, "mvz", [P, C, 2])
            st_std = sb(st, "stdz", [P, C])
            st_rstd = sb(st, "rstdz", [P, C])
            st_tmp = sb(st, "tmpz", [P, C])
            EB = 2 * EXPERTS
            top_l = sb(st, "top_l", [P, C * 2])
            shifted = sb(st, "shifted", [P, C * 2, EXPERTS])
            expd = sb(st, "expd", [P, C * 2, EXPERTS])
            gate = sb(st, "gate", [P, C * 2])
            descend = sb(st, "descend", [P, EXPERTS])
            pick = sb(st, "pick", [P, C * 2, EXPERTS])
            picked = sb(st, "picked", [P, C * 2])
            one_hot = sb(st, "one_hot", [P, C, EB], BF16)
            carried = sb(st, "carried", [P, EB])
            place = sb(st, "place", [P, C, EB])
            gates = sb(st, "gates", [P, C, EB + 1])
            rest = sb(st, "rest", [P, C, EB])
            parts = sb(st, "parts", [P, C, 3 * EB], BF16)
            parts_t = sb(st, "parts_t", [3 * EB, C, R], BF16)
            spread = sb(st, "spread", [3 * EB, 8, P], BF16)
            upto = sb(st, "upto", [P, P], BF16)
            ones_b = sb(st, "ones_b", [P, P], BF16)
            ident_b = sb(st, "ident_b", [P, P], BF16)

            s_x = [sem(f"s_zx{i}") for i in range(2)]
            s_set = sem("s_set")
            s_base = sem("s_base")
            s_bc = sem("s_bc")
            s_n = sem("s_n")
            s_nt = sem("s_nt")
            s_nc = sem("s_nc")
            s_q = sem("s_q")
            s_ql = sem("s_ql")
            s_qe = sem("s_qe")
            s_qp = sem("s_qp")
            s_den = sem("s_den")
            s_rd = sem("s_rd")
            s_qz = sem("s_qz")
            s_mix = sem("s_mix")
            s_xp = sem("s_xp")
            s_v = sem("s_v")
            s_r = sem("s_r")
            s_x2 = sem("s_x2")
            s_xt = sem("s_xt")
            s_xc = sem("s_xc")
            s_lg = sem("s_lg")
            s_sh = sem("s_sh")
            s_le = sem("s_le")
            s_oh = sem("s_oh")
            s_pos = sem("s_pos")
            s_gate = sem("s_gate")
            s_gt = sem("s_gt")
            s_gc = sem("s_gc")
            s_h = sem("s_h")
            s_ge = sem("s_ge")
            s_mk = sem("s_mk")
            s_hm = sem("s_hm")
            s_y = sem("s_y")
            s_o = sem("s_o")
            s_st = [sem(f"s_st{i}") for i in range(2)]
            s_ch = sem("s_ch5")

            def pipeline(eng, step):
                groups(eng, lambda i, par, half: step(i, par, half, True, not isinstance(i, int) or i > 0))
                step(NG, 0, NG // 2, False, True)

            with nc.Block() as block:
                @block.sync
                def _(sp):
                    def load(i, par):
                        wait(sp, s_xp, (i - 1) * C if not isinstance(i, int) or i >= 2 else 0)
                        dma_rows(sp, x_in[par][0:R], x_g[i], s_x[par])
                        dma_rows(sp, base[par][0:R], u_g[i], s_x[par])

                    def step(i, par, half, front, back):
                        if not isinstance(i, int) or i < NG - 1:
                            load(i + 1, 1 - par)
                        if back:
                            sp.wait_ge(s_o, i * C)
                            dma_rows(sp, out_g[i - 1], x1[1 - par][0:R], s_st[1 - par])
                    load(0, 0)
                    pipeline(sp, step)
                    for k in range(2):
                        sp.wait_ge(s_st[k], 32 * (NG // 2))

                @block.gpsimd
                def _(pool):
                    ch = Chain(pool, s_bc)
                    ch.link(pool.memset(ones_b[:, :], 1.0))
                    ch.link(pool.affine_select(out=upto[:, :], in_=ones_b[:, :], compare_op=ALU.is_ge, fill=0.0,
                                               base=0, pattern=[[1, P]], channel_multiplier=-1))
                    ch.link(pool.tensor_copy(ident_b[:, :], ident[:, :]))
                    ch.link(pool.memset(spread[:, :, :], 0.0))
                    for t in range(3):
                        part = spread[:, :, :].rearrange("k c (e f) -> k c e f", e=2)
                        ch.link(pool.affine_select(out=part, in_=part, compare_op=ALU.not_equal, fill=1.0, base=-t * EB,
                                                   pattern=[[-2, 8], [-1, 2], [0, 64]], channel_multiplier=1))
                    ch.link(pool.iota(descend[:, :], pattern=[[-1, EXPERTS]], base=EXPERTS, channel_multiplier=0,
                                      allow_small_or_imprecise_dtypes=True))
                    pool.memset(gates[:, :, EB:EB + 1], 1.0)
                    pool.memset(carried[:, :], 0.0).then_inc(s_set, 1)

                    def step(i, par, half, front, back):
                        if not front:
                            return
                        ch = Chain(pool, s_bc, 8 + i * 2 * C)
                        pool.wait_ge(s_x[par], 64 * (half + 1))
                        for j in range(C):
                            tile = base[par][0:R, j, :]
                            ch.link(pool.tensor_tensor(tile, tile, scale2[0:R, :], ALU.mult))
                            ch.link(pool.tensor_tensor(tile, tile, shift2[0:R, :], ALU.add))
                            pool.tensor_tensor(tile, tile, x_in[par][0:R, j, :], ALU.add).then_inc(s_base, 1)
                    pipeline(pool, step)

                @block.tensor
                def _(pe):
                    def front_q(i):
                        pe.wait_ge(s_n, i + 1)
                        for c in range(KC):
                            wait(pe, s_rd, i * KC - 1 + c) if c < 2 else wait(pe, s_nc, i * KC + c - 1)
                            for j in range(C):
                                t = pe.transpose(bank[c % 2][:, j * R:j * R + R], xn[0:R, j, c * P:c * P + P], ident[0:R, 0:R])
                            t.then_inc(s_nt, 1)
                        pe.wait_ge(s_nc, (i + 1) * KC)
                        for f in range(KC):
                            wait(pe, s_ge, (i - 1) * FC - 1 + f if not isinstance(i, int) or i >= 2 else 0) if f < 2 \
                                else wait(pe, s_qp, i * KC + f - 1)
                            for c in range(KC):
                                m = pe.matmul(bank[2 + f % 2][:, 0:G], phi_q[:, c, f * P:f * P + P], xn_t[:, c, :],
                                              start=(c == 0), stop=(c == KC - 1))
                            m.then_inc(s_q, 1)

                    def back_logits(b, front):
                        pe.wait_ge(s_x2, b + 1)
                        for c in range(KC):
                            if c >= 2:
                                wait(pe, s_xc, b * KC + c - 1)
                            elif not front:
                                wait(pe, s_rd, b * KC + 3 + c)
                            for j in range(C):
                                t = pe.transpose(bank[c % 2][:, j * R:j * R + R], x2[0:R, j, c * P:c * P + P], ident[0:R, 0:R])
                            t.then_inc(s_xt, 1)
                        pe.wait_ge(s_xc, (b + 1) * KC)
                        wait(pe, s_gc, b)
                        for j in range(C):
                            to = bank[4][0:R, j * EB:j * EB + EB]
                            for c in range(KC):
                                pe.matmul(to, x2_t[:, c, j * R:j * R + R], wr[:, c, :], start=(c == 0), stop=False)
                            m = pe.matmul(to, ones[0:1, 0:R], br[:, :], start=False, stop=True)
                        m.then_inc(s_lg, 1)

                    def front_den(i):
                        for f in range(KC):
                            pe.wait_ge(s_qp, i * KC + f + 1)
                            if f >= 2:
                                wait(pe, s_rd, i * KC + f - 1)
                            pe.matmul(bank[f % 2][:, 0:G], ks_bd[:, f, :], qz[:, f, :], start=True, stop=True).then_inc(s_den, 1)

                    def hidden(b, n, fronts):
                        if n < 2:
                            wait(pe, s_qp, fronts * KC - 1 + n)
                        else:
                            wait(pe, s_ge, b * FC + n - 1)
                        wide = P if n > 0 else 64
                        at = (n - 1) * P if n > 0 else 1024
                        for c in range(KC):
                            m = pe.matmul(bank[2 + n % 2][0:wide, 0:G], w1[:, c, at:at + wide], x2_t[:, c, :],
                                          start=(c == 0), stop=(c == KC - 1))
                        m.then_inc(s_h, 1)

                    def back_places(b):
                        pe.wait_ge(s_oh, b + 1)
                        for j in range(C):
                            for k in range(j + 1):
                                pe.matmul(bank[4][0:R, 64 + j * EB:80 + j * EB], (ones_b if k < j else upto)[0:R, 0:R],
                                          one_hot[0:R, k, :], start=(k == 0), stop=(k == j))
                        for k in range(C):
                            m = pe.matmul(bank[4][0:R, 128:144], ones_b[0:R, 0:R], one_hot[0:R, k, :], start=(k == 0), stop=(k == C - 1))
                        m.then_inc(s_pos, 1)

                    def front_mix(i, back):
                        pe.wait_ge(s_qz, (i + 1) * KC)
                        for j in range(C):
                            wait(pe, s_o, (i - 1) * C - 1 + j if not isinstance(i, int) or i >= 2 else 0) if j < 2 \
                                else wait(pe, s_xp, i * C + j - 1)
                            for f in range(KC):
                                m = pe.matmul(bank[6 + j % 2][0:R, :], qz[:, f, j * R:j * R + R], kvp[:, f, :],
                                              start=(f == 0), stop=(f == KC - 1))
                            m.then_inc(s_mix, 1)

                    def back_gates(b):
                        pe.wait_ge(s_gate, b + 1)
                        wait(pe, s_hm, b * 8)
                        turned = bank[4][0:3 * EB, 0:256].bitcast(BF16)
                        for j in range(C):
                            pe.transpose(bank[5][0:EB + 1, j * R:j * R + R], gates[0:R, j, :], ident[0:R, 0:R])
                        for j in range(C):
                            t = pe.transpose(turned[:, j * P:j * P + R], parts[0:R, j, :], ident_b[0:R, 0:R])
                        t.then_inc(s_gt, 1)

                    def back_mask(b, c):
                        if c == 0:
                            pe.wait_ge(s_gc, b + 1)
                        else:
                            wait(pe, s_hm, b * 8 + c)
                        pe.matmul(bank[5][:, 0:G], spread[:, c, :], parts_t[:, :, :], start=True, stop=True).then_inc(s_mk, 1)

                    def back_out(b, fronts):
                        for j in range(C):
                            wait(pe, s_xp, fronts * C - 1 + j) if j < 2 else wait(pe, s_o, b * C + j - 1)
                            if j == 0:
                                pe.wait_ge(s_hm, (b + 1) * 8)
                            for k in range(FC):
                                rows = P if k < FC - 1 else 81
                                m = pe.matmul(bank[6 + j % 2][0:R, :], gated[0:rows, k, j * R:j * R + R], w2[0:rows, k, :],
                                              start=(k == 0), stop=(k == FC - 1))
                            m.then_inc(s_y, 1)

                    def step(i, par, half, front, back):
                        fronts = i + 1 if front else i
                        if front:
                            front_q(i)
                        if back:
                            back_logits(i - 1, front)
                        if front:
                            front_den(i)
                        if back:
                            hidden(i - 1, 0, fronts)
                            hidden(i - 1, 1, fronts)
                            back_places(i - 1)
                        if front:
                            front_mix(i, back)
                        if back:
                            back_gates(i - 1)
                            for c in range(8):
                                if c < 7:
                                    hidden(i - 1, c + 2, fronts)
                                back_mask(i - 1, c)
                            back_out(i - 1, fronts)
                    pe.wait_ge(s_set, 1)
                    pipeline(pe, step)

                @block.scalar
                def _(act):
                    def front_q(i):
                        for c in range(KC):
                            act.wait_ge(s_nt, i * KC + c + 1)
                            if c == 0:
                                wait(act, s_q, i * KC)
                            act.activation(xn_t[:, c, :], bank[c % 2][:, 0:G], ACT.Copy).then_inc(s_nc, 1)
                        for f in range(KC):
                            act.wait_ge(s_ql, i * KC + f + 1)
                            act.activation(low[:, f % 2, :], low[:, f % 2, :], ACT.Exp).then_inc(s_qe, 1)

                    def back_logits(b):
                        for c in range(KC):
                            act.wait_ge(s_xt, b * KC + c + 1)
                            if c == 0:
                                wait(act, s_h, b * FC)
                            act.activation(x2_t[:, c, :], bank[c % 2][:, 0:G], ACT.Copy).then_inc(s_xc, 1)
                        act.wait_ge(s_sh, b + 1)
                        act.activation(expd[0:R, :, :], shifted[0:R, :, :], ACT.Exp).then_inc(s_le, 1)

                    def gelu(b, n):
                        act.wait_ge(s_h, b * FC + n + 1)
                        if n == 0:
                            wait(act, s_y, b * C)
                            to, wide = gated[0:64, 8, :], 64
                        else:
                            wait(act, s_hm, b * 8 + n - 2)
                            to, wide = hid[:, (n - 1) % 2, :], P
                        k = n - 1 if n > 0 else 8
                        act.activation(to, bank[2 + n % 2][0:wide, 0:G], ACT.Gelu, bias=b1[0:wide, k:k + 1]).then_inc(s_ge, 1)

                    def back_gates(b):
                        act.wait_ge(s_gt, b + 1)
                        wait(act, s_mk, b * 8)
                        turned = bank[4][0:3 * EB, 0:256].bitcast(BF16).rearrange("k (c r) -> k c r", c=C)
                        act.activation(parts_t[:, :, :], turned[:, :, 0:R], ACT.Copy)
                        act.activation(gated[64:64 + EB + 1, 8, :], bank[5][0:EB + 1, 0:G], ACT.Copy).then_inc(s_gc, 1)

                    def front_root(i):
                        act.wait_ge(s_v, i + 1)
                        act.activation(st_std[0:R, :], st_mv[0:R, :, 1], ACT.Sqrt).then_inc(s_r, 1)

                    def step(i, par, half, front, back):
                        if front:
                            front_q(i)
                        if back:
                            back_logits(i - 1)
                            gelu(i - 1, 0)
                            gelu(i - 1, 1)
                            back_gates(i - 1)
                            gelu(i - 1, 2)
                        if front:
                            front_root(i)
                        if back:
                            for n in range(3, FC):
                                gelu(i - 1, n)
                    act.wait_ge(s_set, 1)
                    pipeline(act, step)

                @block.vector
                def _(dve):
                    def normalise_x(ch, i, par, half):
                        dve.wait_ge(s_x[par], 64 * (half + 1))
                        ch.link(dve.tensor_copy(now_stat[0:R, :, :], row_stat[0:R, i, :, :]))
                        wait(dve, s_nt, i * KC)
                        for c in range(C):
                            k = dve.tensor_scalar(xn[0:R, c, :], x_in[par][0:R, c, :], now_stat[0:R, 0, c:c + 1],
                                                  now_stat[0:R, 1, c:c + 1], ALU.subtract, ALU.mult)
                        k.then_inc(s_n, 1)

                    def front_q(i):
                        wait(dve, s_mix, i * C)
                        for f in range(KC):
                            q = bank[2 + f % 2][:, 0:G]
                            dve.wait_ge(s_q, i * KC + f + 1)
                            dve.tensor_scalar(low[:, f % 2, :], q, 0.0, None, ALU.min).then_inc(s_ql, 1)
                            dve.wait_ge(s_qe, i * KC + f + 1)
                            dve.scalar_tensor_tensor(qz[:, f, :], q, 0.0, low[:, f % 2, :], ALU.max, ALU.add).then_inc(s_qp, 1)

                    def back_route(ch, b):
                        logits = bank[4][0:R, 0:C * EB].rearrange("p (a e) -> p a e", e=EXPERTS)
                        wide = [R, C * 2, EXPERTS]
                        dve.wait_ge(s_lg, b + 1)
                        ch.link(dve.tensor_reduce(top_l[0:R, :], logits, AX.X, ALU.max))
                        dve.tensor_tensor(shifted[0:R, :, :], logits, top_l[0:R, :, None].broadcast_to(wide), ALU.subtract).then_inc(s_sh, 1)
                        dve.wait_ge(s_sh, b + 1)
                        ch.link(dve.scalar_tensor_tensor(pick[0:R, :, :], shifted[0:R, :, :], 0.0,
                                                         descend[0:R, None, :].broadcast_to(wide), ALU.is_ge, ALU.mult))
                        ch.link(dve.tensor_reduce(picked[0:R, :], pick[0:R, :, :], AX.X, ALU.max))
                        wait(dve, s_pos, b)
                        dve.tensor_tensor(one_hot[0:R, :, :].rearrange("p c (k e) -> p (c k) e", k=2), pick[0:R, :, :],
                                          picked[0:R, :, None].broadcast_to(wide), ALU.is_equal).then_inc(s_oh, 1)
                        dve.wait_ge(s_le, b + 1)
                        ch.link(dve.tensor_reduce(gate[0:R, :], expd[0:R, :, :], AX.X, ALU.add))
                        ch.link(dve.reciprocal(gate[0:R, :], gate[0:R, :]))

                    def front_den(i):
                        for f in range(KC):
                            dve.wait_ge(s_den, i * KC + f + 1)
                            wait(dve, s_qz, i * KC + f)
                            dve.reciprocal(rden[:, :], bank[f % 2][:, 0:G]).then_inc(s_rd, 1)
                            dve.wait_ge(s_rd, i * KC + f + 1)
                            dve.tensor_tensor(qz[:, f, :], qz[:, f, :], rden[:, :], ALU.mult).then_inc(s_qz, 1)

                    def back_gates(ch, b):
                        dve.wait_ge(s_pos, b + 1)
                        ch.link(dve.tensor_tensor(place[0:R, :, :], bank[4][0:R, 64:128].rearrange("p (c e) -> p c e", c=C),
                                                  carried[0:R, None, :].broadcast_to([R, C, EB]), ALU.add))
                        ch.link(dve.tensor_tensor(carried[0:R, :], carried[0:R, :], bank[4][0:R, 128:144], ALU.add))
                        ch.link(dve.scalar_tensor_tensor(place[0:R, :, :], place[0:R, :, :], float(CAP), one_hot[0:R, :, :],
                                                         ALU.is_le, ALU.mult))
                        wait(dve, s_gt, b)
                        for j in range(C):
                            k = dve.tensor_tensor(gates[0:R, j, 0:EB].rearrange("p (k e) -> p k e", k=2),
                                                  place[0:R, j, :].rearrange("p (k e) -> p k e", k=2),
                                                  gate[0:R, 2 * j:2 * j + 2, None].broadcast_to([R, 2, EXPERTS]), ALU.mult)
                        ch.link(k)
                        ch.link(dve.tensor_copy(parts[0:R, :, 0:EB], gates[0:R, :, 0:EB]))
                        ch.link(dve.tensor_tensor(rest[0:R, :, :], gates[0:R, :, 0:EB], parts[0:R, :, 0:EB], ALU.subtract))
                        ch.link(dve.tensor_copy(parts[0:R, :, EB:2 * EB], rest[0:R, :, :]))
                        ch.link(dve.tensor_tensor(rest[0:R, :, :], rest[0:R, :, :], parts[0:R, :, EB:2 * EB], ALU.subtract))
                        dve.tensor_copy(parts[0:R, :, 2 * EB:3 * EB], rest[0:R, :, :]).then_inc(s_gate, 1)

                    def front_x1(ch, i, par, half):
                        wait(dve, s_st[par], 32 * half)
                        for j in range(C):
                            dve.wait_ge(s_mix, i * C + j + 1)
                            dve.wait_ge(s_base, i * C + j + 1)
                            dve.tensor_tensor(x1[par][0:R, j, :], bank[6 + j % 2][0:R, :], base[par][0:R, j, :], ALU.add).then_inc(s_xp, 1)
                        for j in range(C):
                            dve.wait_ge(s_xp, i * C + j + 1)
                            k = dve.bn_stats(bn[0:R, j, :], x1[par][0:R, j, :])
                        ch.link(k)
                        settle(dve, s_past_dve)
                        for j in range(C):
                            k = dve.bn_aggr(st_mv[0:R, j, :], bn[0:R, j, :])
                        ch.link(k)
                        dve.tensor_scalar(st_mv[0:R, :, 1], st_mv[0:R, :, 1], LN_EPS, None, ALU.add).then_inc(s_v, 1)

                    def front_x2(ch, i, par):
                        dve.wait_ge(s_r, i + 1)
                        inverse_root(ch, dve, st_rstd[0:R, :], st_std[0:R, :], st_mv[0:R, :, 1], st_tmp[0:R, :])
                        wait(dve, s_xt, i * KC)
                        for j in range(C):
                            k = dve.tensor_scalar(x2[0:R, j, :], x1[par][0:R, j, :], st_mv[0:R, j, 0:1], st_rstd[0:R, j:j + 1],
                                                  ALU.subtract, ALU.mult)
                        k.then_inc(s_x2, 1)

                    def back_gated(b, c):
                        if c == 0:
                            wait(dve, s_y, b * C)
                        dve.wait_ge(s_ge, b * FC + c + 2)
                        dve.wait_ge(s_mk, b * 8 + c + 1)
                        dve.tensor_tensor(gated[:, c, :], hid[:, c % 2, :], bank[5][:, 0:G], ALU.mult).then_inc(s_hm, 1)

                    def back_out(b, par):
                        for j in range(C):
                            dve.wait_ge(s_y, b * C + j + 1)
                            dve.tensor_tensor(x1[par][0:R, j, :], bank[6 + j % 2][0:R, :], x1[par][0:R, j, :], ALU.add).then_inc(s_o, 1)

                    def step(i, par, half, front, back):
                        ch = Chain(dve, s_ch, 1 if isinstance(i, int) and i == 0 else 21 * i - 12 if front else 21 * i - 13)
                        if front:
                            front_q(i)
                        if back:
                            back_route(ch, i - 1)
                        if front:
                            front_den(i)
                        if back:
                            back_gates(ch, i - 1)
                        if not isinstance(i, int) or i < NG - 1:
                            normalise_x(ch, i + 1, 1 - par, half + par)
                        if front:
                            front_x1(ch, i, par, half)
                        if back:
                            back_gated(i - 1, 0)
                            back_gated(i - 1, 1)
                        if front:
                            front_x2(ch, i, par)
                        if back:
                            for c in range(2, 8):
                                back_gated(i - 1, c)
                            back_out(i - 1, 1 - par)
                        if not isinstance(i, int) or i == 1:
                            assert ch.n == 21, ch.n
                        if isinstance(i, int) and i == 0:
                            assert ch.n == 8, ch.n
                    dve.wait_ge(s_set, 1)
                    ch = Chain(dve, s_ch)
                    normalise_x(ch, 0, 0, 0)
                    pipeline(dve, step)
        ffn.close()
        mid.close()


_INS = ["x", "src", "dst"] + ["L0_gnn_" + n for n in (
    "norm1_g", "norm1_b", "norm2_g", "norm2_b", "W_conv", "b_conv", "Wq", "Wk", "Wv", "Wo", "proj")] + [
    "L0_mix_" + n for n in ("w_qkv", "proj_mat", "w_proj", "b_proj")] + ["L0_ffn_" + n for n in (
        "Wr_sp", "br_sp", "Wr_fq", "br_fq", "Ws1", "bs1", "Ws2", "bs2", "W1_sp", "b1_sp", "W2_sp", "b2_sp",
        "W1_fq", "b1_fq", "W2_fq", "b2_fq")]


def kernel(**inputs):
    import numpy as _np
    import concourse.bacc as _bacc
    from concourse import mybir as _mybir
    from concourse.bass_utils import run_bass_kernel_spmd as _run

    nc = _bacc.Bacc("TRN2", target_bir_lowering=False, num_devices=1)
    arrays, args = {}, {}
    for name in _INS:
        array = _np.ascontiguousarray(inputs[name])
        arrays[f"in_{name}"] = array
        args[name] = nc.dram_tensor(f"in_{name}", array.shape, _mybir.dt.from_np(array.dtype), kind="ExternalInput").ap()
    result = nc.dram_tensor("out_0", (N, D), F32, kind="ExternalOutput").ap()
    gps_layer_kernel(nc, args, result)
    r = _run(nc, [arrays], core_ids=[0])
    return r.results[0]["out_0"]
```

```python
from contextlib import ExitStack

import concourse.bass as bass
from concourse import mybir

F32 = mybir.dt.float32
F32R = mybir.dt.float32r
BF16 = mybir.dt.bfloat16
I32 = mybir.dt.int32
ALU = mybir.AluOpType
ACT = mybir.ActivationFunctionType
AX = mybir.AxisListType

N, D, E = 10000, 512, 10000
P = 128
R = 125
C = 4
G = R * C
NG = N // G
NT = N // R
KC = D // P
SPRAY = 112
AGG_W = 520
AGG_ROWS = 10240
LN_EPS = 1e-5
BN_EPS = 1e-5
ATT_ROWS, ATT_HEADS, ATT_DH, ATT_M = 64, 8, 64, 256
ATT_KEPS = 1e-6
EXPERTS, FF = 8, 64
CAP = 5120
W1_COLS = 2 * EXPERTS * FF + FF + 2 * EXPERTS
FC = 9


def wait(eng, sem, value):
    if isinstance(value, int) and value <= 0:
        return
    eng.wait_ge(sem, value)


def settle(eng, passed):
    eng.sem_inc(passed)


class Chain:

    def __init__(self, eng, sem, base=0):
        self.eng, self.sem, self.base, self.n = eng, sem, base, 0

    def link(self, ins):
        ins.then_inc(self.sem, 1)
        self.n += 1
        self.eng.wait_ge(self.sem, self.base + self.n)


def inverse_root(ch, dve, out, root, var, tmp):
    ch.link(dve.reciprocal(out, root))
    ch.link(dve.tensor_tensor(tmp, out, out, ALU.mult))
    ch.link(dve.tensor_tensor(tmp, tmp, var, ALU.mult))
    ch.link(dve.tensor_scalar(tmp, tmp, -0.5, 1.5, ALU.mult, ALU.add))
    ch.link(dve.tensor_tensor(out, out, tmp, ALU.mult))


def dma_rows(eng, out, in_, sem):
    eng.dma_start(out[0:SPRAY], in_[0:SPRAY]).then_inc(sem, 16)
    eng.dma_start(out[SPRAY:R], in_[SPRAY:R]).then_inc(sem, 16)


def split_product(pe, out, weights, moving, first, last):
    pe.matmul(out, weights[0], moving[1], start=first, stop=False)
    pe.matmul(out, weights[1], moving[0], start=False, stop=False)
    return pe.matmul(out, weights[0], moving[0], start=False, stop=last)


def groups(eng, step):
    step(0, 0, 0)
    step(1, 1, 0)
    with eng.Fori(1, NG // 2 - 1) as r:
        step(r * 2, 0, r)
        step(r * 2 + 1, 1, r)
    step(NG - 2, 0, NG // 2 - 1)
    step(NG - 1, 1, NG // 2 - 1)


def gps_layer_kernel(nc, a, out):
    x_g = a["x"].rearrange("(s c p) d -> s p c d", c=C, p=R)
    out_g = out.rearrange("(s c p) d -> s p c d", c=C, p=R)
    agg = nc.dram_tensor("agg", [AGG_ROWS, AGG_W], F32, kind="Internal").ap()
    agg_g = agg[0:N, :].rearrange("(s c p) d -> s p c d", c=C, p=R)
    u_dram = nc.dram_tensor("u_dram", [N, D], F32, kind="Internal").ap()
    u_g = u_dram.rearrange("(s c p) d -> s p c d", c=C, p=R)

    top = ExitStack()
    with top:
        def sem(name):
            return top.enter_context(nc.semaphore(name))

        def sb(stack, name, shape, dt=F32):
            return stack.enter_context(nc.sbuf_tensor(name, shape, dt))

        bank = [top.enter_context(nc.psum_tensor(f"bank{i}", [P, 512], F32)) for i in range(8)]

        ident = sb(top, "ident", [P, P])
        ones = sb(top, "ones", [P, P])
        row_stat = sb(top, "row_stat", [P, NG, 2, C])
        att_delta = sb(top, "att_delta", [P, D])
        phi_q = sb(top, "phi_q", [P, KC, D])
        w_proj = sb(top, "w_proj", [P, KC, D])
        kvp = sb(top, "kvp", [P, KC, D])
        ks_bd = sb(top, "ks_bd", [P, KC, P])
        s_const = sem("s_const")
        s_zero = sem("s_zero")
        s_past_dve = sem("s_past_dve")
        s_past_pool = sem("s_past_pool")
        s_past_sp = sem("s_past_sp")

        mid = ExitStack()
        w_v = sb(mid, "w_v", [P, KC, D])
        w_conv = sb(mid, "w_conv", [P, KC, D])
        bn_part = sb(mid, "bn_part", [P, KC, NG * 6])
        ks_acc = sb(mid, "ks_acc", [P, D])
        block_mask = sb(mid, "block_mask", [P, P])

        first = ExitStack()
        phi_k = sb(first, "phi_k", [P, KC, D])
        src_i = sb(first, "src_i", [P, NT], I32)
        dst_f = sb(first, "dst_f", [P, NT])
        spare = sb(first, "spare", [P, NT])
        dst_rows = sb(first, "dst_rows", [P, E], I32)
        before = sb(first, "before", [P, R])
        s_dst = sem("s_dst")

        with ExitStack() as st:
            w_qk = sb(st, "w_qk", [P, KC, 2 * D])
            proj_bd = sb(st, "proj_bd", [P, KC, P])
            w_turned = sb(st, "w_turned", [P, D])
            idx_in = sb(st, "idx_in", [NT, 2, R], I32)
            idx_f = sb(st, "idx_f", [NT, 2, R])
            zeros = sb(st, "zeros", [P, 5, AGG_W])
            node_no = sb(st, "node_no", [P, 1])
            g_w = [sb(st, f"g_w{n}", [P, KC, D]) for n in "qkvo"]
            proj2 = sb(st, "proj2", [P, 2, P])
            x64 = sb(st, "x64", [ATT_ROWS, D])
            x64_t = sb(st, "x64_t", [P, KC, ATT_ROWS])
            proj_t = sb(st, "proj_t", [P, ATT_M])
            bn6 = sb(st, "bn6", [ATT_ROWS, 6])
            mv = sb(st, "mv", [ATT_ROWS, 2])
            small = sb(st, "small", [ATT_ROWS, 4])
            qk = sb(st, "qk", [ATT_ROWS, 2, D])
            diag = sb(st, "diag", [ATT_ROWS, 2, ATT_HEADS])
            v_aug = sb(st, "v_aug", [ATT_ROWS, ATT_HEADS, ATT_DH + 1])
            qk_t = sb(st, "qk_t", [P, 2, KC, ATT_ROWS])
            feat = sb(st, "feat", [ATT_ROWS, 2, ATT_HEADS, ATT_M])
            sq = feat[:, 0, 0:4, :].rearrange("p a b -> p (a b)").rearrange("p (w d) -> p w d", w=2)
            top_u = sb(st, "top_u", [ATT_ROWS, 2, ATT_HEADS])
            top_k = sb(st, "top_k", [ATT_HEADS, 1])
            top_d = sb(st, "top_d", [ATT_HEADS, ATT_HEADS])
            qf_t = sb(st, "qf_t", [P, 2 * ATT_HEADS, ATT_ROWS])
            kv_aug = sb(st, "kv_aug", [P, 2 * ATT_HEADS, ATT_DH + 1])
            z_att = sb(st, "z_att", [ATT_ROWS, ATT_HEADS])
            att = sb(st, "att", [ATT_ROWS, D])
            att_t = sb(st, "att_t", [P, KC, ATT_ROWS])
            att_out = sb(st, "att_out", [ATT_ROWS, D])
            delta_sel = sb(st, "delta_sel", [ATT_ROWS, P])

            s_pool = sem("s_pool")
            s_wqk = sem("s_wqk")
            s_bd = sem("s_bd")
            s_wv = sem("s_wv")
            s_idx = sem("s_idx")
            s_att_in = sem("s_att_in")
            s_zeroed = sem("s_zeroed")
            s_turn = sem("s_turn")
            s_turned = sem("s_turned")
            s_fused = sem("s_fused")
            s_fcopy = sem("s_fcopy")
            s_idx_f = sem("s_idx_f")
            s_idx_t = sem("s_idx_t")
            s_idx_c = sem("s_idx_c")
            s_att = sem("s_att")
            s_chain = sem("s_chain")
            STAGES = ["var", "std", "norm", "turn", "turned", "qkv", "scaled", "turn2", "turned2", "u",
                      "top", "turn_top", "top_d", "top_b", "arg", "exp", "phi", "kv", "kv_copy", "att",
                      "att_z", "turn3", "turned3", "wo", "wo_copy", "delta", "done"]
            after = {name: i + 1 for i, name in enumerate(STAGES)}

            with nc.Block() as block:
                @block.sync
                def _(sp):
                    sp.dma_start(x64[:, :], a["x"][0:ATT_ROWS, :]).then_inc(s_att_in, 16)
                    for w, name in zip(g_w, ("Wq", "Wk", "Wv", "Wo")):
                        sp.dma_start(w[:, :, :], a["L0_gnn_" + name].rearrange("(c p) n -> p c n", p=P)).then_inc(s_att_in, 16)
                    for twice in range(2):
                        sp.dma_start(proj2[:, :, twice * 64:twice * 64 + 64],
                                     a["L0_gnn_proj"].rearrange("(c p) d -> p c d", p=P)).then_inc(s_att_in, 16)
                    qkv = a["L0_mix_w_qkv"].rearrange("(c p) n -> p c n", p=P)
                    sp.dma_start(w_qk[:, :, :], qkv[:, :, 0:2 * D]).then_inc(s_wqk, 16)
                    sp.dma_start(idx_in[:, 0, :], a["src"].rearrange("(t p) -> t p", p=R)).then_inc(s_idx, 16)
                    sp.dma_start(idx_in[:, 1, :], a["dst"].rearrange("(t p) -> t p", p=R)).then_inc(s_idx, 16)
                    every = a["dst"].rearrange("(a e) -> a e", a=1).broadcast_to([P, E])
                    sp.dma_start(dst_rows[:, :], every).then_inc(s_dst, 16)
                    sp.dma_start(w_v[:, :, :], qkv[:, :, 2 * D:3 * D]).then_inc(s_wv, 16)
                    sp.dma_start(w_proj[:, :, :], a["L0_mix_w_proj"].rearrange("(c p) n -> p c n", p=P)).then_inc(s_wv, 16)
                    sp.dma_start(w_conv[:, :, :], a["L0_gnn_W_conv"].rearrange("(c p) n -> p c n", p=P)).then_inc(s_wv, 16)
                    sp.wait_ge(s_zero, 1)
                    agg_z = agg.rearrange("(p k r) w -> k p r w", p=P, r=5)
                    for k in range(AGG_ROWS // (P * 5)):
                        sp.dma_start(agg_z[k], zeros[:, :, :]).then_inc(s_zeroed, 16)
                    sp.wait_ge(s_zeroed, 16 * (AGG_ROWS // (P * 5)))
                    sp.wait_ge(s_dst, 16)
                    sp.wait_ge(s_wv, 48)

                @block.gpsimd
                def _(pool):
                    ch = Chain(pool, s_pool)
                    ch.link(pool.memset(proj_bd[:, :, :], 0.0))
                    for h in range(8):
                        b = 64 * (h % 2)
                        pool.dma_start(proj_bd[b:b + 64, h // 2, b:b + 64],
                                       a["L0_mix_proj_mat"][h]).then_inc(s_bd, 16)
                    pool.memset(zeros[:, :, :], 0.0).then_inc(s_zero, 1)
                    pool.memset(ones[:, :], 1.0)
                    ch.link(pool.memset(ident[:, :], 0.0))
                    ch.link(pool.affine_select(out=ident[:, :], in_=ident[:, :], compare_op=ALU.not_equal, fill=1.0,
                                               base=0, pattern=[[-1, P]], channel_multiplier=1))
                    ch.link(pool.affine_select(out=before[0:R, :], in_=ones[0:R, 0:R], compare_op=ALU.is_gt, fill=0.0,
                                               base=0, pattern=[[-1, R]], channel_multiplier=1))
                    ch.link(pool.memset(block_mask[:, :], 0.0))
                    pool.memset(block_mask[0:64, 0:64], 1.0)
                    ch.link(pool.memset(block_mask[64:P, 64:P], 1.0))
                    ch.link(pool.iota(node_no[:, :], pattern=[[0, 1]], base=N, channel_multiplier=1,
                                      allow_small_or_imprecise_dtypes=True))
                    ch.link(pool.tensor_copy(delta_sel[:, :], ident[0:ATT_ROWS, :]))
                    ch.link(pool.affine_select(out=delta_sel[:, 0:63], in_=delta_sel[:, 0:63],
                                               compare_op=ALU.not_equal, fill=-1.0, base=-63,
                                               pattern=[[0, 63]], channel_multiplier=1))
                    ch.link(pool.memset(delta_sel[:, 63:64], 0.0))
                    pool.memset(v_aug[:, :, ATT_DH:ATT_DH + 1], 1.0)
                    pool.memset(ks_acc[:, :], 0.0).then_inc(s_const, 1)

                @block.tensor
                def _(pe):
                    pe.wait_ge(s_const, 1)
                    pe.wait_ge(s_att, after["norm"])
                    pe.wait_ge(s_att_in, 16 * 7)
                    for c in range(KC):
                        pe.transpose(bank[0][:, c * 64:c * 64 + 64], x64[:, c * P:c * P + P], ident[0:64, 0:64])
                    for m in range(2):
                        t = pe.transpose(bank[1][:, m * P:m * P + P], proj2[:, m, :], ident[:, :])
                    t.then_inc(s_att, 1)
                    pe.wait_ge(s_att, after["turned"])
                    for w in range(3):
                        for c in range(KC):
                            m = pe.matmul(bank[2 + w][0:64, :], x64_t[:, c, :], g_w[w][:, c, :],
                                          start=(c == 0), stop=(c == KC - 1))
                    m.then_inc(s_att, 1)
                    pe.wait_ge(s_att, after["scaled"])
                    for w in range(2):
                        for c in range(KC):
                            t = pe.transpose(bank[w][:, c * 64:c * 64 + 64], qk[:, w, c * P:c * P + P], ident[0:64, 0:64])
                    t.then_inc(s_att, 1)
                    pe.wait_ge(s_att, after["turned2"])
                    for w in range(2):
                        for h in range(ATT_HEADS):
                            b = 64 * (h % 2)
                            g, at = 2 * (h % 2) + h // 4, h // 2 % 2
                            m = pe.matmul(bank[(2 + 4 * w + g) % 8][0:64, at * ATT_M:(at + 1) * ATT_M],
                                          qk_t[b:b + 64, w, h // 2, :], proj_t[b:b + 64, :], start=True, stop=True)
                    m.then_inc(s_att, 1)
                    pe.wait_ge(s_att, after["top"])
                    pe.transpose(bank[2][0:8, 0:64], top_u[:, 1, :], ident[0:64, 0:64]).then_inc(s_att, 1)
                    pe.wait_ge(s_att, after["top_d"])
                    pe.matmul(bank[2][0:64, 64:72], ones[0:8, 0:64], top_d[:, :], start=True, stop=True).then_inc(s_att, 1)
                    pe.wait_ge(s_att, after["phi"])
                    for hm in range(2 * ATT_HEADS):
                        h, m = hm // 2, hm % 2
                        pe.transpose(bank[2 + hm // 8][:, (hm % 8) * 64:(hm % 8) * 64 + 64],
                                     feat[:, 0, h, m * P:m * P + P], ident[0:64, 0:64])
                    for hm in range(2 * ATT_HEADS):
                        h, m = hm // 2, hm % 2
                        mm = pe.matmul(bank[4 + hm // 4][:, (hm % 4) * 65:(hm % 4) * 65 + 65],
                                       feat[:, 1, h, m * P:m * P + P], v_aug[:, h, :], start=True, stop=True)
                    mm.then_inc(s_att, 1)
                    pe.wait_ge(s_att, after["kv_copy"])
                    for h in range(ATT_HEADS):
                        for m in range(2):
                            mm = pe.matmul(bank[h // 4][0:64, (h % 4) * 65:(h % 4) * 65 + 65],
                                           qf_t[:, 2 * h + m, :], kv_aug[:, 2 * h + m, :], start=(m == 0), stop=(m == 1))
                    mm.then_inc(s_att, 1)
                    pe.wait_ge(s_att, after["att_z"])
                    for c in range(KC):
                        t = pe.transpose(bank[2][:, c * 64:c * 64 + 64], att[:, c * P:c * P + P], ident[0:64, 0:64])
                    t.then_inc(s_att, 1)
                    pe.wait_ge(s_att, after["turned3"])
                    for c in range(KC):
                        m = pe.matmul(bank[3][0:64, :], att_t[:, c, :], g_w[3][:, c, :], start=(c == 0), stop=(c == KC - 1))
                    m.then_inc(s_att, 1)
                    pe.wait_ge(s_att, after["wo_copy"])
                    pe.matmul(bank[4][:, :], delta_sel[:, :], att_out[:, :], start=True, stop=True).then_inc(s_att, 1)
                    pe.wait_ge(s_wqk, 16)
                    pe.wait_ge(s_bd, 16 * 8)
                    for n in range(8):
                        wait(pe, s_turned, n)
                        for c in range(KC):
                            t = pe.transpose(bank[5][:, c * P:c * P + P], w_qk[:, c, n * P:n * P + P], ident[:, :])
                        t.then_inc(s_turn, 1)
                        pe.wait_ge(s_turned, n + 1)
                        wait(pe, s_fcopy, n)
                        for c in range(KC):
                            m = pe.matmul(bank[6][:, c * P:c * P + P], w_turned[:, c * P:c * P + P],
                                          proj_bd[:, n % 4, :], start=True, stop=True)
                        m.then_inc(s_fused, 1)
                    pe.wait_ge(s_idx_f, 1)
                    for k in range(2):
                        t = pe.transpose(bank[7][0:R, k * P:k * P + NT], idx_f[:, k, :], ident[0:NT, 0:NT])
                    t.then_inc(s_idx_t, 1)

                @block.scalar
                def _(act):
                    act.wait_ge(s_att, after["var"])
                    act.activation(small[:, 0:1], mv[:, 1:2], ACT.Sqrt).then_inc(s_att, 1)
                    act.wait_ge(s_att, after["turn"])
                    act.activation(x64_t[:, :, :].rearrange("p c n -> p (c n)"), bank[0][:, 0:256], ACT.Copy)
                    act.activation(proj_t[:, :], bank[1][:, 0:256], ACT.Copy).then_inc(s_att, 1)
                    act.wait_ge(s_att, after["turn2"])
                    for w in range(2):
                        i = act.activation(qk_t[:, w, :, :].rearrange("p c n -> p (c n)"), bank[w][:, 0:256], ACT.Copy)
                    i.then_inc(s_att, 1)
                    act.wait_ge(s_att, after["arg"])
                    act.activation(feat[:, :, :, :].rearrange("p a h m -> p (a h m)"),
                                   feat[:, :, :, :].rearrange("p a h m -> p (a h m)"), ACT.Exp).then_inc(s_att, 1)
                    act.wait_ge(s_att, after["kv"])
                    for k in range(2):
                        act.activation(qf_t[:, 8 * k:8 * k + 8, :].rearrange("p a n -> p (a n)"), bank[2 + k][:, :], ACT.Copy)
                    for k in range(4):
                        i = act.activation(kv_aug[:, 4 * k:4 * k + 4, :].rearrange("p a n -> p (a n)"),
                                           bank[4 + k][:, 0:260], ACT.Copy)
                    i.then_inc(s_att, 1)
                    act.wait_ge(s_att, after["turn3"])
                    act.activation(att_t[:, :, :].rearrange("p c n -> p (c n)"), bank[2][:, 0:256], ACT.Copy).then_inc(s_att, 1)
                    act.wait_ge(s_att, after["wo"])
                    act.activation(att_out[:, :], bank[3][0:64, :], ACT.Copy).then_inc(s_att, 1)
                    act.wait_ge(s_att, after["delta"])
                    act.activation(att_delta[:, :], bank[4][:, :], ACT.Copy).then_inc(s_att, 1)
                    for n in range(8):
                        act.wait_ge(s_turn, n + 1)
                        wait(act, s_fused, n)
                        act.activation(w_turned[:, :], bank[5][:, :], ACT.Copy).then_inc(s_turned, 1)

                @block.vector
                def _(dve):
                    ch = Chain(dve, s_chain)
                    dve.wait_ge(s_att_in, 16 * 7)
                    ch.link(dve.bn_stats(bn6[:, :], x64[:, :]))
                    ch.link(dve.bn_aggr(mv[:, :], bn6[:, :]))
                    dve.tensor_scalar_add(mv[:, 1:2], mv[:, 1:2], LN_EPS).then_inc(s_att, 1)
                    dve.wait_ge(s_att, after["std"])
                    inverse_root(ch, dve, small[:, 1:2], small[:, 0:1], mv[:, 1:2], small[:, 2:3])
                    dve.tensor_scalar(x64[:, :], x64[:, :], mv[:, 0:1], small[:, 1:2], ALU.subtract, ALU.mult).then_inc(s_att, 1)
                    dve.wait_ge(s_const, 1)
                    dve.wait_ge(s_att, after["qkv"])
                    for w in range(2):
                        ch.link(dve.tensor_scalar(qk[:, w, :], bank[2 + w][0:64, :], ATT_DH ** -0.25, None, ALU.mult))
                    dve.tensor_copy(v_aug[:, :, 0:ATT_DH],
                                    bank[4][0:64, :].rearrange("p (h d) -> p h d", h=ATT_HEADS)).then_inc(s_att, 1)
                    for w in range(2):
                        ch.link(dve.tensor_tensor(sq[:, w, :], qk[:, w, :], qk[:, w, :], ALU.mult))
                    ch.link(dve.tensor_reduce(diag[:, :, :], sq[:, :, :].rearrange("p a (h d) -> p a h d", h=ATT_HEADS), AX.X, ALU.add))
                    ch.link(dve.tensor_scalar(diag[:, :, :], diag[:, :, :], 0.5, None, ALU.mult))
                    dve.wait_ge(s_att, after["u"])
                    for w in range(2):
                        for g in range(4):
                            u = bank[(2 + 4 * w + g) % 8][0:64, :].rearrange("p (h m) -> p h m", h=2)
                            h = 4 * (g % 2) + g // 2
                            i = dve.tensor_reduce(top_u[:, w, h:h + 3:2], u, AX.X, ALU.max)
                    ch.link(i)
                    for w in range(2):
                        for g in range(4):
                            u = bank[(2 + 4 * w + g) % 8][0:64, :].rearrange("p (h m) -> p h m", h=2)
                            h = 4 * (g % 2) + g // 2
                            i = dve.tensor_tensor(feat[:, w, h:h + 3:2, :], u,
                                                  diag[:, w, h:h + 3:2, None].broadcast_to([ATT_ROWS, 2, ATT_M]), ALU.subtract)
                    i.then_inc(s_att, 1)
                    dve.wait_ge(s_att, after["turn_top"])
                    ch.link(dve.tensor_reduce(top_k[:, :], bank[2][0:8, 0:64], AX.X, ALU.max))
                    dve.tensor_scalar(top_d[:, :], ident[0:8, 0:8], top_k[:, 0:1], None, ALU.mult).then_inc(s_att, 1)
                    dve.wait_ge(s_att, after["top_b"])
                    ch.link(dve.tensor_copy(top_u[:, 1, :], bank[2][0:64, 64:72]))
                    for w in range(2):
                        i = dve.tensor_tensor(feat[:, w, :, :], feat[:, w, :, :],
                                              top_u[:, w, :, None].broadcast_to([ATT_ROWS, ATT_HEADS, ATT_M]), ALU.subtract)
                    i.then_inc(s_att, 1)
                    dve.wait_ge(s_att, after["exp"])
                    dve.tensor_scalar(feat[:, :, :, :].rearrange("p a h m -> p (a h m)"),
                                      feat[:, :, :, :].rearrange("p a h m -> p (a h m)"),
                                      ATT_M ** -0.5, ATT_KEPS, ALU.mult, ALU.add).then_inc(s_att, 1)
                    dve.wait_ge(s_att, after["att"])
                    for k in range(2):
                        num = bank[k][0:64, 0:260].rearrange("p (h d) -> p h d", h=4)
                        ch.link(dve.tensor_scalar(z_att[:, 4 * k:4 * k + 4, None], num[:, :, 64:65], ATT_KEPS, None, ALU.add))
                    ch.link(dve.reciprocal(z_att[:, :], z_att[:, :]))
                    for k in range(2):
                        num = bank[k][0:64, 0:260].rearrange("p (h d) -> p h d", h=4)
                        i = dve.tensor_tensor(att[:, 256 * k:256 * k + 256].rearrange("p (h d) -> p h d", h=4),
                                              num[:, :, 0:64], z_att[:, 4 * k:4 * k + 4, None].broadcast_to([ATT_ROWS, 4, 64]), ALU.mult)
                    i.then_inc(s_att, 1)
                    for n in range(8):
                        dve.wait_ge(s_fused, n + 1)
                        to = (phi_q, phi_k)[n // 4][:, :, (n % 4) * P:(n % 4) * P + P]
                        dve.tensor_copy(to, bank[6][:, :].rearrange("p (c f) -> p c f", c=KC)).then_inc(s_fcopy, 1)
                    dve.wait_ge(s_idx, 32)
                    dve.tensor_copy(idx_f[:, :, :], idx_in[:, :, :]).then_inc(s_idx_f, 1)
                    dve.wait_ge(s_idx_t, 1)
                    ch.link(dve.tensor_copy(src_i[0:R, :], bank[7][0:R, 0:NT]))
                    ch.link(dve.tensor_copy(dst_f[0:R, :], bank[7][0:R, P:P + NT]))
                    ch.link(dve.tensor_scalar(spare[0:R, :], dst_f[0:R, :], -1.0, node_no[0:R, 0:1], ALU.mult, ALU.add))
        with ExitStack() as st:
            x_in = [sb(st, f"x_in{i}", [P, C, D]) for i in range(2)]
            xn = [sb(st, f"xn{i}", [P, C, D]) for i in range(2)]
            xn_t = sb(st, "xn_t", [P, KC, G])
            gat = [sb(st, f"gat{i}", [P, C, D]) for i in range(2)]
            src_now = [sb(st, f"src_now{i}", [P, C], I32) for i in range(2)]
            dst_now = [sb(st, f"dst_now{i}", [P, C], I32) for i in range(2)]
            same = [sb(st, f"same{i}", [P, C, R]) for i in range(2)]
            count = [sb(st, f"count{i}", [P, C]) for i in range(2)]
            repeat = sb(st, "repeat", [P, C])
            scratch = sb(st, "scratch", [P, R])
            sums = sb(st, "sums", [P, C, AGG_W])
            low = sb(st, "low", [P, 2, D])
            ph = sb(st, "ph", [P, 2, D])
            bn = sb(st, "bn", [P, 2, C, 6])
            st_mv = sb(st, "st_mv", [P, 2, C, 2])
            st_std = sb(st, "st_std", [P, 2, C])
            st_tmp = sb(st, "st_tmp", [P, 2, C])
            st_rstd = sb(st, "st_rstd", [P, 2, C])

            s_x = [sem(f"s_x{i}") for i in range(2)]
            s_gat = [sem(f"s_gat{i}") for i in range(2)]
            s_src = sem("s_src")
            s_var = sem("s_var")
            s_std = sem("s_std")
            s_xn = sem("s_xn")
            s_gn = sem("s_gn")
            s_t = sem("s_t")
            s_tc = sem("s_tc")
            s_k = sem("s_k")
            s_low = sem("s_low")
            s_exp = sem("s_exp")
            s_ph = sem("s_ph")
            s_g = sem("s_g")
            s_acc = sem("s_acc")
            s_e = sem("s_e")
            s_ec = sem("s_ec")
            s_scat = sem("s_scat")
            s_col = sem("s_col")
            s_ch = sem("s_ch1")
            CHAIN = 30

            with nc.Block() as block:
                @block.sync
                def _(sp):
                    def load(s, par, half):
                        wait(sp, s_xn, (s - 1) * C if not isinstance(s, int) or s >= 2 else 0)
                        dma_rows(sp, x_in[par][0:R], x_g[s], s_x[par])
                    groups(sp, load)

                @block.gpsimd
                def _(pool):
                    pool.memset(sums[:, :, D + 1:AGG_W], 0.0).then_inc(s_ch, 1)

                    def gather(s, par):
                        pool.wait_ge(s_src, s + 1)
                        wait(pool, s_e, (s - 1) * C if not isinstance(s, int) or s >= 2 else 0)
                        settle(pool, s_past_pool)
                        for c in range(C):
                            pool.indirect_dma_start(
                                out=gat[par][0:R, c, :], out_offset=None, in_=a["x"],
                                in_offset=bass.IndirectOffsetOnAxis(ap=src_now[par][0:R, c:c + 1], axis=0),
                            ).then_inc(s_gat[par], 16)

                    def scatter(s, par):
                        for c in range(C):
                            pool.wait_ge(s_ec, s * C + c + 1)
                            wait(pool, s_scat, (s * C + c) * 16)
                            settle(pool, s_past_pool)
                            pool.indirect_dma_start(
                                out=agg, in_=sums[0:R, c, :], in_offset=None, compute_op=ALU.add,
                                out_offset=bass.IndirectOffsetOnAxis(ap=dst_now[par][0:R, c:c + 1], axis=0),
                            ).then_inc(s_scat, 16)

                    def step(s, par, half):
                        gather(s, par)
                        if not isinstance(s, int) or s >= 1:
                            scatter(s - 1, 1 - par)
                    groups(pool, step)
                    scatter(NG - 1, (NG - 1) % 2)
                    pool.wait_ge(s_scat, 16 * NT)

                @block.tensor
                def _(pe):
                    def turn(s, par):
                        for c in range(C):
                            if c == 0:
                                pe.wait_ge(s_xn, (s + 1) * C)
                            n = s * KC + c
                            wait(pe, s_tc, n - 1)
                            if c == 1:
                                wait(pe, s_ec, (s - 1) * C)
                            for j in range(C):
                                t = pe.transpose(bank[4 + c % 2][:, j * R:j * R + R],
                                                 xn[par][0:R, j, c * P:c * P + P], ident[0:R, 0:R])
                            t.then_inc(s_t, 1)

                    def keys(s, j):
                        if j == 0:
                            pe.wait_ge(s_tc, (s + 1) * KC)
                        wait(pe, s_ph, s * C + j - 1)
                        for c in range(KC):
                            m = pe.matmul(bank[6 + j % 2][0:R, :], xn_t[:, c, j * R:j * R + R], phi_k[:, c, :],
                                          start=(c == 0), stop=(c == KC - 1))
                        m.then_inc(s_k, 1)

                    def edges(s, par, j):
                        if j == 0:
                            pe.wait_ge(s_gn, s + 1)
                        wait(pe, s_ec, s * C + j)
                        pe.matmul(bank[5][0:R, :], same[par][0:R, j, :], gat[par][0:R, j, :],
                                  start=True, stop=True).then_inc(s_e, 1)

                    def products(s, par, j):
                        pe.wait_ge(s_ph, s * C + j + 1)
                        for f in range(KC):
                            m = pe.matmul(bank[f][:, :], ph[0:R, j % 2, f * P:f * P + P], xn[par][0:R, j, :],
                                          start=(isinstance(s, int) and s == 0 and j == 0),
                                          stop=(isinstance(s, int) and s == NG - 1 and j == C - 1))
                        m.then_inc(s_g, 1)

                    def step(s, par, half):
                        for j in range(C):
                            keys(s, j)
                            if not isinstance(s, int) or s >= 1:
                                edges(s - 1, 1 - par, j)
                            if j >= 1:
                                products(s, par, j - 1)
                        products(s, par, C - 1)
                        if not isinstance(s, int) or s < NG - 1:
                            turn(s + 1, 1 - par)
                    turn(0, 0)
                    groups(pe, step)
                    for j in range(C):
                        edges(NG - 1, (NG - 1) % 2, j)

                @block.scalar
                def _(act):
                    def root_x(s):
                        act.wait_ge(s_var, 2 * s + 2 if not isinstance(s, int) or s >= 0 else 1)
                        act.activation(st_std[0:R, 0, :], st_mv[0:R, 0, :, 1], ACT.Sqrt).then_inc(s_std, 1)

                    def root_g(s):
                        act.wait_ge(s_var, 2 * s + 3 if not isinstance(s, int) or s < NG - 1 else 2 * NG)
                        act.activation(st_std[0:R, 1, :], st_mv[0:R, 1, :, 1], ACT.Sqrt).then_inc(s_std, 1)

                    def exp(s, j):
                        act.wait_ge(s_low, s * C + j + 1)
                        act.activation(low[0:R, j % 2, :], low[0:R, j % 2, :], ACT.Exp).then_inc(s_exp, 1)

                    def copy_sums(s, par, j):
                        act.wait_ge(s_e, s * C + j + 1)
                        wait(act, s_scat, 16 * (s * C + j - C + 1))
                        act.activation(sums[0:R, j, D:D + 1], count[par][0:R, j:j + 1], ACT.Copy)
                        act.activation(sums[0:R, j, 0:D], bank[5][0:R, :], ACT.Copy).then_inc(s_ec, 1)

                    def copy_turned(s):
                        for c in range(KC):
                            act.wait_ge(s_t, s * KC + c + 1)
                            if c == 0:
                                wait(act, s_col, s)
                            act.activation(xn_t[:, c, :], bank[4 + c % 2][:, 0:G], ACT.Copy).then_inc(s_tc, 1)

                    act.wait_ge(s_ch, 1)
                    root_x(-1)
                    copy_turned(0)

                    def step(s, par, half):
                        for j in range(C):
                            exp(s, j)
                            if not isinstance(s, int) or s >= 1:
                                copy_sums(s - 1, 1 - par, j)
                            if j == 0 and (not isinstance(s, int) or s < NG - 1):
                                root_x(s)
                            if j == 2:
                                root_g(s)
                        if not isinstance(s, int) or s < NG - 1:
                            copy_turned(s + 1)

                    groups(act, step)
                    for j in range(C):
                        copy_sums(NG - 1, (NG - 1) % 2, j)

                @block.vector
                def _(dve):
                    def variances(ch, s, rows, k):
                        for c in range(C):
                            i = dve.bn_stats(bn[0:R, k, c, :], rows[0:R, c, :])
                        ch.link(i)
                        settle(dve, s_past_dve)
                        for c in range(C):
                            i = dve.bn_aggr(st_mv[0:R, k, c, :], bn[0:R, k, c, :])
                        ch.link(i)
                        dve.tensor_scalar(st_mv[0:R, k, :, 1], st_mv[0:R, k, :, 1], LN_EPS, None, ALU.add).then_inc(s_var, 1)

                    def normalise(ch, rows, out_rows, k, last):
                        inverse_root(ch, dve, st_rstd[0:R, k, :], st_std[0:R, k, :], st_mv[0:R, k, :, 1], st_tmp[0:R, k, :])
                        for c in range(C):
                            i = dve.tensor_scalar(out_rows[0:R, c, :], rows[0:R, c, :], st_mv[0:R, k, c, 0:1],
                                                  st_rstd[0:R, k, c:c + 1], ALU.subtract, ALU.mult)
                            if last is not None:
                                i.then_inc(last, 1)
                        return i

                    def x_variances(ch, s, par, half):
                        dve.wait_ge(s_x[par], 32 * (half + 1))
                        variances(ch, s, x_in[par], 0)

                    def x_normalise(ch, s, par):
                        dve.wait_ge(s_std, 2 * s if not isinstance(s, int) or s > 0 else 1)
                        wait(dve, s_g, (s - 1) * C if not isinstance(s, int) or s >= 2 else 0)
                        normalise(ch, x_in[par], xn[par], 0, s_xn)
                        ch.link(dve.tensor_copy(row_stat[0:R, s, 0, :], st_mv[0:R, 0, :, 0]))
                        ch.link(dve.tensor_copy(row_stat[0:R, s, 1, :], st_rstd[0:R, 0, :]))

                    def sources(s, par, half):
                        wait(dve, s_gat[par], 64 * half)
                        dve.tensor_copy(src_now[par][0:R, :], src_i[0:R, bass.ds(s * C, C)]).then_inc(s_src, 1)

                    def phi(ch, s, j):
                        dve.wait_ge(s_k, s * C + j + 1)
                        dve.tensor_scalar(low[0:R, j % 2, :], bank[6 + j % 2][0:R, :], 0.0, None, ALU.min).then_inc(s_low, 1)
                        dve.wait_ge(s_exp, s * C + j + 1)
                        wait(dve, s_g, s * C + j - 1)
                        dve.scalar_tensor_tensor(ph[0:R, j % 2, :], bank[6 + j % 2][0:R, :], 0.0, low[0:R, j % 2, :],
                                                 ALU.max, ALU.add).then_inc(s_ph, 1)
                        dve.wait_ge(s_ph, s * C + j + 1)
                        ch.link(dve.tensor_tensor(ks_acc[0:R, :], ks_acc[0:R, :], ph[0:R, j % 2, :], ALU.add))

                    def repeats(ch, s, par):
                        wait(dve, s_e, (s - 1) * C if not isinstance(s, int) or s >= 2 else 0)
                        wait(dve, s_scat, 16 * (s - 1) * C if not isinstance(s, int) or s >= 2 else 0)
                        for c in range(C):
                            dst_c = dst_f[0:R, bass.ds(s * C + c, 1)]
                            ch.link(dve.tensor_scalar(same[par][0:R, c, :], dst_rows[0:R, bass.ds(s * G + c * R, R)], dst_c, None,
                                                      ALU.is_equal, ALU.add, accum_out=count[par][0:R, c:c + 1]))
                            i = dve.tensor_tensor_reduce(scratch[0:R, :], same[par][0:R, c, :], before[0:R, :], 1.0, 0.0,
                                                         ALU.mult, ALU.add, repeat[0:R, c:c + 1])
                            ch.link(i)
                        ch.link(dve.scalar_tensor_tensor(repeat[0:R, :], repeat[0:R, :], 0.0, spare[0:R, bass.ds(s * C, C)],
                                                         ALU.is_gt, ALU.mult))
                        ch.link(dve.tensor_tensor(dst_now[par][0:R, :], repeat[0:R, :], dst_f[0:R, bass.ds(s * C, C)], ALU.add))

                    def step(s, par, half):
                        ch = Chain(dve, s_ch, 1 + FIRST + s * CHAIN)
                        more = not isinstance(s, int) or s < NG - 1
                        for j in range(C):
                            phi(ch, s, j)
                            if j == 0 and more:
                                sources(s + 1, 1 - par, half + par)
                                x_variances(ch, s + 1, 1 - par, half + par)
                            if j == 1 and more:
                                x_normalise(ch, s + 1, 1 - par)
                            if j == 1:
                                dve.wait_ge(s_tc, (s + 1) * KC)
                                for c in range(KC):
                                    i = dve.bn_stats(bn_part[:, c, bass.ds(s * 6, 6)], xn_t[:, c, :])
                                i.then_inc(s_col, 1)
                            if j == 2:
                                dve.wait_ge(s_gat[par], 64 * (half + 1))
                                variances(ch, s, gat[par], 1)
                                repeats(ch, s, par)
                            if j == 3:
                                dve.wait_ge(s_std, 2 * s + 3 if more else 2 * NG)
                                normalise(ch, gat[par], gat[par], 1, None).then_inc(s_gn, 1)
                        assert not more or ch.n == CHAIN, ch.n

                    FIRST = 9
                    ch = Chain(dve, s_ch, 1)
                    dve.wait_ge(s_ch, 1)
                    sources(0, 0, 0)
                    x_variances(ch, 0, 0, 0)
                    x_normalise(ch, 0, 0)
                    assert ch.n == FIRST
                    groups(dve, step)
        first.close()

        ffn = ExitStack()
        w1_hi = sb(ffn, "w1_hi", [P, KC, W1_COLS], F32R)
        w2_hi = sb(ffn, "w2_hi", [P, FC, D], F32R)
        w1_lo = sb(ffn, "w1_lo", [P, KC, W1_COLS], F32R)
        w2_lo = sb(ffn, "w2_lo", [P, FC, D], F32R)
        b1 = sb(ffn, "b1", [P, FC])
        scale2 = sb(ffn, "scale2", [P, D])
        shift2 = sb(ffn, "shift2", [P, D])
        s_ffn = sem("s_ffn")
        FFN_DMAS = 22
        conv_rows = sb(ffn, "conv_rows", [2, D])
        sums = ExitStack()
        u_acc = sb(sums, "u_acc", [P, D])
        q_acc = sb(sums, "q_acc", [P, D])
        w1 = sb(sums, "w1", [P, KC, W1_COLS])
        w2 = sb(sums, "w2", [P, FC, D])

        def load_experts(eng):
            n = 0
            for k, bank_name in enumerate(("sp", "fq")):
                for c in range(KC):
                    to = w1[:, c, k * 512:k * 512 + 512].rearrange("p (e f) -> p e f", e=EXPERTS)
                    eng.dma_start(to, a["L0_ffn_W1_" + bank_name][:, c * P:c * P + P, :].rearrange("e p f -> p e f")).then_inc(s_ffn, 16)
                    n += 1
                two = a["L0_ffn_W2_" + bank_name].rearrange("e f d -> (e f) d").rearrange("(c p) d -> p c d", p=P)
                eng.dma_start(w2[:, 4 * k:4 * k + 4, :], two).then_inc(s_ffn, 16)
                eng.dma_start(w2[64 + 8 * k:72 + 8 * k, 8, :], a["L0_ffn_b2_" + bank_name]).then_inc(s_ffn, 16)
                eng.dma_start(w1[:, :, 1088 + 8 * k:1096 + 8 * k], a["L0_ffn_Wr_" + bank_name].rearrange("(c p) e -> p c e", p=P)).then_inc(s_ffn, 16)
                eng.dma_start(b1[64 + 8 * k:72 + 8 * k, 8:9], a["L0_ffn_br_" + bank_name].rearrange("(e a) -> e a", a=1), allow_slow_non_contiguous=True).then_inc(s_ffn, 16)
                eng.dma_start(b1[:, 4 * k:4 * k + 4], a["L0_ffn_b1_" + bank_name].rearrange("e f -> (e f)").rearrange("(c p) -> p c", p=P), allow_slow_non_contiguous=True).then_inc(s_ffn, 16)
                n += 5
            eng.dma_start(w1[:, :, 1024:1088], a["L0_ffn_Ws1"].rearrange("(c p) f -> p c f", p=P)).then_inc(s_ffn, 16)
            eng.dma_start(w2[0:64, 8, :], a["L0_ffn_Ws2"]).then_inc(s_ffn, 16)
            eng.dma_start(w2[80:81, 8, :], a["L0_ffn_bs2"].rearrange("(a d) -> a d", a=1)).then_inc(s_ffn, 16)
            eng.dma_start(b1[0:64, 8:9], a["L0_ffn_bs1"].rearrange("(f a) -> f a", a=1), allow_slow_non_contiguous=True).then_inc(s_ffn, 16)
            assert n + 4 == FFN_DMAS

        with ExitStack() as st:
            g_all = sb(st, "g_all", [P, KC, D])
            g_t = sb(st, "g_t", [P, KC, D])
            kv_bd = sb(st, "kv_bd", [P, KC, P])
            gamma = sb(st, "gamma", [P, KC])
            beta = sb(st, "beta", [P, KC])
            col = sb(st, "col", [P, KC, 2])
            col_std = sb(st, "col_std", [P, KC])
            col_tmp = sb(st, "col_tmp", [P, KC])
            scale1 = sb(st, "scale1", [P, KC])
            shift1 = sb(st, "shift1", [P, KC])

            s_mid_in = sem("s_mid_in")
            s_col_var = sem("s_col_var")
            s_col_std = sem("s_col_std")
            s_shift = sem("s_shift")
            s_tw = sem("s_tw")
            s_kv = sem("s_kv")
            s_ch = sem("s_ch2")
            STAGES2 = ["g_copy", "turn_g", "gt", "kv", "bd", "kvp", "done"]
            now = {name: i + 1 for i, name in enumerate(STAGES2)}

            with nc.Block() as block:
                @block.sync
                def _(sp):
                    sp.dma_start(gamma[:, :], a["L0_gnn_norm1_g"].rearrange("(c p) -> p c", p=P), allow_slow_non_contiguous=True).then_inc(s_mid_in, 16)
                    sp.dma_start(beta[:, :], a["L0_gnn_norm1_b"].rearrange("(c p) -> p c", p=P), allow_slow_non_contiguous=True).then_inc(s_mid_in, 16)
                    sp.dma_start(conv_rows[1:2, :], a["L0_gnn_b_conv"].rearrange("(a d) -> a d", a=1)).then_inc(s_mid_in, 16)
                    load_experts(sp)

                @block.scalar
                def _(act):
                    for f in range(KC):
                        i = act.activation(g_all[:, f, :], bank[f][:, :], ACT.Copy)
                    i.then_inc(s_kv, 1)
                    act.wait_ge(s_col_var, 1)
                    act.activation(col_std[:, :], col[:, :, 1], ACT.Sqrt).then_inc(s_col_std, 1)
                    act.wait_ge(s_kv, now["turn_g"])
                    for c in range(KC):
                        i = act.activation(g_t[:, c, :], bank[4 + c][:, :], ACT.Copy)
                    i.then_inc(s_kv, 1)
                    act.wait_ge(s_kv, now["kvp"])
                    for f in range(KC):
                        i = act.activation(kvp[:, f, :], bank[f][:, :], ACT.Copy)
                    i.then_inc(s_kv, 1)

                @block.tensor
                def _(pe):
                    pe.wait_ge(s_kv, now["g_copy"])
                    for c in range(KC):
                        for f in range(KC):
                            t = pe.transpose(bank[4 + c][:, f * P:f * P + P], g_all[:, f, c * P:c * P + P], ident[:, :])
                    t.then_inc(s_kv, 1)
                    pe.wait_ge(s_kv, now["gt"])
                    for h in range(KC):
                        for c in range(KC):
                            m = pe.matmul(bank[0][:, h * P:h * P + P], w_v[:, c, h * P:h * P + P],
                                          g_t[:, c, h * P:h * P + P], start=(c == 0), stop=(c == KC - 1))
                    m.then_inc(s_kv, 1)
                    for f in range(KC):
                        m = pe.matmul(bank[4][:, f:f + 1], ks_acc[0:R, f * P:f * P + P], ones[0:R, 0:1], start=True, stop=True)
                    pe.wait_ge(s_shift, 1)
                    pe.wait_ge(s_mid_in, 48)
                    for c in range(KC):
                        m = pe.matmul(bank[5][0:1, :], shift1[:, c:c + 1], w_conv[:, c, :], start=(c == 0), stop=(c == KC - 1))
                    m.then_inc(s_tw, 1)
                    pe.wait_ge(s_kv, now["bd"])
                    for h in range(KC):
                        m = pe.matmul(bank[h][:, :], kv_bd[:, h, :], w_proj[:, h, :], start=True, stop=True)
                    m.then_inc(s_kv, 1)

                @block.vector
                def _(dve):
                    ch = Chain(dve, s_ch)
                    for c in range(KC):
                        i = dve.bn_aggr(col[:, c, :], bn_part[:, c, :])
                    ch.link(i)
                    dve.tensor_scalar(col[:, :, 1], col[:, :, 1], BN_EPS, None, ALU.add).then_inc(s_col_var, 1)
                    dve.wait_ge(s_col_std, 1)
                    inverse_root(ch, dve, scale1[:, :], col_std[:, :], col[:, :, 1], col_tmp[:, :])
                    dve.wait_ge(s_mid_in, 48)
                    ch.link(dve.tensor_tensor(scale1[:, :], scale1[:, :], gamma[:, :], ALU.mult))
                    ch.link(dve.tensor_tensor(shift1[:, :], col[:, :, 0], scale1[:, :], ALU.mult))
                    dve.tensor_tensor(shift1[:, :], beta[:, :], shift1[:, :], ALU.subtract).then_inc(s_shift, 1)
                    dve.wait_ge(s_kv, now["kv"])
                    dve.tensor_tensor(kv_bd[:, :, :], bank[0][:, :].rearrange("p (h f) -> p h f", h=KC),
                                      block_mask[:, None, :].broadcast_to([P, KC, P]), ALU.mult).then_inc(s_kv, 1)
                    dve.wait_ge(s_tw, 1)
                    dve.tensor_copy(conv_rows[0:1, :], bank[5][0:1, :])
                    for f in range(KC):
                        dve.tensor_scalar(ks_bd[:, f, :], block_mask[:, :], bank[4][:, f:f + 1], None, ALU.mult)
                        dve.tensor_scalar(w_conv[:, f, :], w_conv[:, f, :], scale1[:, f:f + 1], None, ALU.mult)

        with ExitStack() as st:
            u = [sb(st, f"u{i}", [P, C, D]) for i in range(2)]
            mean = [sb(st, f"mean{i}", [P, C, AGG_W]) for i in range(2)]
            mean_t = w_v
            deg_t = sb(st, "deg_t", [2, G])
            deg = sb(st, "deg", [P, 2, C])
            now_stat = sb(st, "now_stat", [P, 2, C])
            squares = sb(st, "squares", [P, 2, D])

            s_in = [sem(f"s_in{i}") for i in range(2)]
            s_mean = sem("s_mean")
            s_yn = sem("s_yn")
            s_mt = sem("s_mt")
            s_mc = sem("s_mc")
            s_conv = sem("s_conv")
            s_u = sem("s_u")
            s_sq = sem("s_sq")
            s_q_acc = sem("s_q_acc")
            s_ust = [sem(f"s_ust{i}") for i in range(2)]
            s_ch = sem("s_ch3")
            s_pc = sem("s_pc3")
            FIRST3, CHAIN3 = 5, 8
            s_wh = sem("s_wh")

            def halves(k):
                if k < KC:
                    return w1[:, k, :], w1_hi[:, k, :], w1_lo[:, k, :]
                k, rows = k - KC, P if k - KC < FC - 1 else 64 + 2 * EXPERTS + 1
                return w2[0:rows, k, :], w2_hi[0:rows, k, :], w2_lo[0:rows, k, :]

            def pieces(s, j):
                if not isinstance(s, int) or s < NG - 2:
                    return range(0)
                return range(j, j + 1) if s == NG - 2 else range(KC + FC * j // C, KC + FC * (j + 1) // C)

            with nc.Block() as block:
                @block.sync
                def _(sp):
                    def load(s, par, half):
                        wait(sp, s_mt, (s - 1) * (KC + 1) if not isinstance(s, int) or s >= 2 else 0)
                        dma_rows(sp, mean[par][0:R], agg_g[s], s_in[par])
                        wait(sp, s_ust[par], 32 * half)
                        settle(sp, s_past_sp)
                        wait(sp, s_sq, (s - 1) * C if not isinstance(s, int) or s >= 2 else 0)
                        settle(sp, s_past_sp)
                        wait(sp, s_ch, FIRST3 + (s - 1) * CHAIN3 if not isinstance(s, int) or s >= 2 else 0)
                        dma_rows(sp, u[par][0:R], x_g[s], s_in[par])

                    def store(s, par):
                        sp.wait_ge(s_u, (s + 1) * C)
                        dma_rows(sp, u_g[s], u[par][0:R], s_ust[par])

                    def step(s, par, half):
                        if not isinstance(s, int) or s < NG - 1:
                            load(s + 1, 1 - par, half + par)
                        store(s, par)
                    load(0, 0, 0)
                    groups(sp, step)
                    for i in range(2):
                        sp.wait_ge(s_ust[i], 32 * (NG // 2))
                    sp.wait_ge(s_ffn, 16 * FFN_DMAS)

                @block.gpsimd
                def _(pool):
                    pool.memset(q_acc[:, :], 0.0).then_inc(s_pc, 1)

                    def step(s, par, half):
                        for j in range(C):
                            n = s * C + j
                            pool.wait_ge(s_sq, n + 1)
                            pool.wait_ge(s_q_acc, n) if not isinstance(s, int) or n > 0 else pool.wait_ge(s_pc, 1)
                            pool.tensor_tensor(q_acc[0:R, :], q_acc[0:R, :], squares[0:R, j % 2, :], ALU.add).then_inc(s_q_acc, 1)
                            for k in pieces(s, j):
                                whole, high, low = halves(k)
                                pool.wait_ge(s_wh, k + 1)
                                pool.tensor_tensor(low, whole, high.bitcast(F32), ALU.subtract)
                    groups(pool, step)

                @block.tensor
                def _(pe):
                    def turn(s, par):
                        pe.wait_ge(s_mean, s + 1)
                        for c in range(KC + 1):
                            wait(pe, s_mc, s * (KC + 1) + c - 1)
                            wide = P if c < KC else 2
                            for j in range(C):
                                t = pe.transpose(bank[c % 2][0:wide, j * R:j * R + R],
                                                 mean[par][0:R, j, c * P:c * P + wide], ident[0:R, 0:R])
                            t.then_inc(s_mt, 1)

                    def conv(s, j):
                        if j == 0:
                            pe.wait_ge(s_mc, (s + 1) * (KC + 1))
                        wait(pe, s_u, s * C + j - 1)
                        to = bank[2 + j % 2][0:R, :]
                        for c in range(KC):
                            pe.matmul(to, mean_t[:, c, j * R:j * R + R], w_conv[:, c, :], start=(c == 0), stop=False)
                        pe.matmul(to, deg_t[:, j * R:j * R + R], conv_rows[:, :], start=False, stop=True).then_inc(s_conv, 1)

                    def step(s, par, half):
                        for j in range(C):
                            conv(s, j)
                        if not isinstance(s, int) or s < NG - 1:
                            turn(s + 1, 1 - par)
                    turn(0, 0)
                    groups(pe, step)

                @block.scalar
                def _(act):
                    def copies(s):
                        for c in range(KC + 1):
                            act.wait_ge(s_mt, s * (KC + 1) + c + 1)
                            if c == 0:
                                wait(act, s_conv, s * C)
                            if c < KC:
                                act.activation(mean_t[:, c, 0:G], bank[c % 2][:, 0:G], ACT.Copy).then_inc(s_mc, 1)
                            else:
                                act.activation(deg_t[:, :], bank[c % 2][0:2, 0:G], ACT.Copy).then_inc(s_mc, 1)

                    def step(s, par, half):
                        for j in range(C):
                            n = s * C + j
                            act.wait_ge(s_u, n + 1)
                            wait(act, s_q_acc, n - 1)
                            act.activation(squares[0:R, j % 2, :], u[par][0:R, j, :], ACT.Square).then_inc(s_sq, 1)
                            for k in pieces(s, j):
                                whole, high, _ = halves(k)
                                act.wait_ge(s_ffn, 16 * FFN_DMAS)
                                act.activation(high, whole, ACT.Copy).then_inc(s_wh, 1)
                        if not isinstance(s, int) or s < NG - 1:
                            copies(s + 1)
                    copies(0)
                    groups(act, step)

                @block.vector
                def _(dve):
                    def prepare(ch, s, par, half):
                        dve.wait_ge(s_in[par], 64 * (half + 1))
                        ch.link(dve.tensor_scalar(deg[0:R, 0, :], mean[par][0:R, :, D], 1.0, None, ALU.max))
                        ch.link(dve.reciprocal(deg[0:R, 1, :], deg[0:R, 0, :]))
                        dve.memset(mean[par][0:R, :, D + 1:D + 2], 1.0)
                        dve.tensor_scalar(mean[par][0:R, :, D:D + 1], mean[par][0:R, :, D:D + 1], 1.0, None, ALU.min)
                        for c in range(C):
                            i = dve.tensor_scalar(mean[par][0:R, c, 0:D], mean[par][0:R, c, 0:D], deg[0:R, 1, c:c + 1], None, ALU.mult)
                        i.then_inc(s_mean, 1)
                        ch.link(dve.tensor_copy(now_stat[0:R, :, :], row_stat[0:R, s, :, :]))
                        for c in range(C):
                            i = dve.tensor_scalar(u[par][0:R, c, :], u[par][0:R, c, :], now_stat[0:R, 0, c:c + 1],
                                                  now_stat[0:R, 1, c:c + 1], ALU.subtract, ALU.mult)
                        ch.link(i)

                    def step(s, par, half):
                        more = not isinstance(s, int) or s < NG - 1
                        ch = Chain(dve, s_ch, FIRST3 + s * CHAIN3)
                        for j in range(C):
                            n = s * C + j
                            dve.wait_ge(s_conv, n + 1)
                            i = dve.scalar_tensor_tensor(u[par][0:R, j, :], bank[2 + j % 2][0:R, :], 0.0, u[par][0:R, j, :],
                                                         ALU.max, ALU.add)
                            if isinstance(s, int) and n == 0:
                                i.then_inc(s_yn, 1)
                                dve.wait_ge(s_yn, 1)
                                i = dve.tensor_tensor(u[par][0:R, 0, :], u[par][0:R, 0, :], att_delta[0:R, :], ALU.add)
                            i.then_inc(s_u, 1)
                            dve.wait_ge(s_u, n + 1)
                            ch.link(dve.tensor_tensor(u_acc[0:R, :], u_acc[0:R, :], u[par][0:R, j, :], ALU.add))
                            if j == 0 and more:
                                prepare(ch, s + 1, 1 - par, half + par)
                        assert not more or ch.n == CHAIN3, ch.n

                    ch = Chain(dve, s_ch)
                    ch.link(dve.memset(u_acc[:, :], 0.0))
                    prepare(ch, 0, 0, 0)
                    assert ch.n == FIRST3
                    groups(dve, step)

        with ExitStack() as st:
            gain = sb(st, "gain", [P, 3, D])
            mu = sb(st, "mu", [P, D])
            var = sb(st, "var", [P, D])
            std = sb(st, "std", [P, D])
            tmp = sb(st, "tmp", [P, D])
            s_gain = sem("s_gain")
            s_tot = sem("s_tot")
            s_v2 = sem("s_v2")
            s_r2 = sem("s_r2")
            s_ch = sem("s_ch4")
            with nc.Block() as block:
                @block.sync
                def _(sp):
                    for k, name in enumerate(("L0_gnn_norm2_g", "L0_gnn_norm2_b", "L0_mix_b_proj")):
                        sp.dma_start(gain[:, k, :], a[name].rearrange("(a d) -> a d", a=1).broadcast_to([P, D])).then_inc(s_gain, 16)

                @block.tensor
                def _(pe):
                    pe.matmul(bank[0][:, :], ones[0:R, :], u_acc[0:R, :], start=True, stop=True)
                    pe.matmul(bank[1][:, :], ones[0:R, :], q_acc[0:R, :], start=True, stop=True).then_inc(s_tot, 1)

                @block.scalar
                def _(act):
                    act.wait_ge(s_v2, 1)
                    act.activation(std[:, :], var[:, :], ACT.Sqrt).then_inc(s_r2, 1)

                @block.vector
                def _(dve):
                    ch = Chain(dve, s_ch)
                    dve.wait_ge(s_tot, 1)
                    ch.link(dve.tensor_scalar(mu[:, :], bank[0][:, :], 1.0 / N, None, ALU.mult))
                    ch.link(dve.tensor_tensor(tmp[:, :], mu[:, :], mu[:, :], ALU.mult))
                    ch.link(dve.scalar_tensor_tensor(var[:, :], bank[1][:, :], 1.0 / N, tmp[:, :], ALU.mult, ALU.subtract))
                    dve.tensor_scalar(var[:, :], var[:, :], 0.0, BN_EPS, ALU.max, ALU.add).then_inc(s_v2, 1)
                    dve.wait_ge(s_r2, 1)
                    inverse_root(ch, dve, scale2[:, :], std[:, :], var[:, :], tmp[:, :])
                    dve.wait_ge(s_gain, 48)
                    ch.link(dve.tensor_tensor(scale2[:, :], scale2[:, :], gain[:, 0, :], ALU.mult))
                    ch.link(dve.tensor_tensor(tmp[:, :], mu[:, :], scale2[:, :], ALU.mult))
                    ch.link(dve.tensor_tensor(shift2[:, :], gain[:, 1, :], gain[:, 2, :], ALU.add))
                    ch.link(dve.tensor_tensor(shift2[:, :], shift2[:, :], tmp[:, :], ALU.subtract))
        sums.close()
        with ExitStack() as st:
            z = [sb(st, f"z{i}", [P, C, D]) for i in range(2)]
            x_in, xn, x2 = w_proj, w_conv, w_v
            xn_t = sb(st, "zn_t", [P, KC, G])
            low = sb(st, "lowq", [P, 2, G])
            qz = sb(st, "qz", [P, KC, G])
            rden = sb(st, "rden", [P, G])
            x2_hi = sb(st, "x2_hi", [P, KC, G], F32R)
            x2_lo = sb(st, "x2_lo", [P, KC, G], F32R)
            hid = sb(st, "hid", [P, 2, G])
            shared = sb(st, "shared", [P, G])
            gated_hi = sb(st, "gated_hi", [P, 2, G], F32R)
            gated_lo = sb(st, "gated_lo", [P, 2, G], F32R)
            logit_t = sb(st, "logit_t", [P, G])
            now_stat = sb(st, "z_stat", [P, 2, C])
            bn = sb(st, "bnz", [P, C, 6])
            st_mv = sb(st, "mvz", [P, C, 2])
            st_std = sb(st, "stdz", [P, C])
            st_rstd = sb(st, "rstdz", [P, C])
            st_tmp = sb(st, "tmpz", [P, C])
            EB = 2 * EXPERTS
            LAST = 64 + EB + 1
            top_l = sb(st, "top_l", [P, C * 2])
            shifted = sb(st, "shifted", [P, C * 2, EXPERTS])
            expd = sb(st, "expd", [P, C * 2, EXPERTS])
            gate = sb(st, "gate", [P, C * 2])
            descend = sb(st, "descend", [P, EXPERTS])
            pick = sb(st, "pick", [P, C * 2, EXPERTS])
            picked = sb(st, "picked", [P, C * 2])
            one_hot = sb(st, "one_hot", [P, C, EB], BF16)
            carried = sb(st, "carried", [P, EB])
            place = sb(st, "place", [P, C, EB])
            gates = sb(st, "gates", [P, C, EB + 1])
            rest = sb(st, "rest", [P, C, EB])
            parts = sb(st, "parts", [P, C, 3 * EB], BF16)
            parts_t = sb(st, "parts_t", [3 * EB, C, R], BF16)
            spread = sb(st, "spread", [3 * EB, 8, P], BF16)
            upto = sb(st, "upto", [P, P], BF16)
            ones_b = sb(st, "ones_b", [P, P], BF16)
            ident_b = sb(st, "ident_b", [P, P], BF16)

            s_x = sem("s_zx")
            s_ul = sem("s_ul")
            s_set = sem("s_set")
            s_base = sem("s_base")
            s_bc = sem("s_bc")
            s_n = sem("s_n")
            s_nt = sem("s_nt")
            s_nc = sem("s_nc")
            s_q = sem("s_q")
            s_ql = sem("s_ql")
            s_qe = sem("s_qe")
            s_qp = sem("s_qp")
            s_den = sem("s_den")
            s_rd = sem("s_rd")
            s_qz = sem("s_qz")
            s_mix = sem("s_mix")
            s_xp = sem("s_xp")
            s_v = sem("s_v")
            s_r = sem("s_r")
            s_x2 = sem("s_x2")
            s_xt = sem("s_xt")
            s_xc = sem("s_xc")
            s_xl = sem("s_xl")
            s_lc = sem("s_lc")
            s_lg = sem("s_lg")
            s_sh = sem("s_sh")
            s_le = sem("s_le")
            s_oh = sem("s_oh")
            s_pos = sem("s_pos")
            s_gate = sem("s_gate")
            s_gt = sem("s_gt")
            s_gc = sem("s_gc")
            s_h = sem("s_h")
            s_ge = sem("s_ge")
            s_mk = sem("s_mk")
            s_hm = sem("s_hm")
            s_gh = sem("s_gh")
            s_gl = sem("s_gl")
            s_out = sem("s_out")
            OUTS = FC - 1 + C
            s_o = sem("s_o")
            s_st = [sem(f"s_st{i}") for i in range(2)]
            s_ch = sem("s_ch5")
            s_past_pe = sem("s_past_pe")

            def pipeline(eng, step):
                groups(eng, lambda i, par, half: step(i, par, half, True, not isinstance(i, int) or i > 0))
                step(NG, 0, NG // 2, False, True)

            with nc.Block() as block:
                @block.sync
                def _(sp):
                    def load_x(i):
                        wait(sp, s_n, i)
                        settle(sp, s_past_sp)
                        wait(sp, s_base, i * C)
                        dma_rows(sp, x_in[0:R], x_g[i], s_x)

                    def step(i, par, half, front, back):
                        if front:
                            wait(sp, s_st[par], 32 * half)
                            dma_rows(sp, z[par][0:R], u_g[i], s_ul)
                        if not isinstance(i, int) or i < NG - 1:
                            load_x(i + 1)
                        if back:
                            sp.wait_ge(s_o, i * C)
                            dma_rows(sp, out_g[i - 1], z[1 - par][0:R], s_st[1 - par])
                    load_x(0)
                    pipeline(sp, step)
                    for k in range(2):
                        sp.wait_ge(s_st[k], 32 * (NG // 2))

                @block.gpsimd
                def _(pool):
                    ch = Chain(pool, s_bc)
                    ch.link(pool.memset(ones_b[:, :], 1.0))
                    ch.link(pool.affine_select(out=upto[:, :], in_=ones_b[:, :], compare_op=ALU.is_ge, fill=0.0,
                                               base=0, pattern=[[1, P]], channel_multiplier=-1))
                    ch.link(pool.tensor_copy(ident_b[:, :], ident[:, :]))
                    ch.link(pool.memset(spread[:, :, :], 0.0))
                    for t in range(3):
                        part = spread[:, :, :].rearrange("k c (e f) -> k c e f", e=2)
                        ch.link(pool.affine_select(out=part, in_=part, compare_op=ALU.not_equal, fill=1.0, base=-t * EB,
                                                   pattern=[[-2, 8], [-1, 2], [0, 64]], channel_multiplier=1))
                    ch.link(pool.iota(descend[:, :], pattern=[[-1, EXPERTS]], base=EXPERTS, channel_multiplier=0,
                                      allow_small_or_imprecise_dtypes=True))
                    pool.memset(gates[:, :, EB:EB + 1], 1.0)
                    pool.memset(carried[:, :], 0.0).then_inc(s_set, 1)

                    def base(i, par):
                        ch = Chain(pool, s_bc, 8 + i * 2 * C)
                        pool.wait_ge(s_x, 32 * (i + 1))
                        pool.wait_ge(s_ul, 32 * (i + 1))
                        for j in range(C):
                            tile = z[par][0:R, j, :]
                            ch.link(pool.tensor_tensor(tile, tile, scale2[0:R, :], ALU.mult))
                            ch.link(pool.tensor_tensor(tile, tile, shift2[0:R, :], ALU.add))
                            pool.tensor_tensor(tile, tile, x_in[0:R, j, :], ALU.add).then_inc(s_base, 1)

                    def low_half(b, n):
                        pool.wait_ge(s_gh, b * FC + n + 1)
                        wait(pool, s_out, b * OUTS + max(n - 1, 0))
                        whole, rows = (shared[0:LAST, :], LAST) if n == 0 else (hid[:, n % 2, :], P)
                        pool.tensor_tensor(gated_lo[0:rows, n % 2, :], whole, gated_hi[0:rows, n % 2, :].bitcast(F32),
                                           ALU.subtract).then_inc(s_gl, 1)

                    def step(i, par, half, front, back):
                        if front:
                            base(i, par)
                        if back:
                            for n in range(FC):
                                low_half(i - 1, n)
                    pipeline(pool, step)

                @block.tensor
                def _(pe):
                    def turn_x(i):
                        pe.wait_ge(s_n, i + 1)
                        for c in range(KC):
                            wait(pe, s_o, (i - 2) * C + c + 1 if not isinstance(i, int) or i >= 2 else 0)
                            for j in range(C):
                                t = pe.transpose(bank[c][:, j * R:j * R + R], xn[0:R, j, c * P:c * P + P], ident[0:R, 0:R])
                            t.then_inc(s_nt, 1)

                    def turn_x2(i, b, front):
                        pe.wait_ge(s_x2, b + 1)
                        for c in range(KC):
                            if front:
                                pe.wait_ge(s_nc, i * KC + c + 1)
                            else:
                                pe.wait_ge(s_o, (i - 2) * C + c + 1)
                            for j in range(C):
                                t = pe.transpose(bank[c][:, j * R:j * R + R], x2[0:R, j, c * P:c * P + P], ident[0:R, 0:R])
                            t.then_inc(s_xt, 1)

                    def front_q(i, f, back):
                        if f == 0:
                            pe.wait_ge(s_nc, (i + 1) * KC)
                        if back:
                            pe.wait_ge(s_xl, (i - 1) * KC + f + 1)
                        for c in range(KC):
                            m = pe.matmul(bank[f][:, 0:G], phi_q[:, c, f * P:f * P + P], xn_t[:, c, :],
                                          start=(c == 0), stop=(c == KC - 1))
                        m.then_inc(s_q, 1)

                    def hidden(b, n):
                        if n == 0:
                            pe.wait_ge(s_xl, (b + 1) * KC)
                        wait(pe, s_ge, b * FC + max(n - 1, 0))
                        wide = P if n > 0 else 64 + EB
                        at = (n - 1) * P if n > 0 else 2 * EXPERTS * FF
                        for c in range(KC):
                            m = split_product(pe, bank[4 + n % 2][0:wide, 0:G],
                                              (w1_hi[:, c, at:at + wide], w1_lo[:, c, at:at + wide]),
                                              (x2_hi[:, c, :], x2_lo[:, c, :]), c == 0, c == KC - 1)
                        m.then_inc(s_h, 1)

                    def turn_logits(i, b):
                        pe.wait_ge(s_lc, b + 1)
                        pe.wait_ge(s_xp, i * C)
                        settle(pe, s_past_pe)
                        for j in range(C):
                            t = pe.transpose(bank[7][0:R, j * EB:j * EB + EB], logit_t[64:64 + EB, j * R:j * R + R],
                                             ident[64:64 + EB, 64:64 + EB])
                        t.then_inc(s_lg, 1)

                    def places(b):
                        pe.wait_ge(s_oh, b + 1)
                        for j in range(C):
                            for k in range(j + 1):
                                pe.matmul(bank[7][0:R, 64 + j * EB:80 + j * EB], (ones_b if k < j else upto)[0:R, 0:R],
                                          one_hot[0:R, k, :], start=(k == 0), stop=(k == j))
                        for k in range(C):
                            m = pe.matmul(bank[7][0:R, 128:144], ones_b[0:R, 0:R], one_hot[0:R, k, :], start=(k == 0), stop=(k == C - 1))
                        m.then_inc(s_pos, 1)

                    def turn_gates(b):
                        pe.wait_ge(s_gate, b + 1)
                        wait(pe, s_hm, b * 8)
                        turned = bank[7][0:3 * EB, 0:256].bitcast(BF16)
                        for j in range(C):
                            pe.transpose(bank[6][0:EB + 1, j * R:j * R + R], gates[0:R, j, :], ident[0:R, 0:R])
                        for j in range(C):
                            t = pe.transpose(turned[:, j * P:j * P + R], parts[0:R, j, :], ident_b[0:R, 0:R])
                        t.then_inc(s_gt, 1)

                    def mask(b, n):
                        if n == 1:
                            pe.wait_ge(s_gc, b + 1)
                        else:
                            pe.wait_ge(s_hm, b * 8 + n - 1)
                        pe.matmul(bank[6][:, 0:G], spread[:, n - 1, :], parts_t[:, :, :], start=True, stop=True).then_inc(s_mk, 1)

                    def den(i, f, back):
                        pe.wait_ge(s_qp, i * KC + f + 1)
                        if f > 0:
                            pe.wait_ge(s_rd, i * KC + f)
                        elif back:
                            pe.wait_ge(s_gc, i)
                        pe.matmul(bank[7][:, 0:G], ks_bd[:, f, :], qz[:, f, :], start=True, stop=True).then_inc(s_den, 1)

                    def mix(i, j):
                        if j == 0:
                            pe.wait_ge(s_qz, (i + 1) * KC)
                        else:
                            pe.wait_ge(s_xp, i * C + j)
                        for f in range(KC):
                            m = pe.matmul(bank[7][0:R, :], qz[:, f, j * R:j * R + R], kvp[:, f, :],
                                          start=(f == 0), stop=(f == KC - 1))
                        m.then_inc(s_mix, 1)

                    def outputs(i, b, n, front):
                        if n == 0 and front:
                            pe.wait_ge(s_qp, (i + 1) * KC)
                        pe.wait_ge(s_gl, b * FC + n + 1)
                        rows, k = (P, n - 1) if n > 0 else (LAST, FC - 1)
                        for j in range(C):
                            at = slice(j * R, j * R + R)
                            m = split_product(pe, bank[j][0:R, :],
                                              (gated_hi[0:rows, n % 2, at], gated_lo[0:rows, n % 2, at]),
                                              (w2_hi[0:rows, k, :], w2_lo[0:rows, k, :]), n == 0, n == FC - 1)
                            if n == FC - 1 or j == C - 1:
                                m.then_inc(s_out, 1)

                    def step(i, par, half, front, back):
                        if front:
                            turn_x(i)
                        if back:
                            turn_x2(i, i - 1, front)
                        if front:
                            front_q(i, 0, back)
                        if back:
                            hidden(i - 1, 0)
                        if front:
                            front_q(i, 1, back)
                        if back:
                            turn_logits(i, i - 1)
                        if front:
                            front_q(i, 2, back)
                        if back:
                            hidden(i - 1, 1)
                        if front:
                            front_q(i, 3, back)
                        if back:
                            places(i - 1)
                            hidden(i - 1, 2)
                            turn_gates(i - 1)
                        for n in range(FC):
                            if back and 1 <= n <= FC - 3:
                                hidden(i - 1, n + 2)
                            if back and n < FC - 1:
                                mask(i - 1, n + 1)
                            if front and n < KC:
                                den(i, n, back)
                            if back:
                                outputs(i, i - 1, n, front)
                            if front and KC <= n < KC + C:
                                mix(i, n - KC)
                    pe.wait_ge(s_set, 1)
                    pipeline(pe, step)

                @block.scalar
                def _(act):
                    def copy_x(i):
                        for c in range(KC):
                            act.wait_ge(s_nt, i * KC + c + 1)
                            if c == 0:
                                wait(act, s_q, i * KC)
                            act.activation(xn_t[:, c, :], bank[c][:, 0:G], ACT.Copy).then_inc(s_nc, 1)

                    def high_x2(b):
                        for c in range(KC):
                            act.wait_ge(s_xt, b * KC + c + 1)
                            if c == 0:
                                wait(act, s_h, b * FC)
                            act.activation(x2_hi[:, c, :], bank[c][:, 0:G], ACT.Copy).then_inc(s_xc, 1)

                    def exp_q(i, f):
                        act.wait_ge(s_ql, i * KC + f + 1)
                        act.activation(low[:, f % 2, :], low[:, f % 2, :], ACT.Exp).then_inc(s_qe, 1)

                    def copy_logits(b):
                        act.wait_ge(s_h, b * FC + 1)
                        act.activation(logit_t[64:64 + EB, :], bank[4][64:64 + EB, 0:G], ACT.Identity,
                                       bias=b1[64:64 + EB, 8:9]).then_inc(s_lc, 1)

                    def exp_logits(b):
                        act.wait_ge(s_sh, b + 1)
                        act.activation(expd[0:R, :, :], shifted[0:R, :, :], ACT.Exp).then_inc(s_le, 1)

                    def gelu(b, n):
                        act.wait_ge(s_h, b * FC + n + 1)
                        wait(act, s_gl, b * FC + max(n - 1, 0))
                        to, wide, k = (hid[:, n % 2, :], P, n - 1) if n > 0 else (shared[0:64, :], 64, FC - 1)
                        act.activation(to, bank[4 + n % 2][0:wide, 0:G], ACT.Gelu, bias=b1[0:wide, k:k + 1]).then_inc(s_ge, 1)

                    def copy_gates(b):
                        act.wait_ge(s_gt, b + 1)
                        wait(act, s_mk, b * 8)
                        turned = bank[7][0:3 * EB, 0:256].bitcast(BF16).rearrange("k (c r) -> k c r", c=C)
                        act.activation(parts_t[:, :, :], turned[:, :, 0:R], ACT.Copy)
                        act.activation(shared[64:LAST, :], bank[6][0:EB + 1, 0:G], ACT.Copy).then_inc(s_gc, 1)

                    def high_half(b, n):
                        if n == 0:
                            act.wait_ge(s_gc, b + 1)
                        else:
                            act.wait_ge(s_hm, b * 8 + n)
                        wait(act, s_out, b * OUTS + max(n - 1, 0))
                        whole, rows = (shared[0:LAST, :], LAST) if n == 0 else (hid[:, n % 2, :], P)
                        act.activation(gated_hi[0:rows, n % 2, :], whole, ACT.Copy).then_inc(s_gh, 1)

                    def root(i):
                        act.wait_ge(s_v, i + 1)
                        act.activation(st_std[0:R, :], st_mv[0:R, :, 1], ACT.Sqrt).then_inc(s_r, 1)

                    def step(i, par, half, front, back):
                        if front:
                            copy_x(i)
                        if back:
                            high_x2(i - 1)
                        if front:
                            exp_q(i, 0)
                        if back:
                            copy_logits(i - 1)
                        if front:
                            exp_q(i, 1)
                        if back:
                            exp_logits(i - 1)
                        if front:
                            exp_q(i, 2)
                            exp_q(i, 3)
                        if back:
                            gelu(i - 1, 0)
                            gelu(i - 1, 1)
                            copy_gates(i - 1)
                            for n in range(FC):
                                high_half(i - 1, n)
                                if n + 2 < FC:
                                    gelu(i - 1, n + 2)
                        if front:
                            root(i)
                    act.wait_ge(s_set, 1)
                    pipeline(act, step)

                @block.vector
                def _(dve):
                    def normalise_x(ch, i):
                        dve.wait_ge(s_x, 32 * (i + 1))
                        ch.link(dve.tensor_copy(now_stat[0:R, :, :], row_stat[0:R, i, :, :]))
                        wait(dve, s_nt, i * KC)
                        for c in range(C):
                            k = dve.tensor_scalar(xn[0:R, c, :], x_in[0:R, c, :], now_stat[0:R, 0, c:c + 1],
                                                  now_stat[0:R, 1, c:c + 1], ALU.subtract, ALU.mult)
                        k.then_inc(s_n, 1)

                    def low_x2(b):
                        for c in range(KC):
                            dve.wait_ge(s_xc, b * KC + c + 1)
                            if c == 0:
                                wait(dve, s_h, b * FC)
                            dve.tensor_tensor(x2_lo[:, c, :], bank[c][:, 0:G], x2_hi[:, c, :].bitcast(F32), ALU.subtract).then_inc(s_xl, 1)

                    def phi(i, f):
                        if f == 0:
                            wait(dve, s_mix, i * C)
                        q = bank[f][:, 0:G]
                        dve.wait_ge(s_q, i * KC + f + 1)
                        dve.tensor_scalar(low[:, f % 2, :], q, 0.0, None, ALU.min).then_inc(s_ql, 1)
                        dve.wait_ge(s_qe, i * KC + f + 1)
                        dve.scalar_tensor_tensor(qz[:, f, :], q, 0.0, low[:, f % 2, :], ALU.max, ALU.add).then_inc(s_qp, 1)

                    def route(ch, b):
                        logits = bank[7][0:R, 0:C * EB].rearrange("p (a e) -> p a e", e=EXPERTS)
                        wide = [R, C * 2, EXPERTS]
                        dve.wait_ge(s_lg, b + 1)
                        ch.link(dve.tensor_reduce(top_l[0:R, :], logits, AX.X, ALU.max))
                        dve.tensor_tensor(shifted[0:R, :, :], logits, top_l[0:R, :, None].broadcast_to(wide), ALU.subtract).then_inc(s_sh, 1)
                        dve.wait_ge(s_sh, b + 1)
                        ch.link(dve.scalar_tensor_tensor(pick[0:R, :, :], shifted[0:R, :, :], 0.0,
                                                         descend[0:R, None, :].broadcast_to(wide), ALU.is_ge, ALU.mult))
                        ch.link(dve.tensor_reduce(picked[0:R, :], pick[0:R, :, :], AX.X, ALU.max))
                        wait(dve, s_pos, b)
                        dve.tensor_tensor(one_hot[0:R, :, :].rearrange("p c (k e) -> p (c k) e", k=2), pick[0:R, :, :],
                                          picked[0:R, :, None].broadcast_to(wide), ALU.is_equal).then_inc(s_oh, 1)
                        dve.wait_ge(s_le, b + 1)
                        ch.link(dve.tensor_reduce(gate[0:R, :], expd[0:R, :, :], AX.X, ALU.add))
                        ch.link(dve.reciprocal(gate[0:R, :], gate[0:R, :]))

                    def make_gates(ch, b):
                        dve.wait_ge(s_pos, b + 1)
                        ch.link(dve.tensor_tensor(place[0:R, :, :], bank[7][0:R, 64:128].rearrange("p (c e) -> p c e", c=C),
                                                  carried[0:R, None, :].broadcast_to([R, C, EB]), ALU.add))
                        ch.link(dve.tensor_tensor(carried[0:R, :], carried[0:R, :], bank[7][0:R, 128:144], ALU.add))
                        ch.link(dve.scalar_tensor_tensor(place[0:R, :, :], place[0:R, :, :], float(CAP), one_hot[0:R, :, :],
                                                         ALU.is_le, ALU.mult))
                        wait(dve, s_gt, b)
                        for j in range(C):
                            k = dve.tensor_tensor(gates[0:R, j, 0:EB].rearrange("p (k e) -> p k e", k=2),
                                                  place[0:R, j, :].rearrange("p (k e) -> p k e", k=2),
                                                  gate[0:R, 2 * j:2 * j + 2, None].broadcast_to([R, 2, EXPERTS]), ALU.mult)
                        ch.link(k)
                        ch.link(dve.tensor_copy(parts[0:R, :, 0:EB], gates[0:R, :, 0:EB]))
                        ch.link(dve.tensor_tensor(rest[0:R, :, :], gates[0:R, :, 0:EB], parts[0:R, :, 0:EB], ALU.subtract))
                        ch.link(dve.tensor_copy(parts[0:R, :, EB:2 * EB], rest[0:R, :, :]))
                        ch.link(dve.tensor_tensor(rest[0:R, :, :], rest[0:R, :, :], parts[0:R, :, EB:2 * EB], ALU.subtract))
                        dve.tensor_copy(parts[0:R, :, 2 * EB:3 * EB], rest[0:R, :, :]).then_inc(s_gate, 1)

                    def divide(i, f):
                        dve.wait_ge(s_den, i * KC + f + 1)
                        wait(dve, s_qz, i * KC + f)
                        dve.reciprocal(rden[:, :], bank[7][:, 0:G]).then_inc(s_rd, 1)
                        dve.wait_ge(s_rd, i * KC + f + 1)
                        dve.tensor_tensor(qz[:, f, :], qz[:, f, :], rden[:, :], ALU.mult).then_inc(s_qz, 1)

                    def x_out(i, j, par):
                        dve.wait_ge(s_mix, i * C + j + 1)
                        dve.wait_ge(s_base, i * C + j + 1)
                        dve.tensor_tensor(z[par][0:R, j, :], bank[7][0:R, :], z[par][0:R, j, :], ALU.add).then_inc(s_xp, 1)

                    def variances(ch, i, par):
                        for j in range(C):
                            dve.wait_ge(s_xp, i * C + j + 1)
                            k = dve.bn_stats(bn[0:R, j, :], z[par][0:R, j, :])
                        ch.link(k)
                        settle(dve, s_past_dve)
                        for j in range(C):
                            k = dve.bn_aggr(st_mv[0:R, j, :], bn[0:R, j, :])
                        ch.link(k)
                        dve.tensor_scalar(st_mv[0:R, :, 1], st_mv[0:R, :, 1], LN_EPS, None, ALU.add).then_inc(s_v, 1)

                    def normalise_x2(ch, i, par):
                        dve.wait_ge(s_r, i + 1)
                        inverse_root(ch, dve, st_rstd[0:R, :], st_std[0:R, :], st_mv[0:R, :, 1], st_tmp[0:R, :])
                        wait(dve, s_xt, i * KC)
                        for j in range(C):
                            k = dve.tensor_scalar(x2[0:R, j, :], z[par][0:R, j, :], st_mv[0:R, j, 0:1], st_rstd[0:R, j:j + 1],
                                                  ALU.subtract, ALU.mult)
                        k.then_inc(s_x2, 1)

                    def gated(b, n):
                        dve.wait_ge(s_ge, b * FC + n + 1)
                        dve.wait_ge(s_mk, b * 8 + n)
                        dve.tensor_tensor(hid[:, n % 2, :], hid[:, n % 2, :], bank[6][:, 0:G], ALU.mult).then_inc(s_hm, 1)

                    def outputs(b, par):
                        for j in range(C):
                            dve.wait_ge(s_out, b * OUTS + FC + j)
                            dve.tensor_tensor(z[par][0:R, j, :], bank[j][0:R, :], z[par][0:R, j, :], ALU.add).then_inc(s_o, 1)

                    def step(i, par, half, front, back):
                        ch = Chain(dve, s_ch, 1 if isinstance(i, int) and i == 0 else 21 * i - 12 if front else 21 * i - 13)
                        if back:
                            low_x2(i - 1)
                        if front:
                            phi(i, 0)
                            phi(i, 1)
                        if back:
                            route(ch, i - 1)
                        if front:
                            phi(i, 2)
                            phi(i, 3)
                        if back:
                            make_gates(ch, i - 1)
                        for n in range(FC):
                            if back and n < FC - 1:
                                gated(i - 1, n + 1)
                            if front and n < KC:
                                divide(i, n)
                            if front and KC <= n < KC + C:
                                x_out(i, n - KC, par)
                            if n == 6 and (not isinstance(i, int) or i < NG - 1):
                                normalise_x(ch, i + 1)
                        if front:
                            variances(ch, i, par)
                        if back:
                            outputs(i - 1, 1 - par)
                        if front:
                            normalise_x2(ch, i, par)
                        if not isinstance(i, int) or i == 1:
                            assert ch.n == 21, ch.n
                        if isinstance(i, int) and i == 0:
                            assert ch.n == 8, ch.n
                    dve.wait_ge(s_set, 1)
                    ch = Chain(dve, s_ch)
                    normalise_x(ch, 0)
                    pipeline(dve, step)
        ffn.close()
        mid.close()


_INS = ["x", "src", "dst"] + ["L0_gnn_" + n for n in (
    "norm1_g", "norm1_b", "norm2_g", "norm2_b", "W_conv", "b_conv", "Wq", "Wk", "Wv", "Wo", "proj")] + [
    "L0_mix_" + n for n in ("w_qkv", "proj_mat", "w_proj", "b_proj")] + ["L0_ffn_" + n for n in (
        "Wr_sp", "br_sp", "Wr_fq", "br_fq", "Ws1", "bs1", "Ws2", "bs2", "W1_sp", "b1_sp", "W2_sp", "b2_sp",
        "W1_fq", "b1_fq", "W2_fq", "b2_fq")]


def kernel(**inputs):
    import numpy as _np
    import concourse.bacc as _bacc
    from concourse import mybir as _mybir
    from concourse.bass_utils import run_bass_kernel_spmd as _run

    nc = _bacc.Bacc("TRN2", target_bir_lowering=False, num_devices=1)
    arrays, args = {}, {}
    for name in _INS:
        array = _np.ascontiguousarray(inputs[name])
        arrays[f"in_{name}"] = array
        args[name] = nc.dram_tensor(f"in_{name}", array.shape, _mybir.dt.from_np(array.dtype), kind="ExternalInput").ap()
    result = nc.dram_tensor("out_0", (N, D), F32, kind="ExternalOutput").ap()
    gps_layer_kernel(nc, args, result)
    r = _run(nc, [arrays], core_ids=[0])
    return r.results[0]["out_0"]
```

```python
from contextlib import ExitStack

import concourse.bass as bass
from concourse import mybir

F32 = mybir.dt.float32
F32R = mybir.dt.float32r
BF16 = mybir.dt.bfloat16
I32 = mybir.dt.int32
ALU = mybir.AluOpType
ACT = mybir.ActivationFunctionType
AX = mybir.AxisListType

N, D, E = 10000, 512, 10000
P = 128
R = 125
C = 4
G = R * C
NG = N // G
NT = N // R
KC = D // P
SPRAY = 112
AGG_W = 520
AGG_ROWS = 10240
LN_EPS = 1e-5
BN_EPS = 1e-5
ATT_ROWS, ATT_HEADS, ATT_DH, ATT_M = 64, 8, 64, 256
ATT_KEPS = 1e-6
EXPERTS, FF = 8, 64
CAP = 5120
W1_COLS = 2 * EXPERTS * FF + FF + 2 * EXPERTS
EB = 2 * EXPERTS
LAST = FF + EB + 1
FC = 9


def wait(eng, sem, value):
    if isinstance(value, int) and value <= 0:
        return
    eng.wait_ge(sem, value)


def settle(eng, passed):
    eng.sem_inc(passed)


class Chain:

    def __init__(self, eng, sem, base=0):
        self.eng, self.sem, self.base, self.n = eng, sem, base, 0

    def link(self, ins):
        ins.then_inc(self.sem, 1)
        self.n += 1
        self.eng.wait_ge(self.sem, self.base + self.n)


def inverse_root(ch, dve, out, root, var, tmp):
    ch.link(dve.reciprocal(out, root))
    ch.link(dve.tensor_tensor(tmp, out, out, ALU.mult))
    ch.link(dve.tensor_tensor(tmp, tmp, var, ALU.mult))
    ch.link(dve.tensor_scalar(tmp, tmp, -0.5, 1.5, ALU.mult, ALU.add))
    ch.link(dve.tensor_tensor(out, out, tmp, ALU.mult))


def dma_rows(eng, out, in_, sem):
    eng.dma_start(out[0:SPRAY], in_[0:SPRAY]).then_inc(sem, 16)
    eng.dma_start(out[SPRAY:R], in_[SPRAY:R]).then_inc(sem, 16)


def split_product(pe, out, weights, moving, first, last):
    pe.matmul(out, weights[0], moving[1], start=first, stop=False)
    pe.matmul(out, weights[1], moving[0], start=False, stop=False)
    return pe.matmul(out, weights[0], moving[0], start=False, stop=last)


def groups(eng, step):
    step(0, 0, 0)
    step(1, 1, 0)
    with eng.Fori(1, NG // 2 - 1) as r:
        step(r * 2, 0, r)
        step(r * 2 + 1, 1, r)
    step(NG - 2, 0, NG // 2 - 1)
    step(NG - 1, 1, NG // 2 - 1)


def gps_layer_kernel(nc, a, out):
    x_g = a["x"].rearrange("(s c p) d -> s p c d", c=C, p=R)
    out_g = out.rearrange("(s c p) d -> s p c d", c=C, p=R)
    agg = nc.dram_tensor("agg", [AGG_ROWS, AGG_W], F32, kind="Internal").ap()
    agg_g = agg[0:N, :].rearrange("(s c p) d -> s p c d", c=C, p=R)
    u_dram = nc.dram_tensor("u_dram", [N, D], F32, kind="Internal").ap()
    u_g = u_dram.rearrange("(s c p) d -> s p c d", c=C, p=R)

    top = ExitStack()
    with top:
        def sem(name):
            return top.enter_context(nc.semaphore(name))

        def sb(stack, name, shape, dt=F32):
            return stack.enter_context(nc.sbuf_tensor(name, shape, dt))

        bank = [top.enter_context(nc.psum_tensor(f"bank{i}", [P, 512], F32)) for i in range(8)]

        ident = sb(top, "ident", [P, P])
        ones = sb(top, "ones", [P, P])
        row_stat = sb(top, "row_stat", [P, NG, 2, C])
        att_delta = sb(top, "att_delta", [P, D])
        phi_q_hi = sb(top, "phi_q_hi", [P, KC, D], F32R)
        phi_q_lo = sb(top, "phi_q_lo", [P, KC, D], F32R)
        w_proj = sb(top, "w_proj", [P, KC, D])
        kvp = sb(top, "kvp", [P, KC, D])
        ks_bd = sb(top, "ks_bd", [P, KC, P])
        s_const = sem("s_const")
        s_zero = sem("s_zero")
        s_past_dve = sem("s_past_dve")
        s_past_pool = sem("s_past_pool")
        s_past_sp = sem("s_past_sp")

        mid = ExitStack()
        w_v = sb(mid, "w_v", [P, KC, D])
        w_conv = sb(mid, "w_conv", [P, KC, D])
        bn_part = sb(mid, "bn_part", [P, KC, NG * 6])
        ks_acc = sb(mid, "ks_acc", [P, D])
        block_mask = sb(mid, "block_mask", [P, P])

        first = ExitStack()
        phi_k_hi = sb(first, "phi_k_hi", [P, KC, D], F32R)
        phi_k_lo = sb(first, "phi_k_lo", [P, KC, D], F32R)
        src_i = sb(first, "src_i", [P, NT], I32)
        dst_f = sb(first, "dst_f", [P, NT])
        spare = sb(first, "spare", [P, NT])
        dst_rows = sb(first, "dst_rows", [P, E], I32)
        before = sb(first, "before", [P, R])
        s_dst = sem("s_dst")

        with ExitStack() as st:
            w_qk = sb(st, "w_qk", [P, KC, 2 * D])
            proj_bd = sb(st, "proj_bd", [P, KC, P])
            w_turned = sb(st, "w_turned", [P, D])
            idx_in = sb(st, "idx_in", [NT, 2, R], I32)
            idx_f = sb(st, "idx_f", [NT, 2, R])
            zeros = sb(st, "zeros", [P, 1, AGG_W])
            node_no = sb(st, "node_no", [P, 1])
            g_w = [sb(st, f"g_w{n}", [P, KC, D]) for n in "qkvo"]
            proj2 = sb(st, "proj2", [P, 2, P])
            x64 = sb(st, "x64", [ATT_ROWS, D])
            x64_t = sb(st, "x64_t", [P, KC, ATT_ROWS])
            proj_t = sb(st, "proj_t", [P, ATT_M])
            bn6 = sb(st, "bn6", [ATT_ROWS, 6])
            mv = sb(st, "mv", [ATT_ROWS, 2])
            small = sb(st, "small", [ATT_ROWS, 4])
            qk = sb(st, "qk", [ATT_ROWS, 2, D])
            diag = sb(st, "diag", [ATT_ROWS, 2, ATT_HEADS])
            v_aug = sb(st, "v_aug", [ATT_ROWS, ATT_HEADS, ATT_DH + 1])
            qk_t = sb(st, "qk_t", [P, 2, KC, ATT_ROWS])
            feat = sb(st, "feat", [ATT_ROWS, 2, ATT_HEADS, ATT_M])
            sq = feat[:, 0, 0:4, :].rearrange("p a b -> p (a b)").rearrange("p (w d) -> p w d", w=2)
            top_u = sb(st, "top_u", [ATT_ROWS, 2, ATT_HEADS])
            top_k = sb(st, "top_k", [ATT_HEADS, 1])
            top_d = sb(st, "top_d", [ATT_HEADS, ATT_HEADS])
            flat = [g_w[w][:, :, :].rearrange("p c n -> p (c n)") for w in range(2)]
            qf_t = flat[0][:, 0:2 * ATT_HEADS * ATT_ROWS].rearrange("p (a n) -> p a n", n=ATT_ROWS)
            kv_aug = flat[1][:, 0:2 * ATT_HEADS * (ATT_DH + 1)].rearrange("p (a n) -> p a n", n=ATT_DH + 1)
            z_att = sb(st, "z_att", [ATT_ROWS, ATT_HEADS])
            att = sb(st, "att", [ATT_ROWS, D])
            att_t = sb(st, "att_t", [P, KC, ATT_ROWS])
            att_out = sb(st, "att_out", [ATT_ROWS, D])
            delta_sel = sb(st, "delta_sel", [ATT_ROWS, P])

            s_pool = sem("s_pool")
            s_wqk = sem("s_wqk")
            s_bd = sem("s_bd")
            s_wv = sem("s_wv")
            s_idx = sem("s_idx")
            s_att_in = sem("s_att_in")
            s_zeroed = sem("s_zeroed")
            s_turn = sem("s_turn")
            s_turned = sem("s_turned")
            s_fused = sem("s_fused")
            s_fcopy = sem("s_fcopy")
            s_idx_f = sem("s_idx_f")
            s_idx_t = sem("s_idx_t")
            s_att = sem("s_att")
            s_chain = sem("s_chain")
            STAGES = ["var", "std", "norm", "turn", "turned", "qkv", "scaled", "turn2", "turned2", "u",
                      "top", "turn_top", "top_d", "top_b", "arg", "exp", "phi", "kv", "kv_copy", "att",
                      "att_z", "turn3", "turned3", "wo", "wo_copy", "delta", "done"]
            after = {name: i + 1 for i, name in enumerate(STAGES)}

            with nc.Block() as block:
                @block.sync
                def _(sp):
                    sp.dma_start(x64[:, :], a["x"][0:ATT_ROWS, :]).then_inc(s_att_in, 16)
                    for w, name in zip(g_w, ("Wq", "Wk", "Wv", "Wo")):
                        sp.dma_start(w[:, :, :], a["L0_gnn_" + name].rearrange("(c p) n -> p c n", p=P)).then_inc(s_att_in, 16)
                    for twice in range(2):
                        sp.dma_start(proj2[:, :, twice * 64:twice * 64 + 64],
                                     a["L0_gnn_proj"].rearrange("(c p) d -> p c d", p=P)).then_inc(s_att_in, 16)
                    qkv = a["L0_mix_w_qkv"].rearrange("(c p) n -> p c n", p=P)
                    sp.dma_start(w_qk[:, :, :], qkv[:, :, 0:2 * D]).then_inc(s_wqk, 16)
                    sp.dma_start(idx_in[:, 0, :], a["src"].rearrange("(t p) -> t p", p=R)).then_inc(s_idx, 16)
                    sp.dma_start(idx_in[:, 1, :], a["dst"].rearrange("(t p) -> t p", p=R)).then_inc(s_idx, 16)
                    every = a["dst"].rearrange("(a e) -> a e", a=1).broadcast_to([P, E])
                    sp.dma_start(dst_rows[:, :], every).then_inc(s_dst, 16)
                    sp.dma_start(w_v[:, :, :], qkv[:, :, 2 * D:3 * D]).then_inc(s_wv, 16)
                    sp.dma_start(w_proj[:, :, :], a["L0_mix_w_proj"].rearrange("(c p) n -> p c n", p=P)).then_inc(s_wv, 16)
                    sp.dma_start(w_conv[:, :, :], a["L0_gnn_W_conv"].rearrange("(c p) n -> p c n", p=P)).then_inc(s_wv, 16)
                    sp.wait_ge(s_zero, 1)
                    agg_z = agg.rearrange("(p k r) w -> k p r w", p=P, r=5)
                    for k in range(AGG_ROWS // (P * 5)):
                        sp.dma_start(agg_z[k], zeros[:, :, :].broadcast_to([P, 5, AGG_W])).then_inc(s_zeroed, 16)
                    sp.wait_ge(s_zeroed, 16 * (AGG_ROWS // (P * 5)))
                    sp.wait_ge(s_dst, 16)
                    sp.wait_ge(s_wv, 48)

                @block.gpsimd
                def _(pool):
                    ch = Chain(pool, s_pool)
                    ch.link(pool.memset(proj_bd[:, :, :], 0.0))
                    for h in range(8):
                        b = 64 * (h % 2)
                        pool.dma_start(proj_bd[b:b + 64, h // 2, b:b + 64],
                                       a["L0_mix_proj_mat"][h]).then_inc(s_bd, 16)
                    pool.memset(zeros[:, :, :], 0.0).then_inc(s_zero, 1)
                    pool.memset(ones[:, :], 1.0)
                    ch.link(pool.memset(ident[:, :], 0.0))
                    ch.link(pool.affine_select(out=ident[:, :], in_=ident[:, :], compare_op=ALU.not_equal, fill=1.0,
                                               base=0, pattern=[[-1, P]], channel_multiplier=1))
                    ch.link(pool.affine_select(out=before[0:R, :], in_=ones[0:R, 0:R], compare_op=ALU.is_gt, fill=0.0,
                                               base=0, pattern=[[-1, R]], channel_multiplier=1))
                    ch.link(pool.memset(block_mask[:, :], 0.0))
                    pool.memset(block_mask[0:64, 0:64], 1.0)
                    ch.link(pool.memset(block_mask[64:P, 64:P], 1.0))
                    ch.link(pool.iota(node_no[:, :], pattern=[[0, 1]], base=N, channel_multiplier=1,
                                      allow_small_or_imprecise_dtypes=True))
                    ch.link(pool.tensor_copy(delta_sel[:, :], ident[0:ATT_ROWS, :]))
                    ch.link(pool.affine_select(out=delta_sel[:, 0:63], in_=delta_sel[:, 0:63],
                                               compare_op=ALU.not_equal, fill=-1.0, base=-63,
                                               pattern=[[0, 63]], channel_multiplier=1))
                    ch.link(pool.memset(delta_sel[:, 63:64], 0.0))
                    pool.memset(v_aug[:, :, ATT_DH:ATT_DH + 1], 1.0)
                    pool.memset(ks_acc[:, :], 0.0).then_inc(s_const, 1)

                @block.tensor
                def _(pe):
                    pe.wait_ge(s_const, 1)
                    pe.wait_ge(s_att, after["norm"])
                    pe.wait_ge(s_att_in, 16 * 7)
                    for c in range(KC):
                        pe.transpose(bank[0][:, c * 64:c * 64 + 64], x64[:, c * P:c * P + P], ident[0:64, 0:64])
                    for m in range(2):
                        t = pe.transpose(bank[1][:, m * P:m * P + P], proj2[:, m, :], ident[:, :])
                    t.then_inc(s_att, 1)
                    pe.wait_ge(s_att, after["turned"])
                    for w in range(3):
                        for c in range(KC):
                            m = pe.matmul(bank[2 + w][0:64, :], x64_t[:, c, :], g_w[w][:, c, :],
                                          start=(c == 0), stop=(c == KC - 1))
                    m.then_inc(s_att, 1)
                    pe.wait_ge(s_att, after["scaled"])
                    for w in range(2):
                        for c in range(KC):
                            t = pe.transpose(bank[w][:, c * 64:c * 64 + 64], qk[:, w, c * P:c * P + P], ident[0:64, 0:64])
                    t.then_inc(s_att, 1)
                    pe.wait_ge(s_att, after["turned2"])
                    for w in range(2):
                        for h in range(ATT_HEADS):
                            b = 64 * (h % 2)
                            g, at = 2 * (h % 2) + h // 4, h // 2 % 2
                            m = pe.matmul(bank[(2 + 4 * w + g) % 8][0:64, at * ATT_M:(at + 1) * ATT_M],
                                          qk_t[b:b + 64, w, h // 2, :], proj_t[b:b + 64, :], start=True, stop=True)
                    m.then_inc(s_att, 1)
                    pe.wait_ge(s_att, after["top"])
                    pe.transpose(bank[2][0:8, 0:64], top_u[:, 1, :], ident[0:64, 0:64]).then_inc(s_att, 1)
                    pe.wait_ge(s_att, after["top_d"])
                    pe.matmul(bank[2][0:64, 64:72], ones[0:8, 0:64], top_d[:, :], start=True, stop=True).then_inc(s_att, 1)
                    pe.wait_ge(s_att, after["phi"])
                    for hm in range(2 * ATT_HEADS):
                        h, m = hm // 2, hm % 2
                        pe.transpose(bank[2 + hm // 8][:, (hm % 8) * 64:(hm % 8) * 64 + 64],
                                     feat[:, 0, h, m * P:m * P + P], ident[0:64, 0:64])
                    for hm in range(2 * ATT_HEADS):
                        h, m = hm // 2, hm % 2
                        mm = pe.matmul(bank[4 + hm // 4][:, (hm % 4) * 65:(hm % 4) * 65 + 65],
                                       feat[:, 1, h, m * P:m * P + P], v_aug[:, h, :], start=True, stop=True)
                    mm.then_inc(s_att, 1)
                    pe.wait_ge(s_att, after["kv_copy"])
                    for h in range(ATT_HEADS):
                        for m in range(2):
                            mm = pe.matmul(bank[h // 4][0:64, (h % 4) * 65:(h % 4) * 65 + 65],
                                           qf_t[:, 2 * h + m, :], kv_aug[:, 2 * h + m, :], start=(m == 0), stop=(m == 1))
                    mm.then_inc(s_att, 1)
                    pe.wait_ge(s_att, after["att_z"])
                    for c in range(KC):
                        t = pe.transpose(bank[2][:, c * 64:c * 64 + 64], att[:, c * P:c * P + P], ident[0:64, 0:64])
                    t.then_inc(s_att, 1)
                    pe.wait_ge(s_att, after["turned3"])
                    for c in range(KC):
                        m = pe.matmul(bank[3][0:64, :], att_t[:, c, :], g_w[3][:, c, :], start=(c == 0), stop=(c == KC - 1))
                    m.then_inc(s_att, 1)
                    pe.wait_ge(s_att, after["wo_copy"])
                    pe.matmul(bank[4][:, :], delta_sel[:, :], att_out[:, :], start=True, stop=True).then_inc(s_att, 1)
                    pe.wait_ge(s_wqk, 16)
                    pe.wait_ge(s_bd, 16 * 8)
                    for n in range(8):
                        wait(pe, s_turned, n)
                        for c in range(KC):
                            t = pe.transpose(bank[5][:, c * P:c * P + P], w_qk[:, c, n * P:n * P + P], ident[:, :])
                        t.then_inc(s_turn, 1)
                        pe.wait_ge(s_turned, n + 1)
                        wait(pe, s_fcopy, n)
                        for c in range(KC):
                            m = pe.matmul(bank[6][:, c * P:c * P + P], w_turned[:, c * P:c * P + P],
                                          proj_bd[:, n % 4, :], start=True, stop=True)
                        m.then_inc(s_fused, 1)
                    pe.wait_ge(s_idx_f, 1)
                    for k in range(2):
                        t = pe.transpose(bank[7][0:R, k * P:k * P + NT], idx_f[:, k, :], ident[0:NT, 0:NT])
                    t.then_inc(s_idx_t, 1)

                @block.scalar
                def _(act):
                    act.wait_ge(s_att, after["var"])
                    act.activation(small[:, 0:1], mv[:, 1:2], ACT.Sqrt).then_inc(s_att, 1)
                    act.wait_ge(s_att, after["turn"])
                    act.activation(x64_t[:, :, :].rearrange("p c n -> p (c n)"), bank[0][:, 0:256], ACT.Copy)
                    act.activation(proj_t[:, :], bank[1][:, 0:256], ACT.Copy).then_inc(s_att, 1)
                    act.wait_ge(s_att, after["turn2"])
                    for w in range(2):
                        i = act.activation(qk_t[:, w, :, :].rearrange("p c n -> p (c n)"), bank[w][:, 0:256], ACT.Copy)
                    i.then_inc(s_att, 1)
                    act.wait_ge(s_att, after["arg"])
                    act.activation(feat[:, :, :, :].rearrange("p a h m -> p (a h m)"),
                                   feat[:, :, :, :].rearrange("p a h m -> p (a h m)"), ACT.Exp).then_inc(s_att, 1)
                    act.wait_ge(s_att, after["kv"])
                    for k in range(2):
                        act.activation(qf_t[:, 8 * k:8 * k + 8, :].rearrange("p a n -> p (a n)"), bank[2 + k][:, :], ACT.Copy)
                    for k in range(4):
                        i = act.activation(kv_aug[:, 4 * k:4 * k + 4, :].rearrange("p a n -> p (a n)"),
                                           bank[4 + k][:, 0:260], ACT.Copy)
                    i.then_inc(s_att, 1)
                    act.wait_ge(s_att, after["turn3"])
                    act.activation(att_t[:, :, :].rearrange("p c n -> p (c n)"), bank[2][:, 0:256], ACT.Copy).then_inc(s_att, 1)
                    act.wait_ge(s_att, after["wo"])
                    act.activation(att_out[:, :], bank[3][0:64, :], ACT.Copy).then_inc(s_att, 1)
                    act.wait_ge(s_att, after["delta"])
                    act.activation(att_delta[:, :], bank[4][:, :], ACT.Copy).then_inc(s_att, 1)
                    for n in range(8):
                        act.wait_ge(s_turn, n + 1)
                        wait(act, s_fused, n)
                        act.activation(w_turned[:, :], bank[5][:, :], ACT.Copy).then_inc(s_turned, 1)

                @block.vector
                def _(dve):
                    ch = Chain(dve, s_chain)
                    dve.wait_ge(s_att_in, 16 * 7)
                    ch.link(dve.bn_stats(bn6[:, :], x64[:, :]))
                    ch.link(dve.bn_aggr(mv[:, :], bn6[:, :]))
                    dve.tensor_scalar_add(mv[:, 1:2], mv[:, 1:2], LN_EPS).then_inc(s_att, 1)
                    dve.wait_ge(s_att, after["std"])
                    inverse_root(ch, dve, small[:, 1:2], small[:, 0:1], mv[:, 1:2], small[:, 2:3])
                    dve.tensor_scalar(x64[:, :], x64[:, :], mv[:, 0:1], small[:, 1:2], ALU.subtract, ALU.mult).then_inc(s_att, 1)
                    dve.wait_ge(s_const, 1)
                    dve.wait_ge(s_att, after["qkv"])
                    for w in range(2):
                        ch.link(dve.tensor_scalar(qk[:, w, :], bank[2 + w][0:64, :], ATT_DH ** -0.25, None, ALU.mult))
                    dve.tensor_copy(v_aug[:, :, 0:ATT_DH],
                                    bank[4][0:64, :].rearrange("p (h d) -> p h d", h=ATT_HEADS)).then_inc(s_att, 1)
                    for w in range(2):
                        ch.link(dve.tensor_tensor(sq[:, w, :], qk[:, w, :], qk[:, w, :], ALU.mult))
                    ch.link(dve.tensor_reduce(diag[:, :, :], sq[:, :, :].rearrange("p a (h d) -> p a h d", h=ATT_HEADS), AX.X, ALU.add))
                    ch.link(dve.tensor_scalar(diag[:, :, :], diag[:, :, :], 0.5, None, ALU.mult))
                    dve.wait_ge(s_att, after["u"])
                    for w in range(2):
                        for g in range(4):
                            u = bank[(2 + 4 * w + g) % 8][0:64, :].rearrange("p (h m) -> p h m", h=2)
                            h = 4 * (g % 2) + g // 2
                            i = dve.tensor_reduce(top_u[:, w, h:h + 3:2], u, AX.X, ALU.max)
                    ch.link(i)
                    for w in range(2):
                        for g in range(4):
                            u = bank[(2 + 4 * w + g) % 8][0:64, :].rearrange("p (h m) -> p h m", h=2)
                            h = 4 * (g % 2) + g // 2
                            i = dve.tensor_tensor(feat[:, w, h:h + 3:2, :], u,
                                                  diag[:, w, h:h + 3:2, None].broadcast_to([ATT_ROWS, 2, ATT_M]), ALU.subtract)
                    i.then_inc(s_att, 1)
                    dve.wait_ge(s_att, after["turn_top"])
                    ch.link(dve.tensor_reduce(top_k[:, :], bank[2][0:8, 0:64], AX.X, ALU.max))
                    dve.tensor_scalar(top_d[:, :], ident[0:8, 0:8], top_k[:, 0:1], None, ALU.mult).then_inc(s_att, 1)
                    dve.wait_ge(s_att, after["top_b"])
                    ch.link(dve.tensor_copy(top_u[:, 1, :], bank[2][0:64, 64:72]))
                    for w in range(2):
                        i = dve.tensor_tensor(feat[:, w, :, :], feat[:, w, :, :],
                                              top_u[:, w, :, None].broadcast_to([ATT_ROWS, ATT_HEADS, ATT_M]), ALU.subtract)
                    i.then_inc(s_att, 1)
                    dve.wait_ge(s_att, after["exp"])
                    dve.tensor_scalar(feat[:, :, :, :].rearrange("p a h m -> p (a h m)"),
                                      feat[:, :, :, :].rearrange("p a h m -> p (a h m)"),
                                      ATT_M ** -0.5, ATT_KEPS, ALU.mult, ALU.add).then_inc(s_att, 1)
                    dve.wait_ge(s_att, after["att"])
                    for k in range(2):
                        num = bank[k][0:64, 0:260].rearrange("p (h d) -> p h d", h=4)
                        ch.link(dve.tensor_scalar(z_att[:, 4 * k:4 * k + 4, None], num[:, :, 64:65], ATT_KEPS, None, ALU.add))
                    ch.link(dve.reciprocal(z_att[:, :], z_att[:, :]))
                    for k in range(2):
                        num = bank[k][0:64, 0:260].rearrange("p (h d) -> p h d", h=4)
                        i = dve.tensor_tensor(att[:, 256 * k:256 * k + 256].rearrange("p (h d) -> p h d", h=4),
                                              num[:, :, 0:64], z_att[:, 4 * k:4 * k + 4, None].broadcast_to([ATT_ROWS, 4, 64]), ALU.mult)
                    i.then_inc(s_att, 1)
                    for n in range(8):
                        dve.wait_ge(s_fused, n + 1)
                        fused = bank[6][:, :].rearrange("p (c f) -> p c f", c=KC)
                        at = slice(n % 4 * P, n % 4 * P + P)
                        high, low = ((phi_q_hi, phi_q_lo), (phi_k_hi, phi_k_lo))[n // 4]
                        ch.link(dve.tensor_copy(high[:, :, at], fused))
                        dve.tensor_tensor(low[:, :, at], fused, high[:, :, at].bitcast(F32), ALU.subtract).then_inc(s_fcopy, 1)
                    dve.wait_ge(s_idx, 32)
                    dve.tensor_copy(idx_f[:, :, :], idx_in[:, :, :]).then_inc(s_idx_f, 1)
                    dve.wait_ge(s_idx_t, 1)
                    ch.link(dve.tensor_copy(src_i[0:R, :], bank[7][0:R, 0:NT]))
                    ch.link(dve.tensor_copy(dst_f[0:R, :], bank[7][0:R, P:P + NT]))
                    ch.link(dve.tensor_scalar(spare[0:R, :], dst_f[0:R, :], -1.0, node_no[0:R, 0:1], ALU.mult, ALU.add))
        TURN = ((0, 6), (3, 4), (2, 5), (1, 7))
        with ExitStack() as st:
            xn = [sb(st, f"xn{i}", [P, C, D]) for i in range(2)]
            xn_hi = sb(st, "xn_hi", [P, C, D], F32R)
            xn_lo = sb(st, "xn_lo", [P, C, D], F32R)
            xt_hi = sb(st, "xt_hi", [P, KC, G], F32R)
            xt_lo = sb(st, "xt_lo", [P, KC, G], F32R)
            gat = [sb(st, f"gat{i}", [P, C, D]) for i in range(2)]
            src_now = [sb(st, f"src_now{i}", [P, C], I32) for i in range(2)]
            dst_now = [sb(st, f"dst_now{i}", [P, C], I32) for i in range(2)]
            same = [sb(st, f"same{i}", [P, C, R]) for i in range(2)]
            count = [sb(st, f"count{i}", [P, C]) for i in range(2)]
            repeat = sb(st, "repeat", [P, C])
            scratch = sb(st, "scratch", [P, R])
            sums = sb(st, "sums", [P, C, AGG_W])
            ph = sb(st, "ph", [P, 2, D])
            ph_hi = sb(st, "ph_hi", [P, 2, D], F32R)
            ph_lo = sb(st, "ph_lo", [P, 2, D], F32R)
            bn = sb(st, "bn", [P, 2, C, 6])
            st_mv = sb(st, "st_mv", [P, 2, C, 2])
            st_std = sb(st, "st_std", [P, 2, C])
            st_tmp = sb(st, "st_tmp", [P, 2, C])
            st_rstd = sb(st, "st_rstd", [P, 2, C])
            st_shift = sb(st, "st_shift", [P, C])

            s_x = [sem(f"s_x{i}") for i in range(2)]
            s_gat = [sem(f"s_gat{i}") for i in range(2)]
            s_src = sem("s_src")
            s_var = sem("s_var")
            s_std = sem("s_std")
            s_xn = sem("s_xn")
            s_gr = sem("s_gr")
            s_gn = sem("s_gn")
            s_xh = sem("s_xh")
            s_xl = sem("s_xl1")
            s_t = sem("s_t")
            s_th = sem("s_th")
            s_tl = sem("s_tl")
            s_bn = sem("s_bn")
            s_k = sem("s_k")
            s_low = sem("s_low")
            s_exp = sem("s_exp")
            s_ph = sem("s_ph")
            s_g = sem("s_g")
            s_acc = sem("s_acc")
            s_ph_hi = sem("s_ph_hi")
            s_ph_lo = sem("s_ph_lo")
            s_e = sem("s_e")
            s_ec = sem("s_ec")
            s_scat = sem("s_scat")
            s_ch = sem("s_ch1")
            CHAIN = 26

            with nc.Block() as block:
                @block.sync
                def _(sp):
                    def load(s, par, half):
                        wait(sp, s_t, (s - 1) * KC if not isinstance(s, int) or s >= 2 else 0)
                        settle(sp, s_past_sp)
                        wait(sp, s_xl, (s - 1) * C if not isinstance(s, int) or s >= 2 else 0)
                        dma_rows(sp, xn[par][0:R], x_g[s], s_x[par])
                    groups(sp, load)

                @block.gpsimd
                def _(pool):
                    pool.memset(sums[:, :, D + 1:AGG_W], 0.0).then_inc(s_ch, 1)

                    def gather(s, par):
                        pool.wait_ge(s_src, s + 1)
                        wait(pool, s_e, (s - 1) * C if not isinstance(s, int) or s >= 2 else 0)
                        settle(pool, s_past_pool)
                        for c in range(C):
                            pool.indirect_dma_start(
                                out=gat[par][0:R, c, :], out_offset=None, in_=a["x"],
                                in_offset=bass.IndirectOffsetOnAxis(ap=src_now[par][0:R, c:c + 1], axis=0),
                            ).then_inc(s_gat[par], 16)

                    def scatter(s, par, c):
                        pool.wait_ge(s_ec, s * C + c + 1)
                        wait(pool, s_scat, (s * C + c) * 16)
                        settle(pool, s_past_pool)
                        pool.indirect_dma_start(
                            out=agg, in_=sums[0:R, c, :], in_offset=None, compute_op=ALU.add,
                            out_offset=bass.IndirectOffsetOnAxis(ap=dst_now[par][0:R, c:c + 1], axis=0),
                        ).then_inc(s_scat, 16)

                    def x_low(s, par, c):
                        pool.wait_ge(s_xh, s * C + c + 1)
                        pool.tensor_tensor(xn_lo[0:R, c, :], xn[par][0:R, c, :], xn_hi[0:R, c, :].bitcast(F32),
                                           ALU.subtract).then_inc(s_xl, 1)

                    def phi_low(s, j):
                        pool.wait_ge(s_ph_hi, s * C + j + 1)
                        pool.tensor_tensor(ph_lo[0:R, j % 2, :], ph[0:R, j % 2, :], ph_hi[0:R, j % 2, :].bitcast(F32),
                                           ALU.subtract).then_inc(s_ph_lo, 1)
                        wait(pool, s_acc, s * C + j)
                        pool.tensor_tensor(ks_acc[0:R, :], ks_acc[0:R, :], ph[0:R, j % 2, :], ALU.add).then_inc(s_acc, 1)

                    def step(s, par, half):
                        gather(s, par)
                        later = not isinstance(s, int) or s >= 1
                        for j in range(C):
                            if j < 2:
                                x_low(s, par, 2 * j)
                                x_low(s, par, 2 * j + 1)
                            if later and j >= 2:
                                scatter(s - 1, 1 - par, j - 2)
                            phi_low(s, j)
                        if later:
                            scatter(s - 1, 1 - par, 2)
                            scatter(s - 1, 1 - par, 3)
                    groups(pool, step)
                    for c in range(C):
                        scatter(NG - 1, (NG - 1) % 2, c)
                    pool.wait_ge(s_scat, 16 * NT)

                @block.tensor
                def _(pe):
                    def turn(s, par, n):
                        c, b = TURN[n]
                        if n == 0:
                            pe.wait_ge(s_xn, (s + 1) * C)
                            wait(pe, s_ph, s * C - 1)
                        if n == 2:
                            wait(pe, s_ec, (s - 1) * C)
                        if n == 3:
                            wait(pe, s_ph, s * C)
                        for j in range(C):
                            t = pe.transpose(bank[b][:, j * R:j * R + R],
                                             xn[par][0:R, j, c * P:c * P + P], ident[0:R, 0:R])
                        t.then_inc(s_t, 1)

                    def keys(s, j):
                        if j < 2:
                            pe.wait_ge(s_bn, s * KC + (1, KC)[j])
                        else:
                            pe.wait_ge(s_ph, s * C + j - 1)
                        for n, (c, _) in enumerate(TURN):
                            if j == 0:
                                pe.wait_ge(s_tl, s * KC + n + 1)
                            at = slice(j * R, j * R + R)
                            m = split_product(pe, bank[6 + j % 2][0:R, :], (xt_hi[:, c, at], xt_lo[:, c, at]),
                                              (phi_k_hi[:, c, :], phi_k_lo[:, c, :]), n == 0, n == KC - 1)
                        m.then_inc(s_k, 1)

                    def edges(s, par, j):
                        if j == 0:
                            pe.wait_ge(s_gn, s + 1)
                            wait(pe, s_bn, min(s + 2, NG) * KC - 1 if isinstance(s, int) else (s + 2) * KC - 1)
                        wait(pe, s_ec, s * C + j)
                        pe.matmul(bank[5][0:R, :], same[par][0:R, j, :], gat[par][0:R, j, :],
                                  start=True, stop=True).then_inc(s_e, 1)

                    def products(s, j):
                        pe.wait_ge(s_xl, s * C + j + 1)
                        pe.wait_ge(s_ph_lo, s * C + j + 1)
                        for f in range(KC):
                            at = slice(f * P, f * P + P)
                            m = split_product(pe, bank[f][:, :], (ph_hi[0:R, j % 2, at], ph_lo[0:R, j % 2, at]),
                                              (xn_hi[0:R, j, :], xn_lo[0:R, j, :]),
                                              isinstance(s, int) and s == 0 and j == 0,
                                              isinstance(s, int) and s == NG - 1 and j == C - 1)
                        m.then_inc(s_g, 1)

                    def step(s, par, half):
                        more = not isinstance(s, int) or s < NG - 1
                        later = not isinstance(s, int) or s >= 1
                        for j in range(C):
                            keys(s, j)
                            if j >= 2:
                                products(s, j - 2)
                            if later and j >= 2:
                                edges(s - 1, 1 - par, j - 2)
                        if more:
                            turn(s + 1, 1 - par, 0)
                        if later:
                            edges(s - 1, 1 - par, 2)
                        if more:
                            turn(s + 1, 1 - par, 1)
                        products(s, 2)
                        if later:
                            edges(s - 1, 1 - par, 3)
                        if more:
                            turn(s + 1, 1 - par, 2)
                            turn(s + 1, 1 - par, 3)
                        products(s, 3)
                    for n in range(KC):
                        turn(0, 0, n)
                    groups(pe, step)
                    for j in range(C):
                        edges(NG - 1, (NG - 1) % 2, j)

                @block.scalar
                def _(act):
                    def root_x(s):
                        act.wait_ge(s_var, 2 * s + 2 if not isinstance(s, int) or s >= 0 else 1)
                        act.activation(st_std[0:R, 0, :], st_mv[0:R, 0, :, 1], ACT.Sqrt).then_inc(s_std, 1)

                    def root_g(s):
                        act.wait_ge(s_var, 2 * s + 3 if not isinstance(s, int) or s < NG - 1 else 2 * NG)
                        act.activation(st_std[0:R, 1, :], st_mv[0:R, 1, :, 1], ACT.Sqrt).then_inc(s_std, 1)

                    def exp(s, j):
                        act.wait_ge(s_low, s * C + j + 1)
                        act.activation(ph[0:R, j % 2, :], ph[0:R, j % 2, :], ACT.Exp).then_inc(s_exp, 1)

                    def phi_high(s, j):
                        act.wait_ge(s_ph, s * C + j + 1)
                        wait(act, s_g, s * C + j - 1)
                        act.activation(ph_hi[0:R, j % 2, :], ph[0:R, j % 2, :], ACT.Copy).then_inc(s_ph_hi, 1)

                    def x_high(s, par, c):
                        act.wait_ge(s_xn, s * C + c + 1)
                        wait(act, s_g, s * C)
                        act.activation(xn_hi[0:R, c, :], xn[par][0:R, c, :], ACT.Copy).then_inc(s_xh, 1)

                    def copy_sums(s, par, j):
                        act.wait_ge(s_e, s * C + j + 1)
                        wait(act, s_scat, 16 * (s * C + j - C + 1))
                        act.activation(sums[0:R, j, D:D + 1], count[par][0:R, j:j + 1], ACT.Copy)
                        act.activation(sums[0:R, j, 0:D], bank[5][0:R, :], ACT.Copy).then_inc(s_ec, 1)

                    def turned_high(s, which):
                        for n in which:
                            c, b = TURN[n]
                            act.wait_ge(s_t, s * KC + n + 1)
                            if n == 0:
                                wait(act, s_k, s * C)
                            act.activation(xt_hi[:, c, :], bank[b][:, 0:G], ACT.Copy).then_inc(s_th, 1)

                    act.wait_ge(s_ch, 1)
                    root_x(-1)
                    turned_high(0, range(KC))

                    def normalise_gathered(s, par):
                        act.wait_ge(s_gr, s + 1)
                        for c in range(C):
                            i = act.activation(gat[par][0:R, c, :], gat[par][0:R, c, :], ACT.Identity,
                                               bias=st_shift[0:R, c:c + 1], scale=st_rstd[0:R, 1, c:c + 1])
                        i.then_inc(s_gn, 1)

                    def step(s, par, half):
                        later = not isinstance(s, int) or s >= 1
                        for j in range(C):
                            if j < 2:
                                x_high(s, par, 2 * j)
                                x_high(s, par, 2 * j + 1)
                            if later and j >= 2:
                                copy_sums(s - 1, 1 - par, j - 2)
                            if j == 1 and (not isinstance(s, int) or s < NG - 1):
                                root_x(s)
                            exp(s, j)
                            phi_high(s, j)
                            if j == 0 and later:
                                normalise_gathered(s - 1, 1 - par)
                        more = not isinstance(s, int) or s < NG - 1
                        if more:
                            turned_high(s + 1, range(0, 1))
                        if later:
                            copy_sums(s - 1, 1 - par, 2)
                        if more:
                            turned_high(s + 1, range(1, 2))
                        if later:
                            copy_sums(s - 1, 1 - par, 3)
                        if more:
                            turned_high(s + 1, range(2, KC))
                        root_g(s)

                    groups(act, step)
                    normalise_gathered(NG - 1, (NG - 1) % 2)
                    for j in range(C):
                        copy_sums(NG - 1, (NG - 1) % 2, j)

                @block.vector
                def _(dve):
                    def variances(ch, s, rows, k):
                        for c in range(C):
                            i = dve.bn_stats(bn[0:R, k, c, :], rows[0:R, c, :])
                        ch.link(i)
                        settle(dve, s_past_dve)
                        for c in range(C):
                            i = dve.bn_aggr(st_mv[0:R, k, c, :], bn[0:R, k, c, :])
                        ch.link(i)
                        dve.tensor_scalar(st_mv[0:R, k, :, 1], st_mv[0:R, k, :, 1], LN_EPS, None, ALU.add).then_inc(s_var, 1)

                    def factors(ch, k):
                        inverse_root(ch, dve, st_rstd[0:R, k, :], st_std[0:R, k, :], st_mv[0:R, k, :, 1], st_tmp[0:R, k, :])

                    def x_variances(ch, s, par, half):
                        dve.wait_ge(s_x[par], 32 * (half + 1))
                        variances(ch, s, xn[par], 0)

                    def x_normalise(ch, s, par):
                        dve.wait_ge(s_std, 2 * s if not isinstance(s, int) or s > 0 else 1)
                        factors(ch, 0)
                        for c in range(C):
                            dve.tensor_scalar(xn[par][0:R, c, :], xn[par][0:R, c, :], st_mv[0:R, 0, c, 0:1],
                                              st_rstd[0:R, 0, c:c + 1], ALU.subtract, ALU.mult).then_inc(s_xn, 1)
                        ch.link(dve.tensor_copy(row_stat[0:R, s, 0, :], st_mv[0:R, 0, :, 0]))
                        ch.link(dve.tensor_copy(row_stat[0:R, s, 1, :], st_rstd[0:R, 0, :]))

                    def sources(s, par, half):
                        wait(dve, s_gat[par], 64 * half)
                        dve.tensor_copy(src_now[par][0:R, :], src_i[0:R, bass.ds(s * C, C)]).then_inc(s_src, 1)

                    def phi(s, j):
                        dve.wait_ge(s_k, s * C + j + 1)
                        wait(dve, s_acc, s * C + j - 1)
                        dve.tensor_scalar(ph[0:R, j % 2, :], bank[6 + j % 2][0:R, :], 0.0, None, ALU.min).then_inc(s_low, 1)
                        dve.wait_ge(s_exp, s * C + j + 1)
                        dve.scalar_tensor_tensor(ph[0:R, j % 2, :], bank[6 + j % 2][0:R, :], 0.0, ph[0:R, j % 2, :],
                                                 ALU.max, ALU.add).then_inc(s_ph, 1)

                    def turned_low(s, which):
                        for n in which:
                            c, b = TURN[n]
                            dve.wait_ge(s_th, s * KC + n + 1)
                            if n == 0:
                                wait(dve, s_k, s * C)
                            dve.tensor_tensor(xt_lo[:, c, :], bank[b][:, 0:G], xt_hi[:, c, :].bitcast(F32), ALU.subtract).then_inc(s_tl, 1)
                            dve.bn_stats(bn_part[:, c, bass.ds(s * 6, 6)], bank[b][:, 0:G]).then_inc(s_bn, 1)

                    def repeats(ch, s, par, c):
                        if c == 0:
                            wait(dve, s_e, (s - 1) * C if not isinstance(s, int) or s >= 2 else 0)
                        dst_c = dst_f[0:R, bass.ds(s * C + c, 1)]
                        ch.link(dve.tensor_scalar(same[par][0:R, c, :], dst_rows[0:R, bass.ds(s * G + c * R, R)], dst_c, None,
                                                  ALU.is_equal, ALU.add, accum_out=count[par][0:R, c:c + 1]))
                        ch.link(dve.tensor_tensor_reduce(scratch[0:R, :], same[par][0:R, c, :], before[0:R, :], 1.0, 0.0,
                                                         ALU.mult, ALU.add, repeat[0:R, c:c + 1]))

                    def destinations(ch, s, par):
                        wait(dve, s_scat, 16 * (s - 1) * C if not isinstance(s, int) or s >= 2 else 0)
                        ch.link(dve.scalar_tensor_tensor(repeat[0:R, :], repeat[0:R, :], 0.0, spare[0:R, bass.ds(s * C, C)],
                                                         ALU.is_gt, ALU.mult))
                        ch.link(dve.tensor_tensor(dst_now[par][0:R, :], repeat[0:R, :], dst_f[0:R, bass.ds(s * C, C)], ALU.add))

                    def gathered_factors(ch, s):
                        dve.wait_ge(s_std, 2 * s + 3 if not isinstance(s, int) or s < NG - 1 else 2 * NG)
                        wait(dve, s_gn, s)
                        factors(ch, 1)
                        dve.scalar_tensor_tensor(st_shift[0:R, :], st_mv[0:R, 1, :, 0], -1.0, st_rstd[0:R, 1, :],
                                                 ALU.mult, ALU.mult).then_inc(s_gr, 1)

                    def step(s, par, half):
                        first = isinstance(s, int) and s == 0
                        ch = Chain(dve, s_ch, 1 + FIRST + (0 if first else s * CHAIN - 5))
                        more = not isinstance(s, int) or s < NG - 1
                        for j in range(C):
                            phi(s, j)
                            if j == 0 and not first:
                                gathered_factors(ch, s - 1)
                            repeats(ch, s, par, j)
                            if j == 0 and more:
                                sources(s + 1, 1 - par, half + par)
                                x_variances(ch, s + 1, 1 - par, half + par)
                            if j == 1 and more:
                                x_normalise(ch, s + 1, 1 - par)
                            if j == 3:
                                destinations(ch, s, par)
                                if more:
                                    turned_low(s + 1, range(KC // 2))
                                dve.wait_ge(s_gat[par], 64 * (half + 1))
                                variances(ch, s, gat[par], 1)
                                if more:
                                    turned_low(s + 1, range(KC // 2, KC))
                                if not more:
                                    gathered_factors(ch, s)
                        assert not more or ch.n == (CHAIN - 5 if first else CHAIN), ch.n

                    FIRST = 9
                    ch = Chain(dve, s_ch, 1)
                    dve.wait_ge(s_ch, 1)
                    sources(0, 0, 0)
                    x_variances(ch, 0, 0, 0)
                    x_normalise(ch, 0, 0)
                    assert ch.n == FIRST
                    turned_low(0, range(KC))
                    groups(dve, step)
        first.close()

        ffn = ExitStack()
        w1_hi = sb(ffn, "w1_hi", [P, KC, W1_COLS], F32R)
        w2_hi = sb(ffn, "w2_hi", [P, FC, D], F32R)
        w1_lo = sb(ffn, "w1_lo", [P, KC, W1_COLS], F32R)
        w2_lo = sb(ffn, "w2_lo", [P, FC, D], F32R)
        b1 = sb(ffn, "b1", [P, FC])
        scale2 = sb(ffn, "scale2", [P, D])
        shift2 = sb(ffn, "shift2", [P, D])
        s_ffn = sem("s_ffn")
        FFN_DMAS = 22
        conv_rows = sb(ffn, "conv_rows", [2, D])
        conv_hi, conv_lo = w2_lo[:, 0:KC, :], w2_lo[:, KC:2 * KC, :]
        mean_hi, mean_lo = w2_hi[:, 0:KC, :], w2_hi[:, KC:2 * KC, :]
        rows_hi, rows_lo = w2_hi[0:2, 2 * KC, :], w2_lo[0:2, 2 * KC, :]
        sums = ExitStack()
        squares, u_acc, q_acc = w_v[:, 0:2, :], w_v[:, 2, :], w_v[:, 3, :]
        w1 = sb(sums, "w1", [P, KC, W1_COLS])
        w2 = sb(sums, "w2", [P, FC, D])

        def load_experts(eng):
            n = 0
            for k, bank_name in enumerate(("sp", "fq")):
                for c in range(KC):
                    to = w1[:, c, k * 512:k * 512 + 512].rearrange("p (e f) -> p e f", e=EXPERTS)
                    eng.dma_start(to, a["L0_ffn_W1_" + bank_name][:, c * P:c * P + P, :].rearrange("e p f -> p e f")).then_inc(s_ffn, 16)
                    n += 1
                two = a["L0_ffn_W2_" + bank_name].rearrange("e f d -> (e f) d").rearrange("(c p) d -> p c d", p=P)
                eng.dma_start(w2[:, 4 * k:4 * k + 4, :], two).then_inc(s_ffn, 16)
                eng.dma_start(w2[64 + 8 * k:72 + 8 * k, 8, :], a["L0_ffn_b2_" + bank_name]).then_inc(s_ffn, 16)
                eng.dma_start(w1[:, :, 1088 + 8 * k:1096 + 8 * k], a["L0_ffn_Wr_" + bank_name].rearrange("(c p) e -> p c e", p=P)).then_inc(s_ffn, 16)
                eng.dma_start(b1[64 + 8 * k:72 + 8 * k, 8:9], a["L0_ffn_br_" + bank_name].rearrange("(e a) -> e a", a=1), allow_slow_non_contiguous=True).then_inc(s_ffn, 16)
                eng.dma_start(b1[:, 4 * k:4 * k + 4], a["L0_ffn_b1_" + bank_name].rearrange("e f -> (e f)").rearrange("(c p) -> p c", p=P), allow_slow_non_contiguous=True).then_inc(s_ffn, 16)
                n += 5
            eng.dma_start(w1[:, :, 1024:1088], a["L0_ffn_Ws1"].rearrange("(c p) f -> p c f", p=P)).then_inc(s_ffn, 16)
            eng.dma_start(w2[0:64, 8, :], a["L0_ffn_Ws2"]).then_inc(s_ffn, 16)
            eng.dma_start(w2[80:81, 8, :], a["L0_ffn_bs2"].rearrange("(a d) -> a d", a=1)).then_inc(s_ffn, 16)
            eng.dma_start(b1[0:64, 8:9], a["L0_ffn_bs1"].rearrange("(f a) -> f a", a=1), allow_slow_non_contiguous=True).then_inc(s_ffn, 16)
            assert n + 4 == FFN_DMAS

        with ExitStack() as st:
            g_all = sb(st, "g_all", [P, KC, D])
            g_t = sb(st, "g_t", [P, KC, D])
            kv_bd = sb(st, "kv_bd", [P, KC, P])
            gamma = sb(st, "gamma", [P, KC])
            beta = sb(st, "beta", [P, KC])
            col = sb(st, "col", [P, KC, 2])
            col_std = sb(st, "col_std", [P, KC])
            col_tmp = sb(st, "col_tmp", [P, KC])
            scale1 = sb(st, "scale1", [P, KC])
            shift1 = sb(st, "shift1", [P, KC])

            s_mid_in = sem("s_mid_in")
            s_col_var = sem("s_col_var")
            s_col_std = sem("s_col_std")
            s_shift = sem("s_shift")
            s_tw = sem("s_tw")
            s_kv = sem("s_kv")
            s_ch = sem("s_ch2")
            STAGES2 = ["g_copy", "turn_g", "gt", "kv", "bd", "kvp", "done"]
            now = {name: i + 1 for i, name in enumerate(STAGES2)}

            with nc.Block() as block:
                @block.sync
                def _(sp):
                    sp.dma_start(gamma[:, :], a["L0_gnn_norm1_g"].rearrange("(c p) -> p c", p=P), allow_slow_non_contiguous=True).then_inc(s_mid_in, 16)
                    sp.dma_start(beta[:, :], a["L0_gnn_norm1_b"].rearrange("(c p) -> p c", p=P), allow_slow_non_contiguous=True).then_inc(s_mid_in, 16)
                    sp.dma_start(conv_rows[1:2, :], a["L0_gnn_b_conv"].rearrange("(a d) -> a d", a=1)).then_inc(s_mid_in, 16)
                    load_experts(sp)

                @block.scalar
                def _(act):
                    for f in range(KC):
                        i = act.activation(g_all[:, f, :], bank[f][:, :], ACT.Copy)
                    i.then_inc(s_kv, 1)
                    act.wait_ge(s_col_var, 1)
                    act.activation(col_std[:, :], col[:, :, 1], ACT.Sqrt).then_inc(s_col_std, 1)
                    act.wait_ge(s_kv, now["turn_g"])
                    for c in range(KC):
                        i = act.activation(g_t[:, c, :], bank[4 + c][:, :], ACT.Copy)
                    i.then_inc(s_kv, 1)
                    act.wait_ge(s_kv, now["kvp"])
                    for f in range(KC):
                        i = act.activation(kvp[:, f, :], bank[f][:, :], ACT.Copy)
                    i.then_inc(s_kv, 1)

                @block.tensor
                def _(pe):
                    pe.wait_ge(s_kv, now["g_copy"])
                    for c in range(KC):
                        for f in range(KC):
                            t = pe.transpose(bank[4 + c][:, f * P:f * P + P], g_all[:, f, c * P:c * P + P], ident[:, :])
                    t.then_inc(s_kv, 1)
                    pe.wait_ge(s_kv, now["gt"])
                    for h in range(KC):
                        for c in range(KC):
                            m = pe.matmul(bank[0][:, h * P:h * P + P], w_v[:, c, h * P:h * P + P],
                                          g_t[:, c, h * P:h * P + P], start=(c == 0), stop=(c == KC - 1))
                    m.then_inc(s_kv, 1)
                    for f in range(KC):
                        m = pe.matmul(bank[4][:, f:f + 1], ks_acc[0:R, f * P:f * P + P], ones[0:R, 0:1], start=True, stop=True)
                    pe.wait_ge(s_shift, 1)
                    pe.wait_ge(s_mid_in, 48)
                    for c in range(KC):
                        m = pe.matmul(bank[5][0:1, :], shift1[:, c:c + 1], w_conv[:, c, :], start=(c == 0), stop=(c == KC - 1))
                    m.then_inc(s_tw, 1)
                    pe.wait_ge(s_kv, now["bd"])
                    for h in range(KC):
                        m = pe.matmul(bank[h][:, :], kv_bd[:, h, :], w_proj[:, h, :], start=True, stop=True)
                    m.then_inc(s_kv, 1)

                @block.vector
                def _(dve):
                    ch = Chain(dve, s_ch)
                    for c in range(KC):
                        i = dve.bn_aggr(col[:, c, :], bn_part[:, c, :])
                    ch.link(i)
                    dve.tensor_scalar(col[:, :, 1], col[:, :, 1], BN_EPS, None, ALU.add).then_inc(s_col_var, 1)
                    dve.wait_ge(s_col_std, 1)
                    inverse_root(ch, dve, scale1[:, :], col_std[:, :], col[:, :, 1], col_tmp[:, :])
                    dve.wait_ge(s_mid_in, 48)
                    ch.link(dve.tensor_tensor(scale1[:, :], scale1[:, :], gamma[:, :], ALU.mult))
                    ch.link(dve.tensor_tensor(shift1[:, :], col[:, :, 0], scale1[:, :], ALU.mult))
                    dve.tensor_tensor(shift1[:, :], beta[:, :], shift1[:, :], ALU.subtract).then_inc(s_shift, 1)
                    dve.wait_ge(s_kv, now["kv"])
                    dve.tensor_tensor(kv_bd[:, :, :], bank[0][:, :].rearrange("p (h f) -> p h f", h=KC),
                                      block_mask[:, None, :].broadcast_to([P, KC, P]), ALU.mult).then_inc(s_kv, 1)
                    dve.wait_ge(s_tw, 1)
                    ch.link(dve.tensor_copy(conv_rows[0:1, :], bank[5][0:1, :]))
                    ch.link(dve.tensor_copy(rows_hi, conv_rows[:, :]))
                    dve.tensor_tensor(rows_lo, conv_rows[:, :], rows_hi.bitcast(F32), ALU.subtract)
                    for f in range(KC):
                        dve.tensor_scalar(ks_bd[:, f, :], block_mask[:, :], bank[4][:, f:f + 1], None, ALU.mult)
                        i = dve.tensor_scalar(conv_hi[:, f, :], w_conv[:, f, :], scale1[:, f:f + 1], None, ALU.mult)
                    ch.link(i)
                    for f in range(KC):
                        dve.scalar_tensor_tensor(conv_lo[:, f, :], w_conv[:, f, :], scale1[:, f:f + 1],
                                                 conv_hi[:, f, :].bitcast(F32), ALU.mult, ALU.subtract)

        with ExitStack() as st:
            u = [sb(st, f"u{i}", [P, C, D]) for i in range(2)]
            mean = [sb(st, f"mean{i}", [P, C, AGG_W]) for i in range(2)]
            deg_t = sb(st, "deg_t", [2, G], F32R)
            deg = sb(st, "deg", [P, 2, C])
            now_stat = sb(st, "now_stat", [P, 2, C])

            s_agg = [sem(f"s_agg{i}") for i in range(2)]
            s_in = [sem(f"s_in{i}") for i in range(2)]
            s_mean = sem("s_mean")
            s_yn = sem("s_yn")
            s_mt = sem("s_mt")
            s_mc = sem("s_mc")
            s_ml = sem("s_ml")
            s_conv = sem("s_conv")
            s_u = sem("s_u")
            s_sq = sem("s_sq")
            s_q_acc = sem("s_q_acc")
            s_ust = [sem(f"s_ust{i}") for i in range(2)]
            s_ch = sem("s_ch3")
            s_pc = sem("s_pc3")
            FIRST3, CHAIN3 = 5, 8
            s_wh = sem("s_wh")

            def pieces(s, j):
                return range(j, j + 1) if isinstance(s, int) and s == NG - 1 else range(0)

            with nc.Block() as block:
                @block.sync
                def _(sp):
                    def load(s, par, half):
                        wait(sp, s_mt, (s - 1) * (KC + 1) if not isinstance(s, int) or s >= 2 else 0)
                        dma_rows(sp, mean[par][0:R], agg_g[s], s_agg[par])
                        wait(sp, s_ust[par], 32 * half)
                        settle(sp, s_past_sp)
                        wait(sp, s_sq, (s - 1) * C if not isinstance(s, int) or s >= 2 else 0)
                        settle(sp, s_past_sp)
                        wait(sp, s_ch, FIRST3 + (s - 1) * CHAIN3 if not isinstance(s, int) or s >= 2 else 0)
                        dma_rows(sp, u[par][0:R], x_g[s], s_in[par])

                    def store(s, par):
                        sp.wait_ge(s_u, (s + 1) * C)
                        dma_rows(sp, u_g[s], u[par][0:R], s_ust[par])

                    def step(s, par, half):
                        if not isinstance(s, int) or s < NG - 1:
                            load(s + 1, 1 - par, half + par)
                        store(s, par)
                    load(0, 0, 0)
                    groups(sp, step)
                    for i in range(2):
                        sp.wait_ge(s_ust[i], 32 * (NG // 2))
                    sp.wait_ge(s_ffn, 16 * FFN_DMAS)

                @block.gpsimd
                def _(pool):
                    pool.memset(q_acc[:, :], 0.0).then_inc(s_pc, 1)

                    def step(s, par, half):
                        for j in range(C):
                            n = s * C + j
                            pool.wait_ge(s_sq, n + 1)
                            pool.wait_ge(s_q_acc, n) if not isinstance(s, int) or n > 0 else pool.wait_ge(s_pc, 1)
                            pool.tensor_tensor(q_acc[0:R, :], q_acc[0:R, :], squares[0:R, j % 2, :], ALU.add).then_inc(s_q_acc, 1)
                            for k in pieces(s, j):
                                pool.wait_ge(s_wh, k + 1)
                                pool.tensor_tensor(w1_lo[:, k, :], w1[:, k, :], w1_hi[:, k, :].bitcast(F32), ALU.subtract)
                    groups(pool, step)

                @block.tensor
                def _(pe):
                    def turn(s, par):
                        pe.wait_ge(s_mean, s + 1)
                        for c in range(KC + 1):
                            if c == 0:
                                wait(pe, s_ml, s * KC)
                            wide = P if c < KC else 2
                            to = bank[(4 + c) % 8]
                            for j in range(C):
                                t = pe.transpose(to[0:wide, j * R:j * R + R],
                                                 mean[par][0:R, j, c * P:c * P + wide], ident[0:R, 0:R])
                            t.then_inc(s_mt, 1)

                    def conv(s, j):
                        wait(pe, s_u, s * C + j - 1)
                        to = bank[2 + j % 2][0:R, :]
                        at = slice(j * R, j * R + R)
                        for c in range(KC):
                            if j == 0:
                                pe.wait_ge(s_ml, s * KC + c + 1)
                            split_product(pe, to, (mean_hi[:, c, at], mean_lo[:, c, at]),
                                          (conv_hi[:, c, :], conv_lo[:, c, :]), c == 0, False)
                        if j == 0:
                            pe.wait_ge(s_mc, (s + 1) * (KC + 1))
                        pe.matmul(to, deg_t[:, at], rows_lo, start=False, stop=False)
                        pe.matmul(to, deg_t[:, at], rows_hi, start=False, stop=True).then_inc(s_conv, 1)

                    def step(s, par, half):
                        for j in range(C):
                            conv(s, j)
                        if not isinstance(s, int) or s < NG - 1:
                            turn(s + 1, 1 - par)
                    turn(0, 0)
                    groups(pe, step)

                @block.scalar
                def _(act):
                    def copies(s):
                        for c in range(KC + 1):
                            act.wait_ge(s_mt, s * (KC + 1) + c + 1)
                            if c == 0:
                                wait(act, s_conv, s * C)
                            if c < KC:
                                act.activation(mean_hi[:, c, 0:G], bank[4 + c][:, 0:G], ACT.Copy).then_inc(s_mc, 1)
                            else:
                                act.activation(deg_t[:, :], bank[0][0:2, 0:G], ACT.Copy).then_inc(s_mc, 1)

                    def step(s, par, half):
                        for j in range(C):
                            n = s * C + j
                            act.wait_ge(s_u, n + 1)
                            wait(act, s_q_acc, n - 1)
                            act.activation(squares[0:R, j % 2, :], u[par][0:R, j, :], ACT.Square).then_inc(s_sq, 1)
                            for k in pieces(s, j):
                                act.wait_ge(s_ffn, 16 * FFN_DMAS)
                                act.activation(w1_hi[:, k, :], w1[:, k, :], ACT.Copy).then_inc(s_wh, 1)
                        if not isinstance(s, int) or s < NG - 1:
                            copies(s + 1)
                    copies(0)
                    groups(act, step)

                @block.vector
                def _(dve):
                    def prepare_mean(ch, s, par, half):
                        dve.wait_ge(s_agg[par], 32 * (half + 1))
                        ch.link(dve.tensor_scalar(deg[0:R, 0, :], mean[par][0:R, :, D], 1.0, None, ALU.max))
                        ch.link(dve.reciprocal(deg[0:R, 1, :], deg[0:R, 0, :]))
                        dve.memset(mean[par][0:R, :, D + 1:D + 2], 1.0)
                        dve.tensor_scalar(mean[par][0:R, :, D:D + 1], mean[par][0:R, :, D:D + 1], 1.0, None, ALU.min)
                        for c in range(C):
                            i = dve.tensor_scalar(mean[par][0:R, c, 0:D], mean[par][0:R, c, 0:D], deg[0:R, 1, c:c + 1], None, ALU.mult)
                        i.then_inc(s_mean, 1)

                    def prepare_x(ch, s, par, half):
                        dve.wait_ge(s_in[par], 32 * (half + 1))
                        ch.link(dve.tensor_copy(now_stat[0:R, :, :], row_stat[0:R, s, :, :]))
                        for c in range(C):
                            i = dve.tensor_scalar(u[par][0:R, c, :], u[par][0:R, c, :], now_stat[0:R, 0, c:c + 1],
                                                  now_stat[0:R, 1, c:c + 1], ALU.subtract, ALU.mult)
                        ch.link(i)

                    def low_halves(s):
                        for c in range(KC):
                            dve.wait_ge(s_mc, s * (KC + 1) + c + 1)
                            if c == 0:
                                wait(dve, s_conv, s * C)
                            dve.tensor_tensor(mean_lo[:, c, 0:G], bank[4 + c][:, 0:G], mean_hi[:, c, 0:G].bitcast(F32),
                                              ALU.subtract).then_inc(s_ml, 1)

                    def step(s, par, half):
                        more = not isinstance(s, int) or s < NG - 1
                        ch = Chain(dve, s_ch, FIRST3 + s * CHAIN3)
                        for j in range(C):
                            n = s * C + j
                            dve.wait_ge(s_conv, n + 1)
                            i = dve.scalar_tensor_tensor(u[par][0:R, j, :], bank[2 + j % 2][0:R, :], 0.0, u[par][0:R, j, :],
                                                         ALU.max, ALU.add)
                            if isinstance(s, int) and n == 0:
                                i.then_inc(s_yn, 1)
                                dve.wait_ge(s_yn, 1)
                                i = dve.tensor_tensor(u[par][0:R, 0, :], u[par][0:R, 0, :], att_delta[0:R, :], ALU.add)
                            i.then_inc(s_u, 1)
                            dve.wait_ge(s_u, n + 1)
                            ch.link(dve.tensor_tensor(u_acc[0:R, :], u_acc[0:R, :], u[par][0:R, j, :], ALU.add))
                            if j == 1 and more:
                                prepare_mean(ch, s + 1, 1 - par, half + par)
                        if more:
                            low_halves(s + 1)
                            prepare_x(ch, s + 1, 1 - par, half + par)
                        assert not more or ch.n == CHAIN3, ch.n

                    ch = Chain(dve, s_ch)
                    ch.link(dve.memset(u_acc[:, :], 0.0))
                    prepare_mean(ch, 0, 0, 0)
                    prepare_x(ch, 0, 0, 0)
                    assert ch.n == FIRST3
                    low_halves(0)
                    groups(dve, step)

        x_in, zn = w_proj, w_conv
        s_x = sem("s_zx")
        with ExitStack() as st:
            gain = sb(st, "gain", [P, 3, D])
            mu = sb(st, "mu", [P, D])
            var = sb(st, "var", [P, D])
            std = sb(st, "std", [P, D])
            tmp = sb(st, "tmp", [P, D])
            s_gain = sem("s_gain")
            s_wh2 = sem("s_wh2")
            s_tot = sem("s_tot")
            s_v2 = sem("s_v2")
            s_r2 = sem("s_r2")
            s_ch = sem("s_ch4")
            with nc.Block() as block:
                @block.sync
                def _(sp):
                    dma_rows(sp, x_in[0:R], x_g[0], s_x)
                    for k, name in enumerate(("L0_gnn_norm2_g", "L0_gnn_norm2_b", "L0_mix_b_proj")):
                        sp.dma_start(gain[:, k, :], a[name].rearrange("(a d) -> a d", a=1).broadcast_to([P, D])).then_inc(s_gain, 16)

                @block.tensor
                def _(pe):
                    pe.matmul(bank[0][:, :], ones[0:R, :], u_acc[0:R, :], start=True, stop=True)
                    pe.matmul(bank[1][:, :], ones[0:R, :], q_acc[0:R, :], start=True, stop=True).then_inc(s_tot, 1)

                @block.scalar
                def _(act):
                    act.activation(w2_hi[:, 0:FC - 1, :], w2[:, 0:FC - 1, :], ACT.Copy).then_inc(s_wh2, 1)
                    act.activation(w2_hi[0:LAST, FC - 1, :], w2[0:LAST, FC - 1, :], ACT.Copy).then_inc(s_wh2, 1)
                    act.wait_ge(s_v2, 1)
                    act.activation(std[:, :], var[:, :], ACT.Sqrt).then_inc(s_r2, 1)

                @block.gpsimd
                def _(pool):
                    pool.wait_ge(s_wh2, 1)
                    pool.tensor_tensor(w2_lo[:, 0:FC - 1, :], w2[:, 0:FC - 1, :], w2_hi[:, 0:FC - 1, :].bitcast(F32), ALU.subtract)
                    pool.wait_ge(s_wh2, 2)
                    pool.tensor_tensor(w2_lo[0:LAST, FC - 1, :], w2[0:LAST, FC - 1, :], w2_hi[0:LAST, FC - 1, :].bitcast(F32), ALU.subtract)

                @block.vector
                def _(dve):
                    ch = Chain(dve, s_ch)
                    dve.wait_ge(s_x, 32)
                    for c in range(C):
                        dve.tensor_scalar(zn[0:R, c, :], x_in[0:R, c, :], row_stat[0:R, 0, 0, c:c + 1],
                                          row_stat[0:R, 0, 1, c:c + 1], ALU.subtract, ALU.mult)
                    dve.wait_ge(s_tot, 1)
                    ch.link(dve.tensor_scalar(mu[:, :], bank[0][:, :], 1.0 / N, None, ALU.mult))
                    ch.link(dve.tensor_tensor(tmp[:, :], mu[:, :], mu[:, :], ALU.mult))
                    ch.link(dve.scalar_tensor_tensor(var[:, :], bank[1][:, :], 1.0 / N, tmp[:, :], ALU.mult, ALU.subtract))
                    dve.tensor_scalar(var[:, :], var[:, :], 0.0, BN_EPS, ALU.max, ALU.add).then_inc(s_v2, 1)
                    dve.wait_ge(s_r2, 1)
                    inverse_root(ch, dve, scale2[:, :], std[:, :], var[:, :], tmp[:, :])
                    dve.wait_ge(s_gain, 48)
                    ch.link(dve.tensor_tensor(scale2[:, :], scale2[:, :], gain[:, 0, :], ALU.mult))
                    ch.link(dve.tensor_tensor(tmp[:, :], mu[:, :], scale2[:, :], ALU.mult))
                    ch.link(dve.tensor_tensor(shift2[:, :], gain[:, 1, :], gain[:, 2, :], ALU.add))
                    dve.tensor_tensor(shift2[:, :], shift2[:, :], tmp[:, :], ALU.subtract)
        sums.close()
        with ExitStack() as st:
            z = [sb(st, f"z{i}", [P, C, D]) for i in range(2)]
            xn, x2 = zn, w_v
            halves = sb(st, "halves", [P, KC, G], F32R)
            xn_hi = halves
            gated_hi, gated_lo = halves[:, 0:2, :], halves[:, 2:4, :]
            xn_lo = sb(st, "zn_lo", [P, KC, G], F32R)
            low = sb(st, "lowq", [P, 2, G])
            qz = sb(st, "qz", [P, KC, G])
            rden = sb(st, "rden", [P, G])
            x2_hi = sb(st, "x2_hi", [P, KC, G], F32R)
            x2_lo = sb(st, "x2_lo", [P, KC, G], F32R)
            hid = sb(st, "hid", [P, 2, G])
            shared = sb(st, "shared", [P, G])
            logit_t = rden
            now_stat = sb(st, "z_stat", [P, 2, C])
            bn = sb(st, "bnz", [P, C, 6])
            st_mv = sb(st, "mvz", [P, C, 2])
            st_std = sb(st, "stdz", [P, C])
            st_rstd = sb(st, "rstdz", [P, C])
            st_tmp = sb(st, "tmpz", [P, C])
            top_l = sb(st, "top_l", [P, C * 2])
            shifted = sb(st, "shifted", [P, C * 2, EXPERTS])
            expd = sb(st, "expd", [P, C * 2, EXPERTS])
            gate = sb(st, "gate", [P, C * 2])
            descend = sb(st, "descend", [P, EXPERTS])
            pick = sb(st, "pick", [P, C * 2, EXPERTS])
            picked = sb(st, "picked", [P, C * 2])
            one_hot = sb(st, "one_hot", [P, C, EB], BF16)
            carried = sb(st, "carried", [P, EB])
            place = sb(st, "place", [P, C, EB])
            gates = sb(st, "gates", [P, C, EB + 1])
            rest = sb(st, "rest", [P, C, EB])
            parts = sb(st, "parts", [P, C, 3 * EB], BF16)
            parts_t = sb(st, "parts_t", [3 * EB, C, R], BF16)
            spread = sb(st, "spread", [3 * EB, 8, P], BF16)
            upto = sb(st, "upto", [P, P], BF16)
            ones_b = sb(st, "ones_b", [P, P], BF16)
            ident_b = sb(st, "ident_b", [P, P], BF16)

            s_ul = sem("s_ul")
            s_set = sem("s_set")
            s_base = sem("s_base")
            s_bc = sem("s_bc")
            s_n = sem("s_n")
            s_nt = sem("s_nt")
            s_nc = sem("s_nc")
            s_nl = sem("s_nl")
            s_q = sem("s_q")
            s_ql = sem("s_ql")
            s_qe = sem("s_qe")
            s_qp = sem("s_qp")
            s_den = sem("s_den")
            s_rd = sem("s_rd")
            s_qz = sem("s_qz")
            s_mix = sem("s_mix")
            s_xp = sem("s_xp")
            s_v = sem("s_v")
            s_r = sem("s_r")
            s_x2 = sem("s_x2")
            s_xt = sem("s_xt")
            s_xc = sem("s_xc")
            s_xl = sem("s_xl")
            s_lc = sem("s_lc")
            s_lg = sem("s_lg")
            s_sh = sem("s_sh")
            s_le = sem("s_le")
            s_oh = sem("s_oh")
            s_pos = sem("s_pos")
            s_gate = sem("s_gate")
            s_gt = sem("s_gt")
            s_gc = sem("s_gc")
            s_h = sem("s_h")
            s_ge = sem("s_ge")
            s_mk = sem("s_mk")
            s_hm = sem("s_hm")
            s_gh = sem("s_gh")
            s_gl = sem("s_gl")
            s_out = sem("s_out")
            OUTS = FC - 1 + C
            s_o = sem("s_o")
            s_st = [sem(f"s_st{i}") for i in range(2)]
            s_ch = sem("s_ch5")
            s_past_pe = sem("s_past_pe")

            def pipeline(eng, step):
                groups(eng, lambda i, par, half: step(i, par, half, True, not isinstance(i, int) or i > 0))
                step(NG, 0, NG // 2, False, True)

            with nc.Block() as block:
                @block.sync
                def _(sp):
                    def load_x(i):
                        wait(sp, s_n, i - 1)
                        settle(sp, s_past_sp)
                        wait(sp, s_base, i * C)
                        dma_rows(sp, x_in[0:R], x_g[i], s_x)

                    def step(i, par, half, front, back):
                        if front:
                            wait(sp, s_st[par], 32 * half)
                            dma_rows(sp, z[par][0:R], u_g[i], s_ul)
                        if not isinstance(i, int) or i < NG - 1:
                            load_x(i + 1)
                        if back:
                            sp.wait_ge(s_o, i * C)
                            dma_rows(sp, out_g[i - 1], z[1 - par][0:R], s_st[1 - par])
                    pipeline(sp, step)
                    for k in range(2):
                        sp.wait_ge(s_st[k], 32 * (NG // 2))

                @block.gpsimd
                def _(pool):
                    ch = Chain(pool, s_bc)
                    ch.link(pool.memset(ones_b[:, :], 1.0))
                    ch.link(pool.affine_select(out=upto[:, :], in_=ones_b[:, :], compare_op=ALU.is_ge, fill=0.0,
                                               base=0, pattern=[[1, P]], channel_multiplier=-1))
                    ch.link(pool.tensor_copy(ident_b[:, :], ident[:, :]))
                    ch.link(pool.memset(spread[:, :, :], 0.0))
                    for t in range(3):
                        part = spread[:, :, :].rearrange("k c (e f) -> k c e f", e=2)
                        ch.link(pool.affine_select(out=part, in_=part, compare_op=ALU.not_equal, fill=1.0, base=-t * EB,
                                                   pattern=[[-2, 8], [-1, 2], [0, 64]], channel_multiplier=1))
                    ch.link(pool.iota(descend[:, :], pattern=[[-1, EXPERTS]], base=EXPERTS, channel_multiplier=0,
                                      allow_small_or_imprecise_dtypes=True))
                    pool.memset(gates[:, :, EB:EB + 1], 1.0)
                    pool.memset(carried[:, :], 0.0).then_inc(s_set, 1)

                    def base(i, par):
                        ch = Chain(pool, s_bc, 8 + i * 2 * C)
                        pool.wait_ge(s_x, 32 * (i + 1))
                        pool.wait_ge(s_ul, 32 * (i + 1))
                        for j in range(C):
                            tile = z[par][0:R, j, :]
                            ch.link(pool.tensor_tensor(tile, tile, scale2[0:R, :], ALU.mult))
                            ch.link(pool.tensor_tensor(tile, tile, shift2[0:R, :], ALU.add))
                            pool.tensor_tensor(tile, tile, x_in[0:R, j, :], ALU.add).then_inc(s_base, 1)

                    def low_half(b, n):
                        pool.wait_ge(s_gh, b * FC + n + 1)
                        wait(pool, s_out, b * OUTS + max(n - 1, 0))
                        whole, rows = (shared[0:LAST, :], LAST) if n == 0 else (hid[:, n % 2, :], P)
                        pool.tensor_tensor(gated_lo[0:rows, n % 2, :], whole, gated_hi[0:rows, n % 2, :].bitcast(F32),
                                           ALU.subtract).then_inc(s_gl, 1)

                    def step(i, par, half, front, back):
                        if front:
                            base(i, par)
                        if back:
                            for n in range(FC):
                                low_half(i - 1, n)
                    pipeline(pool, step)

                @block.tensor
                def _(pe):
                    def turn_x(i):
                        wait(pe, s_n, i)
                        for c in range(KC):
                            wait(pe, s_o, (i - 2) * C + c + 1 if not isinstance(i, int) or i >= 2 else 0)
                            for j in range(C):
                                t = pe.transpose(bank[c][:, j * R:j * R + R], xn[0:R, j, c * P:c * P + P], ident[0:R, 0:R])
                            t.then_inc(s_nt, 1)

                    def turn_x2(i, b, front):
                        pe.wait_ge(s_x2, b + 1)
                        for c in range(KC):
                            if front:
                                pe.wait_ge(s_nl, i * KC + c + 1)
                            else:
                                pe.wait_ge(s_o, (i - 2) * C + c + 1)
                            for j in range(C):
                                t = pe.transpose(bank[c][:, j * R:j * R + R], x2[0:R, j, c * P:c * P + P], ident[0:R, 0:R])
                            t.then_inc(s_xt, 1)

                    def front_q(i, f, back):
                        if f == 0:
                            pe.wait_ge(s_nl, (i + 1) * KC)
                        if back:
                            pe.wait_ge(s_xl, (i - 1) * KC + f + 1)
                        for c in range(KC):
                            at = slice(f * P, f * P + P)
                            m = split_product(pe, bank[f][:, 0:G], (phi_q_hi[:, c, at], phi_q_lo[:, c, at]),
                                              (xn_hi[:, c, :], xn_lo[:, c, :]), c == 0, c == KC - 1)
                        m.then_inc(s_q, 1)

                    def hidden(b, n):
                        if n == 0:
                            pe.wait_ge(s_xl, (b + 1) * KC)
                        wait(pe, s_ge, b * FC + max(n - 1, 0))
                        wide = P if n > 0 else 64 + EB
                        at = (n - 1) * P if n > 0 else 2 * EXPERTS * FF
                        for c in range(KC):
                            m = split_product(pe, bank[4 + n % 2][0:wide, 0:G],
                                              (w1_hi[:, c, at:at + wide], w1_lo[:, c, at:at + wide]),
                                              (x2_hi[:, c, :], x2_lo[:, c, :]), c == 0, c == KC - 1)
                        m.then_inc(s_h, 1)

                    def turn_logits(i, b):
                        pe.wait_ge(s_lc, b + 1)
                        pe.wait_ge(s_xp, i * C)
                        settle(pe, s_past_pe)
                        for j in range(C):
                            t = pe.transpose(bank[7][0:R, j * EB:j * EB + EB], logit_t[64:64 + EB, j * R:j * R + R],
                                             ident[64:64 + EB, 64:64 + EB])
                        t.then_inc(s_lg, 1)

                    def places(b):
                        pe.wait_ge(s_oh, b + 1)
                        for j in range(C):
                            for k in range(j + 1):
                                pe.matmul(bank[7][0:R, 64 + j * EB:80 + j * EB], (ones_b if k < j else upto)[0:R, 0:R],
                                          one_hot[0:R, k, :], start=(k == 0), stop=(k == j))
                        for k in range(C):
                            m = pe.matmul(bank[7][0:R, 128:144], ones_b[0:R, 0:R], one_hot[0:R, k, :], start=(k == 0), stop=(k == C - 1))
                        m.then_inc(s_pos, 1)

                    def turn_gates(b):
                        pe.wait_ge(s_gate, b + 1)
                        wait(pe, s_hm, b * 8)
                        turned = bank[7][0:3 * EB, 0:256].bitcast(BF16)
                        for j in range(C):
                            pe.transpose(bank[6][0:EB + 1, j * R:j * R + R], gates[0:R, j, :], ident[0:R, 0:R])
                        for j in range(C):
                            t = pe.transpose(turned[:, j * P:j * P + R], parts[0:R, j, :], ident_b[0:R, 0:R])
                        t.then_inc(s_gt, 1)

                    def mask(b, n):
                        if n == 1:
                            pe.wait_ge(s_gc, b + 1)
                        else:
                            pe.wait_ge(s_hm, b * 8 + n - 1)
                        pe.matmul(bank[6][:, 0:G], spread[:, n - 1, :], parts_t[:, :, :], start=True, stop=True).then_inc(s_mk, 1)

                    def den(i, f, back):
                        pe.wait_ge(s_qp, i * KC + f + 1)
                        if f > 0:
                            pe.wait_ge(s_rd, i * KC + f)
                        elif back:
                            pe.wait_ge(s_gc, i)
                        pe.matmul(bank[7][:, 0:G], ks_bd[:, f, :], qz[:, f, :], start=True, stop=True).then_inc(s_den, 1)

                    def mix(i, j):
                        if j == 0:
                            pe.wait_ge(s_qz, (i + 1) * KC)
                        else:
                            pe.wait_ge(s_xp, i * C + j)
                        for f in range(KC):
                            m = pe.matmul(bank[7][0:R, :], qz[:, f, j * R:j * R + R], kvp[:, f, :],
                                          start=(f == 0), stop=(f == KC - 1))
                        m.then_inc(s_mix, 1)

                    def outputs(i, b, n, front):
                        if n == 0 and front:
                            pe.wait_ge(s_qp, (i + 1) * KC)
                        pe.wait_ge(s_gl, b * FC + n + 1)
                        rows, k = (P, n - 1) if n > 0 else (LAST, FC - 1)
                        for j in range(C):
                            at = slice(j * R, j * R + R)
                            m = split_product(pe, bank[j][0:R, :],
                                              (gated_hi[0:rows, n % 2, at], gated_lo[0:rows, n % 2, at]),
                                              (w2_hi[0:rows, k, :], w2_lo[0:rows, k, :]), n == 0, n == FC - 1)
                            if n == FC - 1 or j == C - 1:
                                m.then_inc(s_out, 1)

                    def step(i, par, half, front, back):
                        if isinstance(i, int) and i == 1:
                            pe.wait_ge(s_set, 1)
                        if front:
                            turn_x(i)
                        if back:
                            turn_x2(i, i - 1, front)
                        if front:
                            front_q(i, 0, back)
                        if back:
                            hidden(i - 1, 0)
                        if front:
                            front_q(i, 1, back)
                        if back:
                            turn_logits(i, i - 1)
                        if front:
                            front_q(i, 2, back)
                        if back:
                            hidden(i - 1, 1)
                            places(i - 1)
                        if front:
                            front_q(i, 3, back)
                        if back:
                            turn_gates(i - 1)
                            hidden(i - 1, 2)
                        for n in range(FC):
                            if back and n + 3 < FC:
                                hidden(i - 1, n + 3)
                            if back and n < FC - 1:
                                mask(i - 1, n + 1)
                            if front and n < KC:
                                den(i, n, back)
                            if front and KC <= n < KC + C:
                                mix(i, n - KC)
                            if back:
                                outputs(i, i - 1, n, front)
                    pipeline(pe, step)

                @block.scalar
                def _(act):
                    def copy_x(i):
                        for c in range(KC):
                            act.wait_ge(s_nt, i * KC + c + 1)
                            if c == 0:
                                wait(act, s_q, i * KC)
                                wait(act, s_out, (i - 1) * OUTS if not isinstance(i, int) or i >= 2 else 0)
                            act.activation(xn_hi[:, c, :], bank[c][:, 0:G], ACT.Copy).then_inc(s_nc, 1)

                    def high_x2(b):
                        for c in range(KC):
                            act.wait_ge(s_xt, b * KC + c + 1)
                            if c == 0:
                                wait(act, s_h, b * FC)
                            act.activation(x2_hi[:, c, :], bank[c][:, 0:G], ACT.Copy).then_inc(s_xc, 1)

                    def exp_q(i, f):
                        act.wait_ge(s_ql, i * KC + f + 1)
                        act.activation(low[:, f % 2, :], low[:, f % 2, :], ACT.Exp).then_inc(s_qe, 1)

                    def copy_logits(b):
                        act.wait_ge(s_h, b * FC + 1)
                        act.wait_ge(s_qz, (b + 1) * KC)
                        act.activation(logit_t[64:64 + EB, :], bank[4][64:64 + EB, 0:G], ACT.Identity,
                                       bias=b1[64:64 + EB, 8:9]).then_inc(s_lc, 1)

                    def exp_logits(b):
                        act.wait_ge(s_sh, b + 1)
                        act.activation(expd[0:R, :, :], shifted[0:R, :, :], ACT.Exp).then_inc(s_le, 1)

                    def gelu(b, n):
                        act.wait_ge(s_h, b * FC + n + 1)
                        wait(act, s_gl, b * FC + max(n - 1, 0))
                        to, wide, k = (hid[:, n % 2, :], P, n - 1) if n > 0 else (shared[0:64, :], 64, FC - 1)
                        act.activation(to, bank[4 + n % 2][0:wide, 0:G], ACT.Gelu, bias=b1[0:wide, k:k + 1]).then_inc(s_ge, 1)

                    def copy_gates(b):
                        act.wait_ge(s_gt, b + 1)
                        wait(act, s_mk, b * 8)
                        turned = bank[7][0:3 * EB, 0:256].bitcast(BF16).rearrange("k (c r) -> k c r", c=C)
                        act.activation(parts_t[:, :, :], turned[:, :, 0:R], ACT.Copy)
                        act.activation(shared[64:LAST, :], bank[6][0:EB + 1, 0:G], ACT.Copy).then_inc(s_gc, 1)

                    def high_half(b, n, front):
                        if n == 0:
                            if front:
                                act.wait_ge(s_q, (b + 2) * KC)
                            act.wait_ge(s_gc, b + 1)
                        else:
                            act.wait_ge(s_hm, b * 8 + n)
                        wait(act, s_out, b * OUTS + max(n - 1, 0))
                        whole, rows = (shared[0:LAST, :], LAST) if n == 0 else (hid[:, n % 2, :], P)
                        act.activation(gated_hi[0:rows, n % 2, :], whole, ACT.Copy).then_inc(s_gh, 1)

                    def root(i):
                        act.wait_ge(s_v, i + 1)
                        act.activation(st_std[0:R, :], st_mv[0:R, :, 1], ACT.Sqrt).then_inc(s_r, 1)

                    def step(i, par, half, front, back):
                        if front:
                            copy_x(i)
                        if back:
                            high_x2(i - 1)
                        if front:
                            exp_q(i, 0)
                        if back:
                            copy_logits(i - 1)
                        if front:
                            exp_q(i, 1)
                        if back:
                            exp_logits(i - 1)
                        if front:
                            exp_q(i, 2)
                        if back:
                            gelu(i - 1, 0)
                            gelu(i - 1, 1)
                        if front:
                            exp_q(i, 3)
                        if back:
                            copy_gates(i - 1)
                            for n in range(FC):
                                high_half(i - 1, n, front)
                                if n + 2 < FC:
                                    gelu(i - 1, n + 2)
                        if front:
                            root(i)
                    pipeline(act, step)

                @block.vector
                def _(dve):
                    def normalise_x(ch, i):
                        dve.wait_ge(s_x, 32 * (i + 1))
                        ch.link(dve.tensor_copy(now_stat[0:R, :, :], row_stat[0:R, i, :, :]))
                        wait(dve, s_nt, i * KC)
                        for c in range(C):
                            k = dve.tensor_scalar(xn[0:R, c, :], x_in[0:R, c, :], now_stat[0:R, 0, c:c + 1],
                                                  now_stat[0:R, 1, c:c + 1], ALU.subtract, ALU.mult)
                        k.then_inc(s_n, 1)

                    def low_x(i):
                        for c in range(KC):
                            dve.wait_ge(s_nc, i * KC + c + 1)
                            if c == 0:
                                wait(dve, s_q, i * KC)
                            dve.tensor_tensor(xn_lo[:, c, :], bank[c][:, 0:G], xn_hi[:, c, :].bitcast(F32), ALU.subtract).then_inc(s_nl, 1)

                    def low_x2(b):
                        for c in range(KC):
                            dve.wait_ge(s_xc, b * KC + c + 1)
                            if c == 0:
                                wait(dve, s_h, b * FC)
                            dve.tensor_tensor(x2_lo[:, c, :], bank[c][:, 0:G], x2_hi[:, c, :].bitcast(F32), ALU.subtract).then_inc(s_xl, 1)

                    def phi(i, f):
                        if f == 0:
                            wait(dve, s_mix, i * C)
                        q = bank[f][:, 0:G]
                        dve.wait_ge(s_q, i * KC + f + 1)
                        dve.tensor_scalar(low[:, f % 2, :], q, 0.0, None, ALU.min).then_inc(s_ql, 1)
                        dve.wait_ge(s_qe, i * KC + f + 1)
                        dve.scalar_tensor_tensor(qz[:, f, :], q, 0.0, low[:, f % 2, :], ALU.max, ALU.add).then_inc(s_qp, 1)

                    def route(ch, b):
                        logits = bank[7][0:R, 0:C * EB].rearrange("p (a e) -> p a e", e=EXPERTS)
                        wide = [R, C * 2, EXPERTS]
                        dve.wait_ge(s_lg, b + 1)
                        ch.link(dve.tensor_reduce(top_l[0:R, :], logits, AX.X, ALU.max))
                        dve.tensor_tensor(shifted[0:R, :, :], logits, top_l[0:R, :, None].broadcast_to(wide), ALU.subtract).then_inc(s_sh, 1)
                        dve.wait_ge(s_sh, b + 1)
                        ch.link(dve.scalar_tensor_tensor(pick[0:R, :, :], shifted[0:R, :, :], 0.0,
                                                         descend[0:R, None, :].broadcast_to(wide), ALU.is_ge, ALU.mult))
                        ch.link(dve.tensor_reduce(picked[0:R, :], pick[0:R, :, :], AX.X, ALU.max))
                        wait(dve, s_pos, b)
                        dve.tensor_tensor(one_hot[0:R, :, :].rearrange("p c (k e) -> p (c k) e", k=2), pick[0:R, :, :],
                                          picked[0:R, :, None].broadcast_to(wide), ALU.is_equal).then_inc(s_oh, 1)
                        dve.wait_ge(s_le, b + 1)
                        ch.link(dve.tensor_reduce(gate[0:R, :], expd[0:R, :, :], AX.X, ALU.add))
                        ch.link(dve.reciprocal(gate[0:R, :], gate[0:R, :]))

                    def make_gates(ch, b):
                        dve.wait_ge(s_pos, b + 1)
                        ch.link(dve.tensor_tensor(place[0:R, :, :], bank[7][0:R, 64:128].rearrange("p (c e) -> p c e", c=C),
                                                  carried[0:R, None, :].broadcast_to([R, C, EB]), ALU.add))
                        ch.link(dve.tensor_tensor(carried[0:R, :], carried[0:R, :], bank[7][0:R, 128:144], ALU.add))
                        ch.link(dve.scalar_tensor_tensor(place[0:R, :, :], place[0:R, :, :], float(CAP), one_hot[0:R, :, :],
                                                         ALU.is_le, ALU.mult))
                        wait(dve, s_gt, b)
                        for j in range(C):
                            k = dve.tensor_tensor(gates[0:R, j, 0:EB].rearrange("p (k e) -> p k e", k=2),
                                                  place[0:R, j, :].rearrange("p (k e) -> p k e", k=2),
                                                  gate[0:R, 2 * j:2 * j + 2, None].broadcast_to([R, 2, EXPERTS]), ALU.mult)
                        ch.link(k)
                        ch.link(dve.tensor_copy(parts[0:R, :, 0:EB], gates[0:R, :, 0:EB]))
                        ch.link(dve.tensor_tensor(rest[0:R, :, :], gates[0:R, :, 0:EB], parts[0:R, :, 0:EB], ALU.subtract))
                        ch.link(dve.tensor_copy(parts[0:R, :, EB:2 * EB], rest[0:R, :, :]))
                        ch.link(dve.tensor_tensor(rest[0:R, :, :], rest[0:R, :, :], parts[0:R, :, EB:2 * EB], ALU.subtract))
                        dve.tensor_copy(parts[0:R, :, 2 * EB:3 * EB], rest[0:R, :, :]).then_inc(s_gate, 1)

                    def divide(i, f):
                        dve.wait_ge(s_den, i * KC + f + 1)
                        wait(dve, s_qz, i * KC + f)
                        if f == 0:
                            wait(dve, s_lg, i)
                        dve.reciprocal(rden[:, :], bank[7][:, 0:G]).then_inc(s_rd, 1)
                        dve.wait_ge(s_rd, i * KC + f + 1)
                        dve.tensor_tensor(qz[:, f, :], qz[:, f, :], rden[:, :], ALU.mult).then_inc(s_qz, 1)

                    def x_out(i, j, par):
                        dve.wait_ge(s_mix, i * C + j + 1)
                        dve.wait_ge(s_base, i * C + j + 1)
                        dve.tensor_tensor(z[par][0:R, j, :], bank[7][0:R, :], z[par][0:R, j, :], ALU.add).then_inc(s_xp, 1)
                        dve.wait_ge(s_xp, i * C + j + 1)

                    def variances(ch, stats):
                        ch.link(stats)
                        settle(dve, s_past_dve)
                        for j in range(C):
                            k = dve.bn_aggr(st_mv[0:R, j, :], bn[0:R, j, :])
                        ch.link(k)
                        dve.tensor_scalar(st_mv[0:R, :, 1], st_mv[0:R, :, 1], LN_EPS, None, ALU.add).then_inc(s_v, 1)

                    def root_x2(ch, i):
                        dve.wait_ge(s_r, i + 1)
                        inverse_root(ch, dve, st_rstd[0:R, :], st_std[0:R, :], st_mv[0:R, :, 1], st_tmp[0:R, :])

                    def normalise_x2(i, par):
                        wait(dve, s_xt, i * KC)
                        for j in range(C):
                            k = dve.tensor_scalar(x2[0:R, j, :], z[par][0:R, j, :], st_mv[0:R, j, 0:1], st_rstd[0:R, j:j + 1],
                                                  ALU.subtract, ALU.mult)
                        k.then_inc(s_x2, 1)

                    def gated(b, n):
                        dve.wait_ge(s_ge, b * FC + n + 1)
                        dve.wait_ge(s_mk, b * 8 + n)
                        dve.tensor_tensor(hid[:, n % 2, :], hid[:, n % 2, :], bank[6][:, 0:G], ALU.mult).then_inc(s_hm, 1)

                    def outputs(b, par):
                        for j in range(C):
                            dve.wait_ge(s_out, b * OUTS + FC + j)
                            dve.tensor_tensor(z[par][0:R, j, :], bank[j][0:R, :], z[par][0:R, j, :], ALU.add).then_inc(s_o, 1)

                    def step(i, par, half, front, back):
                        ch = Chain(dve, s_ch, 0 if isinstance(i, int) and i == 0 else 21 * i - 13 if front else 21 * i - 14)
                        if front:
                            low_x(i)
                        if back:
                            low_x2(i - 1)
                        if front:
                            phi(i, 0)
                            phi(i, 1)
                        if back:
                            route(ch, i - 1)
                        if front:
                            phi(i, 2)
                        if back:
                            make_gates(ch, i - 1)
                        if front:
                            phi(i, 3)
                        for n in range(FC):
                            if back and n < FC - 1:
                                gated(i - 1, n + 1)
                            if front and n < KC:
                                divide(i, n)
                            if front and KC <= n < KC + C:
                                x_out(i, n - KC, par)
                                stats = dve.bn_stats(bn[0:R, n - KC, :], z[par][0:R, n - KC, :])
                            if n == 6 and (not isinstance(i, int) or i < NG - 1):
                                normalise_x(ch, i + 1)
                        if front:
                            variances(ch, stats)
                            root_x2(ch, i)
                        if back:
                            outputs(i - 1, 1 - par)
                        if front:
                            normalise_x2(i, par)
                        if not isinstance(i, int) or i == 1:
                            assert ch.n == 21, ch.n
                        if isinstance(i, int) and i == 0:
                            assert ch.n == 8, ch.n
                            dve.wait_ge(s_set, 1)
                    pipeline(dve, step)
        ffn.close()
        mid.close()


_INS = ["x", "src", "dst"] + ["L0_gnn_" + n for n in (
    "norm1_g", "norm1_b", "norm2_g", "norm2_b", "W_conv", "b_conv", "Wq", "Wk", "Wv", "Wo", "proj")] + [
    "L0_mix_" + n for n in ("w_qkv", "proj_mat", "w_proj", "b_proj")] + ["L0_ffn_" + n for n in (
        "Wr_sp", "br_sp", "Wr_fq", "br_fq", "Ws1", "bs1", "Ws2", "bs2", "W1_sp", "b1_sp", "W2_sp", "b2_sp",
        "W1_fq", "b1_fq", "W2_fq", "b2_fq")]


def kernel(**inputs):
    import numpy as _np
    import concourse.bacc as _bacc
    from concourse import mybir as _mybir
    from concourse.bass_utils import run_bass_kernel_spmd as _run

    nc = _bacc.Bacc("TRN2", target_bir_lowering=False, num_devices=1)
    arrays, args = {}, {}
    for name in _INS:
        array = _np.ascontiguousarray(inputs[name])
        arrays[f"in_{name}"] = array
        args[name] = nc.dram_tensor(f"in_{name}", array.shape, _mybir.dt.from_np(array.dtype), kind="ExternalInput").ap()
    result = nc.dram_tensor("out_0", (N, D), F32, kind="ExternalOutput").ap()
    gps_layer_kernel(nc, args, result)
    r = _run(nc, [arrays], core_ids=[0])
    return r.results[0]["out_0"]
```
